# Optimizing a Trainium2 kernel written in Bass

```python
import numpy as np
import jax
import jax.numpy as jnp

def _softmax(x, axis=-1):
    return jax.nn.softmax(x, axis=axis)

def _gelu(x):
    return jax.nn.gelu(x, approximate=True)

def _silu(x):
    return jax.nn.silu(x)

def _sigmoid(x):
    return jax.nn.sigmoid(x)

def _layernorm(x, axis=-1, eps=1e-05):
    m = jnp.mean(x, axis=axis, keepdims=True)
    v = jnp.var(x, axis=axis, keepdims=True)
    return (x - m) / jnp.sqrt(v + eps)

def _scatter_add(tgt, idx, src, axis=0):
    return tgt.at[idx].add(src)

def _segment_sum(src, seg, n):
    return jax.ops.segment_sum(src, seg, n)
kernel_name = 'mk_seq_postln_d2_jaxref_r4_00695f'

def setup_inputs(seed: int=0):
    np.random.seed(seed)
    _w = jnp.asarray

    def _L0_attn_setup():
        import jax, jax.numpy as jnp
        import numpy as np
        BATCH, SEQ, D_MODEL, D_STATE, TIMESCALE = (4, 512, 256, 64, 2)
        EPS = 1e-06

        def _reference_tuple_inner(x, w_in, b_in, A, Bm, Cm, Dv, w_out, b_out, g_norm):
            B, L, D = x.shape
            S = A.shape[1]
            ts = TIMESCALE
            x_sub = x[:, ::ts] if ts > 1 else x
            x_sub = x_sub * jax.lax.rsqrt(jnp.mean(jnp.square(x_sub), axis=-1, keepdims=True) + EPS) * g_norm
            xz = jnp.einsum('bld,ed->ble', x_sub, w_in) + b_in
            x_proj, gate = jnp.split(xz, 2, axis=-1)
            c_sum = Cm.sum(axis=0)
            h0 = jnp.zeros((B, D, S), dtype=x.dtype)

            def step(h, xt):
                h = jnp.tanh(h * A + xt[:, :, None] * Bm)
                y = h @ c_sum + Dv * xt
                return (h, y)
            h_last, ys = jax.lax.scan(step, h0, jnp.swapaxes(x_proj, 0, 1))
            out = jnp.swapaxes(ys, 0, 1)
            out = out * jax.nn.silu(gate)
            out = jnp.einsum('bld,ed->ble', out, w_out) + b_out
            if ts > 1:
                out = jnp.repeat(out, ts, axis=1)[:, :L]
            return (out, h_last)
        key = jax.random.key(seed)
        ks = jax.random.split(key, 6)
        D, S = (D_MODEL, D_STATE)
        return {'x': jax.random.normal(ks[0], (BATCH, SEQ, D), dtype=jnp.float32), 'w_in': jax.random.normal(ks[1], (2 * D, D), dtype=jnp.float32) * 0.02, 'b_in': jnp.zeros((2 * D,), dtype=jnp.float32), 'A': jax.random.normal(ks[2], (D, S), dtype=jnp.float32) * 0.01, 'Bm': jax.random.normal(ks[3], (D, S), dtype=jnp.float32) * 0.01, 'Cm': jax.random.normal(ks[4], (D, S), dtype=jnp.float32) * 0.01, 'Dv': jnp.ones((D,), dtype=jnp.float32), 'w_out': jax.random.normal(ks[5], (D, D), dtype=jnp.float32) * 0.02, 'b_out': jnp.zeros((D,), dtype=jnp.float32), 'g_norm': jnp.ones((D,), dtype=jnp.float32)}
    _L0_attn_in = _L0_attn_setup()

    def _L0_ffn_setup():
        import jax, jax.numpy as jnp
        import numpy as np
        B, S, D = (2, 512, 256)
        E, K, H = (8, 2, 1024)
        CAP_FACTOR = 1.0

        def _moe_forward(x, wg, w1, b1, w2, b2):
            Bb, Ss, Dd = x.shape
            T = Bb * Ss
            cap = int(K * CAP_FACTOR * ((T + E - 1) // E))
            xt = x.reshape(T, Dd)
            logits = xt @ wg
            scores = jax.nn.softmax(logits, axis=-1)
            gates_k, idx_k = jax.lax.top_k(scores, K)
            gates_k = gates_k / jnp.sum(gates_k, axis=-1, keepdims=True)
            masks = jax.nn.one_hot(idx_k, E, dtype=jnp.int32)
            m = jnp.transpose(masks, (1, 0, 2)).reshape(K * T, E)
            locs_full = jnp.cumsum(m, axis=0) - 1
            loc = jnp.sum(locs_full * m, axis=-1)
            loc = loc.reshape(K, T).T
            valid = (loc < cap).astype(xt.dtype)
            loc_c = jnp.clip(loc, 0, cap - 1)
            contrib = (xt[:, None, :] * valid[:, :, None]).reshape(T * K, Dd)
            disp = jnp.zeros((E, cap, Dd), xt.dtype)
            disp = disp.at[idx_k.reshape(-1), loc_c.reshape(-1)].add(contrib)
            h = jax.nn.relu(jnp.einsum('ecd,edh->ech', disp, w1) + b1[:, None, :])
            out = jnp.einsum('ech,ehd->ecd', h, w2) + b2[:, None, :]
            gathered = out[idx_k, loc_c]
            y = jnp.einsum('tk,tkd->td', gates_k * valid, gathered)
            return y.reshape(Bb, Ss, Dd)
        key = jax.random.key(seed)
        ks = jax.random.split(key, 6)
        scale_in = 1.0 / np.sqrt(D)
        scale_h = 1.0 / np.sqrt(H)
        return {'x': jax.random.normal(ks[0], (B, S, D), jnp.float32), 'wg': jax.random.normal(ks[1], (D, E), jnp.float32) * scale_in, 'w1': jax.random.normal(ks[2], (E, D, H), jnp.float32) * scale_in, 'b1': jnp.zeros((E, H), jnp.float32), 'w2': jax.random.normal(ks[3], (E, H, D), jnp.float32) * scale_h, 'b2': jnp.zeros((E, D), jnp.float32)}
    _L0_ffn_in = _L0_ffn_setup()

    def _L1_attn_setup():
        import jax, jax.numpy as jnp
        import numpy as np
        import math
        B, T, C = (2, 512, 256)
        H, L = (16, 64)
        DH = C // H
        DHE = DH // 2
        THETA = 10000.0

        def _rope_cache(t, dim):
            inv_freq = 1.0 / THETA ** (jnp.arange(0, dim, 2, dtype=jnp.float32) / dim)
            freqs = jnp.arange(t, dtype=jnp.float32)[:, None] * inv_freq[None, :]
            emb = jnp.concatenate((freqs, freqs), axis=-1)
            return (jnp.cos(emb), jnp.sin(emb))

        def _apply_rope(x, cos, sin):
            x1 = x[..., 0::2]
            x2 = x[..., 1::2]
            rot = jnp.stack((-x2, x1), axis=-1).reshape(x.shape)
            return x * cos[None, None] + rot * sin[None, None]
        key = jax.random.key(seed)
        ks = jax.random.split(key, 10)
        s = 0.02
        return {'x': jax.random.normal(ks[0], (B, T, C), jnp.float32), 'Wq_down': jax.random.normal(ks[1], (C, H * L), jnp.float32) * s, 'Wk_down': jax.random.normal(ks[2], (C, H * L), jnp.float32) * s, 'Wv_down': jax.random.normal(ks[3], (C, H * L), jnp.float32) * s, 'Wq_up_c': jax.random.normal(ks[4], (L, DHE), jnp.float32) * s, 'Wq_up_e': jax.random.normal(ks[5], (L, DHE), jnp.float32) * s, 'Wk_up_c': jax.random.normal(ks[6], (L, DHE), jnp.float32) * s, 'Wk_up_e': jax.random.normal(ks[7], (L, DHE), jnp.float32) * s, 'Wv_up': jax.random.normal(ks[8], (L, DH), jnp.float32) * s, 'Wc': jax.random.normal(ks[9], (C, C), jnp.float32) * s}
    _L1_attn_in = _L1_attn_setup()

    def _L1_ffn_setup():
        import jax, jax.numpy as jnp
        import numpy as np
        from jax import lax
        DIM = 256
        INTER = 128
        N_EXPERTS = 16
        TOPK = 4
        ROUTE_SCALE = 2.5
        VOCAB = 8000

        def _silu_and_mul(gu):
            gate, up = jnp.split(gu, 2, axis=-1)
            return jax.nn.silu(gate) * up
        key = jax.random.key(seed)
        ks = jax.random.split(key, 8)
        x = jax.random.normal(ks[0], (2, 128, DIM), dtype=jnp.float32)
        input_ids = jax.random.randint(ks[1], (2, 128), 0, VOCAB)
        s = 0.02
        gate_w = jax.random.normal(ks[2], (N_EXPERTS, DIM), dtype=jnp.float32) * s
        gate_b = jax.random.normal(ks[3], (N_EXPERTS,), dtype=jnp.float32) * s
        w13 = jax.random.normal(ks[4], (N_EXPERTS, 2 * INTER, DIM), dtype=jnp.float32) * s
        w2 = jax.random.normal(ks[5], (N_EXPERTS, DIM, INTER), dtype=jnp.float32) * s
        w13_s = jax.random.normal(ks[6], (2 * INTER, DIM), dtype=jnp.float32) * s
        w2_s = jax.random.normal(ks[7], (DIM, INTER), dtype=jnp.float32) * s
        return {'x': x, 'input_ids': input_ids, 'gate_w': gate_w, 'gate_b': gate_b, 'w13': w13, 'w2': w2, 'w13_s': w13_s, 'w2_s': w2_s}
    _L1_ffn_in = _L1_ffn_setup()
    _d = {'L0_attn_x': _L0_attn_in['x'], 'L0_attn_w_in': _L0_attn_in['w_in'], 'L0_attn_b_in': _L0_attn_in['b_in'], 'L0_attn_A': _L0_attn_in['A'], 'L0_attn_Bm': _L0_attn_in['Bm'], 'L0_attn_Cm': _L0_attn_in['Cm'], 'L0_attn_Dv': _L0_attn_in['Dv'], 'L0_attn_w_out': _L0_attn_in['w_out'], 'L0_attn_b_out': _L0_attn_in['b_out'], 'L0_attn_g_norm': _L0_attn_in['g_norm'], 'L0_ffn_wg': _L0_ffn_in['wg'], 'L0_ffn_w1': _L0_ffn_in['w1'], 'L0_ffn_b1': _L0_ffn_in['b1'], 'L0_ffn_w2': _L0_ffn_in['w2'], 'L0_ffn_b2': _L0_ffn_in['b2'], 'L1_attn_Wq_down': _L1_attn_in['Wq_down'], 'L1_attn_Wk_down': _L1_attn_in['Wk_down'], 'L1_attn_Wv_down': _L1_attn_in['Wv_down'], 'L1_attn_Wq_up_c': _L1_attn_in['Wq_up_c'], 'L1_attn_Wq_up_e': _L1_attn_in['Wq_up_e'], 'L1_attn_Wk_up_c': _L1_attn_in['Wk_up_c'], 'L1_attn_Wk_up_e': _L1_attn_in['Wk_up_e'], 'L1_attn_Wv_up': _L1_attn_in['Wv_up'], 'L1_attn_Wc': _L1_attn_in['Wc'], 'L1_ffn_input_ids': _L1_ffn_in['input_ids'], 'L1_ffn_gate_w': _L1_ffn_in['gate_w'], 'L1_ffn_gate_b': _L1_ffn_in['gate_b'], 'L1_ffn_w13': _L1_ffn_in['w13'], 'L1_ffn_w2': _L1_ffn_in['w2'], 'L1_ffn_w13_s': _L1_ffn_in['w13_s'], 'L1_ffn_w2_s': _L1_ffn_in['w2_s']}
    _x0 = _d['L0_attn_x']
    _d['L0_attn_x'] = jax.random.normal(jax.random.fold_in(jax.random.key(seed), 1), (1, 4096, 256), dtype=_x0.dtype)
    del _x0
    return _d

def reference(L0_attn_x, L0_attn_w_in, L0_attn_b_in, L0_attn_A, L0_attn_Bm, L0_attn_Cm, L0_attn_Dv, L0_attn_w_out, L0_attn_b_out, L0_attn_g_norm, L0_ffn_wg, L0_ffn_w1, L0_ffn_b1, L0_ffn_w2, L0_ffn_b2, L1_attn_Wq_down, L1_attn_Wk_down, L1_attn_Wv_down, L1_attn_Wq_up_c, L1_attn_Wq_up_e, L1_attn_Wk_up_c, L1_attn_Wk_up_e, L1_attn_Wv_up, L1_attn_Wc, L1_ffn_input_ids, L1_ffn_gate_w, L1_ffn_gate_b, L1_ffn_w13, L1_ffn_w2, L1_ffn_w13_s, L1_ffn_w2_s):

    def _L0_attn_ref(x, w_in, b_in, A, Bm, Cm, Dv, w_out, b_out, g_norm):
        import jax, jax.numpy as jnp
        import numpy as np
        BATCH, SEQ, D_MODEL, D_STATE, TIMESCALE = (4, 512, 256, 64, 2)
        EPS = 1e-06

        def _reference_tuple_inner(x, w_in, b_in, A, Bm, Cm, Dv, w_out, b_out, g_norm):
            B, L, D = x.shape
            S = A.shape[1]
            ts = TIMESCALE
            x_sub = x[:, ::ts] if ts > 1 else x
            x_sub = x_sub * jax.lax.rsqrt(jnp.mean(jnp.square(x_sub), axis=-1, keepdims=True) + EPS) * g_norm
            xz = jnp.einsum('bld,ed->ble', x_sub, w_in) + b_in
            x_proj, gate = jnp.split(xz, 2, axis=-1)
            c_sum = Cm.sum(axis=0)
            h0 = jnp.zeros((B, D, S), dtype=x.dtype)

            def step(h, xt):
                h = jnp.tanh(h * A + xt[:, :, None] * Bm)
                y = h @ c_sum + Dv * xt
                return (h, y)
            h_last, ys = jax.lax.scan(step, h0, jnp.swapaxes(x_proj, 0, 1))
            out = jnp.swapaxes(ys, 0, 1)
            out = out * jax.nn.silu(gate)
            out = jnp.einsum('bld,ed->ble', out, w_out) + b_out
            if ts > 1:
                out = jnp.repeat(out, ts, axis=1)[:, :L]
            return (out, h_last)
        return _reference_tuple_inner(x, w_in, b_in, A, Bm, Cm, Dv, w_out, b_out, g_norm)[0]

    def _L0_ffn_ref(x, wg, w1, b1, w2, b2):
        import jax, jax.numpy as jnp
        import numpy as np
        B, S, D = (2, 512, 256)
        E, K, H = (8, 2, 1024)
        CAP_FACTOR = 1.0

        def _moe_forward(x, wg, w1, b1, w2, b2):
            Bb, Ss, Dd = x.shape
            T = Bb * Ss
            cap = int(K * CAP_FACTOR * ((T + E - 1) // E))
            xt = x.reshape(T, Dd)
            logits = xt @ wg
            scores = jax.nn.softmax(logits, axis=-1)
            gates_k, idx_k = jax.lax.top_k(scores, K)
            gates_k = gates_k / jnp.sum(gates_k, axis=-1, keepdims=True)
            masks = jax.nn.one_hot(idx_k, E, dtype=jnp.int32)
            m = jnp.transpose(masks, (1, 0, 2)).reshape(K * T, E)
            locs_full = jnp.cumsum(m, axis=0) - 1
            loc = jnp.sum(locs_full * m, axis=-1)
            loc = loc.reshape(K, T).T
            valid = (loc < cap).astype(xt.dtype)
            loc_c = jnp.clip(loc, 0, cap - 1)
            contrib = (xt[:, None, :] * valid[:, :, None]).reshape(T * K, Dd)
            disp = jnp.zeros((E, cap, Dd), xt.dtype)
            disp = disp.at[idx_k.reshape(-1), loc_c.reshape(-1)].add(contrib)
            h = jax.nn.relu(jnp.einsum('ecd,edh->ech', disp, w1) + b1[:, None, :])
            out = jnp.einsum('ech,ehd->ecd', h, w2) + b2[:, None, :]
            gathered = out[idx_k, loc_c]
            y = jnp.einsum('tk,tkd->td', gates_k * valid, gathered)
            return y.reshape(Bb, Ss, Dd)
        return _moe_forward(x, wg, w1, b1, w2, b2)

    def _L1_attn_ref(x, Wq_down, Wk_down, Wv_down, Wq_up_c, Wq_up_e, Wk_up_c, Wk_up_e, Wv_up, Wc):
        import jax, jax.numpy as jnp
        import numpy as np
        import math
        B, T, C = (2, 512, 256)
        H, L = (16, 64)
        DH = C // H
        DHE = DH // 2
        THETA = 10000.0

        def _rope_cache(t, dim):
            inv_freq = 1.0 / THETA ** (jnp.arange(0, dim, 2, dtype=jnp.float32) / dim)
            freqs = jnp.arange(t, dtype=jnp.float32)[:, None] * inv_freq[None, :]
            emb = jnp.concatenate((freqs, freqs), axis=-1)
            return (jnp.cos(emb), jnp.sin(emb))

        def _apply_rope(x, cos, sin):
            x1 = x[..., 0::2]
            x2 = x[..., 1::2]
            rot = jnp.stack((-x2, x1), axis=-1).reshape(x.shape)
            return x * cos[None, None] + rot * sin[None, None]
        b, t, c = x.shape
        q_lat = (x @ Wq_down).reshape(b, t, H, L)
        k_lat = (x @ Wk_down).reshape(b, t, H, L)
        v_lat = (x @ Wv_down).reshape(b, t, H, L)
        q_c = jnp.einsum('bthl,ld->bhtd', q_lat, Wq_up_c)
        q_e = jnp.einsum('bthl,ld->bhtd', q_lat, Wq_up_e)
        k_c = jnp.einsum('bthl,ld->bhtd', k_lat, Wk_up_c)
        k_e = jnp.einsum('bthl,ld->bhtd', k_lat, Wk_up_e)
        v = jnp.einsum('bthl,ld->bhtd', v_lat, Wv_up)
        cos, sin = _rope_cache(t, DHE)
        q = jnp.concatenate([q_c, _apply_rope(q_e, cos, sin)], axis=-1)
        k = jnp.concatenate([k_c, _apply_rope(k_e, cos, sin)], axis=-1)
        scale = 1.0 / math.sqrt(DH)
        scores = jnp.einsum('bhqd,bhkd->bhqk', q, k) * scale
        causal = jnp.tril(jnp.ones((t, t), dtype=bool))
        scores = jnp.where(causal[None, None], scores, -jnp.inf)
        att = jax.nn.softmax(scores, axis=-1)
        y = jnp.einsum('bhqk,bhkd->bhqd', att, v)
        y = y.transpose(0, 2, 1, 3).reshape(b, t, c)
        return y @ Wc

    def _L1_ffn_ref(x, input_ids, gate_w, gate_b, w13, w2, w13_s, w2_s):
        import jax, jax.numpy as jnp
        import numpy as np
        from jax import lax
        DIM = 256
        INTER = 128
        N_EXPERTS = 16
        TOPK = 4
        ROUTE_SCALE = 2.5
        VOCAB = 8000

        def _silu_and_mul(gu):
            gate, up = jnp.split(gu, 2, axis=-1)
            return jax.nn.silu(gate) * up
        B, S, D = x.shape
        xt = x.reshape(-1, D)
        T = xt.shape[0]
        scores = jax.nn.sigmoid(xt.astype(jnp.float32) @ gate_w.T)
        biased = scores + gate_b
        _, idx = lax.top_k(biased, TOPK)
        w = jnp.take_along_axis(scores, idx, axis=-1)
        w = w / jnp.sum(w, axis=-1, keepdims=True)
        w = w * ROUTE_SCALE
        comb = jnp.zeros((T, N_EXPERTS), jnp.float32)
        comb = comb.at[jnp.arange(T)[:, None], idx].add(w)
        comb = comb.astype(x.dtype)

        def expert_body(y, args):
            w13_e, w2_e, c_e = args
            h = _silu_and_mul(xt @ w13_e.T)
            return (y + c_e[:, None] * (h @ w2_e.T), None)
        y, _ = lax.scan(expert_body, jnp.zeros_like(xt), (w13, w2, comb.T))
        y = y + _silu_and_mul(xt @ w13_s.T) @ w2_s.T
        return y.astype(x.dtype).reshape(B, S, D)
    x = L0_attn_x
    x = _layernorm(x + _L0_attn_ref(x, L0_attn_w_in, L0_attn_b_in, L0_attn_A, L0_attn_Bm, L0_attn_Cm, L0_attn_Dv, L0_attn_w_out, L0_attn_b_out, L0_attn_g_norm), axis=-1)
    x = _layernorm(x + _L0_ffn_ref(x, L0_ffn_wg, L0_ffn_w1, L0_ffn_b1, L0_ffn_w2, L0_ffn_b2), axis=-1)
    x = _layernorm(x + _L1_attn_ref(x, L1_attn_Wq_down, L1_attn_Wk_down, L1_attn_Wv_down, L1_attn_Wq_up_c, L1_attn_Wq_up_e, L1_attn_Wk_up_c, L1_attn_Wk_up_e, L1_attn_Wv_up, L1_attn_Wc), axis=-1)
    x = _layernorm(x + _L1_ffn_ref(x, L1_ffn_input_ids, L1_ffn_gate_w, L1_ffn_gate_b, L1_ffn_w13, L1_ffn_w2, L1_ffn_w13_s, L1_ffn_w2_s), axis=-1)
    return x

_drawn_inputs = setup_inputs


def setup_inputs(seed=0):
    import zlib

    import numpy as np

    out = dict(_drawn_inputs(seed))
    spreads = {'L0_attn_b_in': (0.0, 0.1),
     'L0_attn_Dv': (1.0, 0.6),
     'L0_attn_b_out': (0.0, 0.1),
     'L0_attn_g_norm': (1.0, 0.6),
     'L0_ffn_b1': (0.0, 0.1),
     'L0_ffn_b2': (0.0, 0.1)}
    factors = {'L0_attn_A': 8.0,
     'L0_attn_Bm': 8.0,
     'L0_attn_Cm': 8.0,
     'L1_attn_Wq_down': 8.0,
     'L1_attn_Wk_down': 8.0,
     'L1_attn_Wv_down': 8.0,
     'L1_attn_Wq_up_c': 8.0,
     'L1_attn_Wq_up_e': 8.0,
     'L1_attn_Wk_up_c': 8.0,
     'L1_attn_Wk_up_e': 8.0,
     'L1_attn_Wv_up': 8.0,
     'L1_attn_Wc': 8.0,
     'L1_ffn_gate_w': 4.521,
     'L1_ffn_gate_b': 8.0,
     'L1_ffn_w13': 3.801,
     'L1_ffn_w2': 3.792,
     'L1_ffn_w13_s': 4.745,
     'L1_ffn_w2_s': 4.758}
    for name, (base, spread) in spreads.items():
        noise = np.random.default_rng([zlib.crc32(name.encode()), seed]).standard_normal(out[name].shape)
        drawn = base * np.exp(spread * noise) if base else spread * noise
        out[name] = jnp.asarray(drawn.astype(out[name].dtype))
    for name, factor in factors.items():
        out[name] = (out[name] * factor).astype(out[name].dtype)
    return out
```

```python
from contextlib import ExitStack

import concourse.bass as bass
from concourse import mybir

P = 128
ACT = mybir.ActivationFunctionType
ALU = mybir.AluOpType
AX = mybir.AxisListType
F32 = mybir.dt.float32
BF16 = mybir.dt.bfloat16
U32 = mybir.dt.uint32
F32R = mybir.dt.float32r

T = 4096
D = 256
DH = D // P
TS = 2
TP = T // TS
NS = 64
NT = T // P
NPAIR = TP // P
CH = 512
CHUNKS = 8
LEN = TP // CHUNKS
WARM = 32
BL = 8
RING_X = 4
XW = WARM + TP + LEN - BL + 2 * BL
RMS_EPS = 1e-6
LN_EPS = 1e-5


HIGH, LOW = 0, 1
SPLIT = ((HIGH, HIGH), (LOW, HIGH), (HIGH, LOW))


class Parts:
    pass


class Steps:

    def __init__(self, sem, base=0):
        self.sem, self.base, self.n = sem, base, 0

    def link(self, eng, ins):
        self.n += 1
        ins.then_inc(self.sem, 1)
        eng.wait_ge(self.sem, self.base + self.n)


def project_in(nc, k, a):
    with ExitStack() as ctx:
        sb, sem = k.sbuf(ctx), k.stage_sem
        xT = sb("xsT", [P, DH, TP])
        sq = sb("xsq", [P, 2, DH, CH])
        rms = sb("rms", [P, 2, CH])
        sig = sb("gate_sig", [P, 2, CH])
        w = sb("w_in_sb", [P, DH, 2 * D])
        g = sb("g_norm_sb", [P, DH])
        b = sb("b_in_sb", [P, 2 * DH])
        w_in, gb_in = sem("w_in_in"), sem("gb_in")
        x_in = [sem(f"xsT_in{c}") for c in range(TP // CH)]
        const_ready, squares, meansq, root, scaled = (sem(n) for n in (
            "ones_ready", "squares_ready", "meansq_ready", "root_ready", "scaled_ready"))
        inv_ready, projected, drained, sigmoid, gated = (sem(n) for n in (
            "inv_rms_ready", "xz_ready", "xz_drained", "gate_sigmoid", "gate_done"))
        NC = TP // CH
        ps = k.psum
        block = ctx.enter_context(nc.Block())

        @block.sync
        def _(sp):
            for c in range(NC):
                sp.dma_start(xT[:, :, c * CH:(c + 1) * CH],
                             a["xs_T"].rearrange("(h p) t -> p h t", p=P)[:, :, c * CH:(c + 1) * CH]).then_inc(x_in[c], 16)
                if c == 0:
                    sp.dma_start(g[:, :], a["g_norm"].rearrange("(h p) -> p h", p=P),
                                 allow_slow_non_contiguous=True).then_inc(gb_in, 16)
                    sp.dma_start(b[:, :], a["b_in"].rearrange("(e p) -> p e", p=P),
                                 allow_slow_non_contiguous=True).then_inc(gb_in, 16)
                    sp.dma_start(w[:, :, :], a["w_in_T"].rearrange("(h p) e -> p h e", p=P)).then_inc(w_in, 16)
            sp.wait_ge(k.zeros_ready, 1)
            for e in range(8):
                sp.dma_start(a["inbox"][e * 1024:(e + 1) * 1024, :].rearrange("(s p) c -> p s c", p=P),
                             k.zeros[:, :].unsqueeze(1).to_broadcast([P, 8, D])).then_inc(k.inbox_zeroed, 16)

        @block.gpsimd
        def _(pool):
            pool.memset(k.ident[:, :], 0.0).then_inc(const_ready, 1)
            pool.memset(k.ones[:, :], 1.0).then_inc(const_ready, 1)
            pool.memset(k.eps[:, 0:1], RMS_EPS).then_inc(const_ready, 1)
            pool.memset(k.eps[:, 1:2], LN_EPS).then_inc(const_ready, 1)
            pool.memset(k.zeros[:, :], 0.0).then_inc(k.zeros_ready, 1)
            pool.wait_ge(const_ready, 4)
            pool.affine_select(out=k.ident[:, :], in_=k.ident[:, :], compare_op=ALU.not_equal, fill=1.0,
                               base=0, pattern=[[-1, P]], channel_multiplier=1).then_inc(const_ready, 1)

        @block.vector
        def _(dve):
            dve.memset(k.xpT[:, :, 0:WARM], 0.0)
            dve.memset(k.xpT[:, :, WARM + TP:], 0.0)
            dve.wait_ge(gb_in, 32)
            for c in range(NC):
                cols = slice(c * CH, (c + 1) * CH)
                dve.wait_ge(x_in[c], 16)
                if c >= 2:
                    dve.wait_ge(meansq, c - 1)
                dve.tensor_tensor(sq[:, c % 2, :, :], xT[:, :, cols], xT[:, :, cols], ALU.mult).then_inc(squares, 1)
            for c in range(NC):
                cols = slice(c * CH, (c + 1) * CH)
                dve.wait_ge(root, c + 1)
                dve.reciprocal(rms[:, c % 2, :], rms[:, c % 2, :]).then_inc(inv_ready, 1)
                dve.wait_ge(inv_ready, c + 1)
                for h in range(DH):
                    dve.scalar_tensor_tensor(xT[:, h, cols], xT[:, h, cols], g[:, h:h + 1], rms[:, c % 2, :],
                                             ALU.mult, ALU.mult).then_inc(scaled, 1)
            for c in range(NC):
                cols = slice(c * CH, (c + 1) * CH)
                for h in range(DH):
                    n = c * DH + h
                    dve.wait_ge(sigmoid, n + 1)
                    dve.scalar_tensor_tensor(k.gateT[:, h, cols], ps[:, 4 + n % 2, :], b[:, DH + h:DH + h + 1],
                                             sig[:, n % 2, :], ALU.add, ALU.mult).then_inc(gated, 1)

        @block.tensor
        def _(pe):
            pe.wait_ge(const_ready, 5)
            for c in range(NC):
                pe.wait_ge(squares, c + 1)
                for h in range(DH):
                    last = pe.matmul(ps[:, c, :], k.ones[:, :], sq[:, c % 2, h, :], start=(h == 0), stop=(h == DH - 1))
                last.then_inc(meansq, 1)
            pe.wait_ge(w_in, 16)
            for c in range(NC):
                cols = slice(c * CH, (c + 1) * CH)
                pe.wait_ge(scaled, DH * (c + 1))
                for e in range(2 * DH):
                    bank = 6 + e if e < DH else 4 + (e - DH)
                    if c >= 1:
                        if e < DH:
                            pe.wait_ge(drained, DH * (c - 1) + e + 1)
                        else:
                            pe.wait_ge(gated, DH * (c - 1) + e - DH + 1)
                    for h in range(DH):
                        last = pe.matmul(ps[:, bank, :], w[:, h, e * P:(e + 1) * P], xT[:, h, cols],
                                         start=(h == 0), stop=(h == DH - 1))
                    last.then_inc(projected, 1)

        @block.scalar
        def _(act):
            act.wait_ge(const_ready, 5)
            for c in range(NC):
                act.wait_ge(meansq, c + 1)
                if c >= 2:
                    act.wait_ge(scaled, DH * (c - 1))
                act.activation(rms[:, c % 2, :], ps[:, c, :], ACT.Sqrt, bias=k.eps[:, 0:1], scale=1.0 / D).then_inc(root, 1)
            for c in range(NC):
                cols = slice(c * CH, (c + 1) * CH)
                for e in range(2 * DH):
                    act.wait_ge(projected, 2 * DH * c + e + 1)
                    if e < DH:
                        act.activation(k.xpT[:, e, WARM + c * CH:WARM + (c + 1) * CH], ps[:, 6 + e, :], ACT.Identity, bias=b[:, e:e + 1]).then_inc(drained, 1)
                    else:
                        n = c * DH + e - DH
                        if n >= 2:
                            act.wait_ge(gated, n - 1)
                        act.activation(sig[:, n % 2, :], ps[:, 4 + n % 2, :], ACT.Sigmoid, bias=b[:, e:e + 1]).then_inc(sigmoid, 1)


def load_scan_weights(nc, k, a):
    with ExitStack() as loc:
        cm = k.sbuf(loc)("cm_sb", [P, DH, NS])
        ab_in, csum, copied, a_copied = k.sem("ab_in"), k.sem("csum_ready"), k.sem("csum_copied"), k.sem("a_copied")
        block = loc.enter_context(nc.Block())

        @block.sync
        def _(sp):
            for dst, src in ((k.A, a["A"]), (k.B, a["Bm"]), (cm, a["Cm"])):
                sp.dma_start(dst[:, :, :], src.rearrange("(h p) s -> p h s", p=P)).then_inc(ab_in, 16)
            sp.dma_start(k.Dv[:, :], a["Dv"].rearrange("(h p) -> p h", p=P), allow_slow_non_contiguous=True).then_inc(ab_in, 16)
            sp.dma_start(a["x_proj"].rearrange("(h p) t -> p h t", p=P), k.xpT[:, :, WARM:WARM + TP]).then_inc(k.x_saved, 16)

        @block.tensor
        def _(pe):
            pe.wait_ge(ab_in, 64)
            for h in range(DH):
                last = pe.matmul(k.psum[:, 1, 0:NS], k.ones[:, :], cm[:, h, :], start=(h == 0), stop=(h == DH - 1))
            last.then_inc(csum, 1)

        @block.vector
        def _(dve):
            dve.wait_ge(ab_in, 64)
            dve.tensor_copy(k.psum[:, 0, 0:DH * NS].rearrange("p (h s) -> p h s", h=DH), k.A[:, :, :]).then_inc(a_copied, 1)
            dve.wait_ge(csum, 1)
            dve.tensor_copy(k.csum[:, 0, :], k.psum[:, 1, 0:NS]).then_inc(copied, 1)
            dve.tensor_copy(k.csum[:, 1, :], k.psum[:, 1, 0:NS]).then_inc(copied, 1)


def scan_chunks(nc, k, a):
    GW = CHUNKS * NS
    NMAIN = LEN // BL
    NWARM = WARM // BL
    with ExitStack() as ctx:
        sb, sem = k.sbuf(ctx), k.stage_sem
        hist = sb("h_hist", [P, 2, BL, DH, GW])
        diag = sb("csum_diag", [P, NS, P])
        xb = sb("x_times_b", [P, RING_X, DH, GW])
        xs = sb("x_slab", [P, 2, DH, CHUNKS, BL])
        warm = sb("warm_end", [P, DH, GW])
        diff = sb("seam_diff", [P, DH, CHUNKS - 1, NS])
        count = sb("seam_count", [P, 1])
        xs_ready, xb_ready, ha_ready, u_ready, h_ready, y_done, y_taken, h_zero, diags, warm_kept = (
            sem("ch_" + n) for n in ("xs", "xb", "ha", "u", "h", "y_done", "y_taken", "h_zero", "diag", "warm"))
        compared, counted, summed, told = (sem("ch_" + n) for n in ("compared", "counted", "summed", "told"))
        ps = k.psum
        ha, u = ps[:, 3:5, :], ps[:, 5:7, :]
        block = ctx.enter_context(nc.Block())

        def ring(B):
            return (B - NWARM) % 2

        @block.vector
        def _(dve):
            dve.memset(hist[:, ring(-1), BL - 1, :, :], 0.0).then_inc(h_zero, 1)
            for s in range(NS):
                last = dve.tensor_scalar(diag[:, s, :], k.ident[:, :], k.csum[:, 0, s:s + 1], None, ALU.mult)
            last.then_inc(diags, 1)

            def slab(B, slot):
                src = k.xpT[:, :, bass.ds(B * BL, TP)].rearrange("p h (c l) -> p h c l", l=LEN)[:, :, :, 0:BL]
                dve.tensor_scalar(xs[:, slot, :, :, :], src, 1.0, None, ALU.mult).then_inc(xs_ready, 1)

            def steps(B, slot):
                for t in range(BL):
                    prev = hist[:, slot, t - 1] if t else hist[:, 1 - slot, BL - 1]
                    for g in range(DH):
                        n = 2 * BL * B + 2 * t + g
                        if isinstance(n, int) and n < 2:
                            dve.wait_ge(h_zero, 1)
                        else:
                            dve.wait_ge(h_ready, n - 1)
                        dve.tensor_tensor(ha[:, g, :].rearrange("p (c s) -> p c s", s=NS), prev[:, g, :].rearrange("p (c s) -> p c s", s=NS),
                                          ps[:, 0, g * NS:(g + 1) * NS].unsqueeze(1).to_broadcast([P, CHUNKS, NS]), ALU.mult).then_inc(ha_ready, 1)
                        dve.wait_ge(xb_ready, n + 1)
                        dve.wait_ge(ha_ready, n + 1)
                        dve.tensor_tensor(u[:, g, :], ha[:, g, :], xb[:, t % RING_X, g, :], ALU.add).then_inc(u_ready, 1)

            def take_y(m, bank):
                dve.wait_ge(y_done, m + 1)
                for h in range(DH):
                    cols = k.xpT[:, h, bass.ds(WARM + m * BL, TP)].rearrange("p (c l) -> p c l", l=LEN)[:, :, 0:BL]
                    last = dve.scalar_tensor_tensor(cols, cols, k.Dv[:, h:h + 1],
                                                    ps[:, 1 + bank, 0:BL * DH * CHUNKS].rearrange("p (t h c) -> p h c t", t=BL, h=DH)[:, h],
                                                    ALU.mult, ALU.add)
                last.then_inc(y_taken, 1)

            slab(0, ring(0))
            for B in range(NWARM):
                slab(B + 1, ring(B + 1))
                steps(B, ring(B))
            dve.wait_ge(k.x_saved, 16)
            slab(NWARM + 1, 1)
            steps(NWARM, 0)
            slab(NWARM + 2, 0)
            steps(NWARM + 1, 1)
            take_y(0, 0)
            with dve.Fori(1, NMAIN // 2) as i:
                slab(NWARM + 2 * i + 1, 1)
                steps(NWARM + 2 * i, 0)
                take_y(2 * i - 1, 1)
                slab(NWARM + 2 * i + 2, 0)
                steps(NWARM + 2 * i + 1, 1)
                take_y(2 * i, 0)
            dve.wait_ge(h_ready, 2 * (WARM + LEN))
            dve.wait_ge(warm_kept, 2)
            for g in range(DH):
                last = dve.tensor_tensor(diff[:, g, :, :].rearrange("p c s -> p (c s)"), warm[:, g, NS:], hist[:, 1, BL - 1, g, 0:GW - NS], ALU.not_equal)
            last.then_inc(compared, 1)
            dve.wait_ge(compared, 1)
            dve.tensor_reduce(count[:, :], diff[:, :, :, :].rearrange("p h c s -> p (h c s)"), AX.X, ALU.add).then_inc(counted, 1)
            take_y(NMAIN - 1, 1)
            dve.wait_ge(summed, 1)
            dve.tensor_copy(k.bad[:, :], ps[:, 7, 0:1]).then_inc(told, 1)
            dve.wait_ge(told, 1)

        @block.gpsimd
        def _(pool):
            def products(B, slot):
                pool.wait_ge(xs_ready, B + 1)
                for t in range(BL):
                    for g in range(DH):
                        n = 2 * BL * B + 2 * t + g
                        if not isinstance(n, int) or n >= 2 * RING_X:
                            pool.wait_ge(u_ready, n - 2 * RING_X + 1)
                        pool.tensor_tensor(xb[:, t % RING_X, g, :].rearrange("p (c s) -> p c s", s=NS),
                                           xs[:, slot, g, :, t].unsqueeze(2).to_broadcast([P, CHUNKS, NS]),
                                           k.B[:, g, :].unsqueeze(1).to_broadcast([P, CHUNKS, NS]), ALU.mult).then_inc(xb_ready, 1)

            for B in range(NWARM):
                products(B, ring(B))
            with pool.Fori(0, NMAIN // 2) as i:
                products(NWARM + 2 * i, 0)
                products(NWARM + 2 * i + 1, 1)

        @block.scalar
        def _(act):
            def steps(B, slot):
                for t in range(BL):
                    for g in range(DH):
                        n = 2 * BL * B + 2 * t + g
                        act.wait_ge(u_ready, n + 1)
                        if isinstance(B, int) and B == NWARM - 1 and t == BL - 1:
                            act.activation(warm[:, g, :], u[:, g, :], ACT.Tanh).then_inc(warm_kept, 1)
                        act.activation(hist[:, slot, t, g, :], u[:, g, :], ACT.Tanh).then_inc(h_ready, 1)

            for B in range(NWARM + 2):
                steps(B, ring(B))
            with act.Fori(1, NMAIN // 2) as i:
                for j in range(2):
                    act.wait_ge(y_done, 2 * i + j - 1)
                    steps(NWARM + 2 * i + j, j)

        @block.tensor
        def _(pe):
            pe.wait_ge(diags, 1)

            def outputs(m, j):
                pe.wait_ge(h_ready, 2 * BL * (NWARM + m + 1))
                for s in range(NS):
                    last = pe.matmul(ps[:, 1 + j, 0:BL * DH * CHUNKS], diag[:, s, :],
                                     hist[:, j, :, :, :].rearrange("p t h (c s) -> p (t h) c s", s=NS)[:, :, :, s],
                                     start=(s == 0), stop=(s == NS - 1))
                last.then_inc(y_done, 1)

            outputs(0, 0)
            outputs(1, 1)
            with pe.Fori(1, NMAIN // 2) as i:
                for j in range(2):
                    pe.wait_ge(y_taken, 2 * i + j - 1)
                    outputs(2 * i + j, j)
            pe.wait_ge(counted, 1)
            pe.matmul(ps[:, 7, 0:1], k.ones[:, :], count[:, :], start=True, stop=True).then_inc(summed, 1)


def reload_x(nc, k, a):
    with ExitStack() as loc:
        back = k.sem("x_back")
        block = loc.enter_context(nc.Block())

        @block.sync
        def _(sp):
            sp.dma_start(k.xpT[:, :, WARM:WARM + TP], a["x_proj"].rearrange("(h p) t -> p h t", p=P)).then_inc(back, 16)
            sp.wait_ge(back, 16)


def scan_steps(nc, k, a):
    U = 8
    with ExitStack() as ctx:
        sb, sem = k.sbuf(ctx), k.stage_sem
        h = sb("seq_h", [P, 2, DH, NS])
        ha = sb("seq_ha", [P, 2, DH, NS])
        u = sb("seq_u", [P, 2, DH, NS])
        junk = sb("seq_junk", [P, NS])
        xs = sb("seq_x", [P, DH, U])
        ys = sb("seq_y", [P, DH, U])
        zeroed, x_slab, ha_ready, u_ready, h_ready, y_ready, y_saved = (sem("seq_" + n) for n in (
            "zeroed", "x_slab", "ha_ready", "u_ready", "h_ready", "y_ready", "y_saved"))
        block = ctx.enter_context(nc.Block())

        @block.vector
        def _(dve):
            dve.memset(h[:, (U - 1) % 2, :, :], 0.0).then_inc(zeroed, 1)
            dve.wait_ge(zeroed, 1)
            with dve.Fori(0, TP // U) as i:
                base = i * U
                dve.tensor_copy(xs[:, :, :], k.xpT[:, :, bass.ds(base + WARM, U)]).then_inc(x_slab, 1)
                dve.wait_ge(x_slab, i + 1)
                for t in range(U + 1):
                    if t < U:
                        if t > 0:
                            dve.wait_ge(h_ready, base + t)
                        dve.tensor_tensor(ha[:, t % 2, :, :], h[:, (t - 1) % 2, :, :], k.A[:, :, :], ALU.mult).then_inc(ha_ready, 1)
                        dve.wait_ge(ha_ready, base + t + 1)
                        for c in range(DH):
                            last = dve.scalar_tensor_tensor(u[:, t % 2, c, :], k.B[:, c, :], xs[:, c, t:t + 1], ha[:, t % 2, c, :],
                                                            ALU.mult, ALU.add)
                        last.then_inc(u_ready, 1)
                    else:
                        dve.wait_ge(h_ready, base + U)
                    if t > 0:
                        for c in range(DH):
                            last = dve.tensor_tensor_reduce(out=junk[:, :], in0=h[:, (t - 1) % 2, c, :], in1=k.csum[:, c, :],
                                                            scale=1.0, scalar=0.0, op0=ALU.mult, op1=ALU.add,
                                                            accum_out=ys[:, c, t - 1:t])
                            last.then_inc(y_ready, 1)
                            dve.wait_ge(y_ready, (base + t - 1) * DH + c + 1)
                for c in range(DH):
                    last = dve.scalar_tensor_tensor(k.xpT[:, c, bass.ds(base + WARM, U)], xs[:, c, :], k.Dv[:, c:c + 1], ys[:, c, :],
                                                    ALU.mult, ALU.add)
                last.then_inc(y_saved, 1)
                dve.wait_ge(y_saved, i + 1)

        @block.scalar
        def _(act):
            with act.Fori(0, TP // U) as i:
                for t in range(U):
                    act.wait_ge(u_ready, i * U + t + 1)
                    act.activation(h[:, t % 2, :, :], u[:, t % 2, :, :], ACT.Tanh).then_inc(h_ready, 1)


def free_semaphores(nc, k):
    nc.all_engine_barrier()
    nc.clear_and_free_semaphores(k.passing)
    nc.all_engine_barrier()
    k.passing = []


def layer_norm_stats(dve, k, n, done):
    dve.bn_stats(k.stats[:, n, :], k.stream[:, n, :]).then_inc(done, 1)


def layer_norm(nc, k):
    turn = k.ln_turn
    k.ln_turn += 1
    added, aggregated, root, inv, done = k.ln_sems
    with nc.Block() as block:
        @block.vector
        def _(dve):
            for n in range(NT):
                layer_norm_stats(dve, k, n, added)
            for n in range(NT):
                dve.wait_ge(added, NT * turn + n + 1)
                dve.bn_aggr(k.moments[:, n, :], k.stats[:, n, :]).then_inc(aggregated, 1)
            dve.wait_ge(root, turn + 1)
            dve.reciprocal(k.rstd[:, :], k.rstd[:, :]).then_inc(inv, 1)
            dve.wait_ge(inv, turn + 1)
            for n in range(NT):
                dve.tensor_scalar(k.stream[:, n, :], k.stream[:, n, :], k.moments[:, n, 0:1], k.rstd[:, n:n + 1],
                                  ALU.subtract, ALU.mult).then_inc(done, 1)

        @block.scalar
        def _(act):
            act.wait_ge(aggregated, NT * (turn + 1))
            act.activation(k.rstd[:, :], k.moments[:, :, 1], ACT.Sqrt, bias=k.eps[:, 1:2]).then_inc(root, 1)


def project_out(nc, k, a):
    with ExitStack() as ctx:
        sb, sem = k.sbuf(ctx), k.stage_sem
        w = sb("w_out_sb", [P, DH, D])
        bo = sb("b_out_sb", [1, D])
        loaded, z_ready, projected, added = (sem("po_" + n) for n in ("loaded", "z", "proj", "added"))
        block = ctx.enter_context(nc.Block())

        @block.sync
        def _(sp):
            sp.dma_start(w[:, :, :], a["w_out_T"].rearrange("(h p) e -> p h e", p=P)).then_inc(loaded, 16)
            sp.dma_start(k.stream[:, :, :].rearrange("p (i j) c -> p i (j c)", j=2),
                         a["x"].rearrange("(i p j) c -> p i (j c)", p=P, j=2)).then_inc(k.x_loaded, 16)
            sp.dma_start(bo[:, :], a["b_out"].rearrange("(o e) -> o e", o=1)).then_inc(loaded, 16)

        @block.vector
        def _(dve):
            NC = TP // CH
            for c in range(NC):
                cols = slice(c * CH, (c + 1) * CH)
                for h in range(DH):
                    dve.tensor_tensor(k.gateT[:, h, cols], k.xpT[:, h, WARM + c * CH:WARM + (c + 1) * CH],
                                      k.gateT[:, h, cols], ALU.mult).then_inc(z_ready, 1)
            dve.wait_ge(k.x_loaded, 16)
            for i in range(NPAIR):
                dve.wait_ge(projected, i + 1)
                pair = k.stream[:, 2 * i:2 * i + 2, :]
                dve.tensor_tensor(pair, pair, k.psum[:, i % 8, 0:D].unsqueeze(1).to_broadcast([P, 2, D]), ALU.add).then_inc(added, 1)

        @block.tensor
        def _(pe):
            pe.wait_ge(loaded, 32)
            for i in range(NPAIR):
                pe.wait_ge(z_ready, DH * (i * P // CH + 1))
                if i >= 8:
                    pe.wait_ge(added, i - 7)
                acc = k.psum[:, i % 8, 0:D]
                for h in range(DH):
                    pe.matmul(acc, k.gateT[:, h, i * P:(i + 1) * P], w[:, h, :], start=(h == 0), stop=False)
                pe.matmul(acc, k.ones[0:1, :], bo[:, :], start=False, stop=True).then_inc(projected, 1)


E_MOE = 8
K_MOE = 2
HID = 1024
CAP = K_MOE * ((T + E_MOE - 1) // E_MOE)
SLOTS = E_MOE * CAP


def make_indices(nc, k):
    with ExitStack() as loc:
        iota_i = k.sbuf(loc)("iota_i", [P, 16], mybir.dt.int32)
        made, tri = k.sem("iota_made"), k.sem("tri_made")
        block = loc.enter_context(nc.Block())

        @block.gpsimd
        def _(pool):
            pool.iota(iota_i[:, :], pattern=[[1, 16]], base=0, channel_multiplier=0).then_inc(made, 1)
            pool.memset(k.before[:, :], 1.0).then_inc(tri, 1)
            pool.wait_ge(tri, 1)
            pool.affine_select(out=k.before[:, :], in_=k.before[:, :], compare_op=ALU.is_ge, fill=0.0,
                               base=-1, pattern=[[1, P]], channel_multiplier=-1).then_inc(tri, 1)

        @block.vector
        def _(dve):
            dve.wait_ge(made, 1)
            dve.tensor_copy(k.iota[:, :], iota_i[:, :]).then_inc(made, 1)


def route_tokens(nc, k, a):
    with ExitStack() as ctx:
        sb, sem = k.sbuf(ctx), k.stage_sem
        wg = sb("wg_sb", [P, DH, E_MOE])
        xt = sb("route_xT", [P, 2, D])
        logits = sb("route_logits", [P, NT, E_MOE])
        top = sb("route_top", [P, NT, 8])
        top_i = sb("route_top_i", [P, NT, 8], U32)
        choice = sb("route_choice", [P, K_MOE, NT])
        mask = sb("route_mask", [P, K_MOE, NT, E_MOE])
        pairs = sb("route_pairs", [P, K_MOE, NPAIR, E_MOE])
        total = sb("route_total", [P, K_MOE, NPAIR, E_MOE])
        upto = sb("route_upto", [P, K_MOE, NPAIR, E_MOE])
        loc = sb("route_loc", [P, K_MOE, NT, E_MOE])
        slot = sb("route_slot", [P, K_MOE, NT])
        valid = sb("route_valid", [P, K_MOE, NT])
        row = sb("route_row", [P, K_MOE, NT])
        loaded, turned, copied, scored, step, prefixed, gap, put_ready = (sem("route_" + n) for n in (
            "loaded", "turned", "copied", "scored", "step", "prefixed", "gap", "put_ready"))
        es = sem("route_exp")
        ps = k.psum
        block = ctx.enter_context(nc.Block())

        @block.sync
        def _(sp):
            sp.dma_start(wg[:, :, :], a["wg"].rearrange("(h p) e -> p h e", p=P)).then_inc(loaded, 16)

        @block.tensor
        def _(pe):
            pe.wait_ge(loaded, 16)
            for n in range(NT + 1):
                if n < NT:
                    if n >= 2:
                        pe.wait_ge(copied, n - 1)
                    for h in range(DH):
                        last = pe.transpose(ps[:, n % 2, h * P:(h + 1) * P], k.stream[:, n, h * P:(h + 1) * P], k.ident[:, :])
                    last.then_inc(turned, 1)
                if n > 0:
                    m = n - 1
                    pe.wait_ge(copied, m + 1)
                    for h in range(DH):
                        last = pe.matmul(ps[:, 7, m * E_MOE:(m + 1) * E_MOE], xt[:, m % 2, h * P:(h + 1) * P], wg[:, h, :],
                                         start=(h == 0), stop=(h == DH - 1))
            last.then_inc(scored, 1)
            pe.wait_ge(step, 4)
            pe.matmul(ps[:, 6, 0:2 * P], k.before[:, :], pairs[:, :, :, :], start=True, stop=True)
            pe.matmul(ps[:, 5, 0:2 * P], k.ones[:, :], pairs[:, :, :, :], start=True, stop=True).then_inc(prefixed, 1)

        @block.scalar
        def _(act):
            for n in range(NT):
                act.wait_ge(turned, n + 1)
                if n >= 2:
                    act.wait_ge(turned, n + 1)
                act.activation(xt[:, n % 2, :], ps[:, n % 2, 0:D], ACT.Copy).then_inc(copied, 1)
            act.wait_ge(gap, 1)
            act.activation(k.gate[:, 1, :], k.gate[:, 0, :], ACT.Exp).then_inc(es, 1)

        @block.vector
        def _(dve):
            s = Steps(step)
            dve.wait_ge(scored, 1)
            s.link(dve, dve.tensor_copy(logits[:, :, :], ps[:, 7, 0:NT * E_MOE].rearrange("p (n e) -> p n e", e=E_MOE)))
            for n in range(NT):
                last = dve.max(top[:, n, :], logits[:, n, :])
            s.link(dve, last)
            for n in range(NT):
                last = dve.max_index(top_i[:, n, :], top[:, n, :], logits[:, n, :])
            s.link(dve, last)
            for c in range(K_MOE):
                last = dve.tensor_copy(choice[:, c, :], top_i[:, :, c])
            chosen = sem("route_chosen")
            last.then_inc(chosen, 1)
            dve.wait_ge(chosen, 1)
            for c in range(K_MOE):
                last = dve.tensor_tensor(mask[:, c, :, :], k.iota[:, 0:E_MOE].unsqueeze(1).to_broadcast([P, NT, E_MOE]),
                                         choice[:, c, :].unsqueeze(2).to_broadcast([P, NT, E_MOE]), ALU.is_equal)
            masked = sem("route_masked")
            last.then_inc(masked, 1)
            dve.wait_ge(masked, 1)
            for c in range(K_MOE):
                two = mask[:, c, :, :].rearrange("p (i j) e -> p i j e", j=2)
                last = dve.tensor_tensor(pairs[:, c, :, :], two[:, :, 0, :], two[:, :, 1, :], ALU.add)
            s.link(dve, last)
            dve.tensor_tensor(k.gate[:, 0, :], top[:, :, 1], top[:, :, 0], ALU.subtract).then_inc(gap, 1)
            dve.wait_ge(prefixed, 1)
            s.link(dve, dve.tensor_copy(total[:, :, :, :], ps[:, 5, 0:2 * P].rearrange("p (c i e) -> p c i e", c=K_MOE, e=E_MOE)))
            for e in range(E_MOE):
                last = dve.tensor_tensor_scan(upto[:, :, :, e].rearrange("p c i -> p (c i)"), k.ones[:, 0:K_MOE * NPAIR],
                                              total[:, :, :, e].rearrange("p c i -> p (c i)"), 0.0, ALU.mult, ALU.add)
            s.link(dve, last)
            s.link(dve, dve.tensor_tensor(upto[:, :, :, :], upto[:, :, :, :], total[:, :, :, :], ALU.subtract))
            s.link(dve, dve.tensor_tensor(upto[:, :, :, :], upto[:, :, :, :],
                                          ps[:, 6, 0:2 * P].rearrange("p (c i e) -> p c i e", c=K_MOE, e=E_MOE), ALU.add))
            for c in range(K_MOE):
                l2 = loc[:, c, :, :].rearrange("p (i j) e -> p i j e", j=2)
                m2 = mask[:, c, :, :].rearrange("p (i j) e -> p i j e", j=2)
                dve.tensor_copy(l2[:, :, 0, :], upto[:, c, :, :])
                last = dve.tensor_tensor(l2[:, :, 1, :], upto[:, c, :, :], m2[:, :, 0, :], ALU.add)
            s.link(dve, last)
            s.link(dve, dve.tensor_tensor(loc[:, :, :, :], loc[:, :, :, :], mask[:, :, :, :], ALU.mult))
            s.link(dve, dve.tensor_reduce(slot[:, :, :], loc[:, :, :, :], AX.X, ALU.add))
            s.link(dve, dve.tensor_scalar(valid[:, :, :], slot[:, :, :], float(CAP), None, ALU.is_lt))
            s.link(dve, dve.scalar_tensor_tensor(row[:, :, :], choice[:, :, :], float(CAP), slot[:, :, :], ALU.mult, ALU.add))
            s.link(dve, dve.tensor_scalar(slot[:, :, :], valid[:, :, :], float(-2 * SLOTS), float(2 * SLOTS), ALU.mult, ALU.add))
            s.link(dve, dve.tensor_tensor(slot[:, :, :], slot[:, :, :], row[:, :, :], ALU.add))
            dve.tensor_copy(k.put[:, :, :], slot[:, :, :]).then_inc(put_ready, 1)
            s.link(dve, dve.tensor_tensor(row[:, :, :], row[:, :, :], valid[:, :, :], ALU.mult))
            dve.tensor_copy(k.take[:, :, :], row[:, :, :]).then_inc(k.take_ready, 1)
            dve.wait_ge(es, 1)
            s.link(dve, dve.tensor_scalar(k.gate[:, 0, :], k.gate[:, 1, :], 1.0, None, ALU.add))
            s.link(dve, dve.reciprocal(k.gate[:, 0, :], k.gate[:, 0, :]))
            s.link(dve, dve.tensor_tensor(k.gate[:, 1, :], k.gate[:, 1, :], k.gate[:, 0, :], ALU.mult))
            s.link(dve, dve.tensor_tensor(k.gate[:, :, :], k.gate[:, :, :], valid[:, :, :], ALU.mult))


def experts(nc, k, a):
    ST = CAP // P
    HT = HID // P
    G = CH // P
    NQ = DH * ST // G
    NM = HT * CAP // CH
    NY = ST // 2
    with ExitStack() as ctx:
        sb, sem = k.sbuf(ctx), k.stage_sem
        w1_raw = sb("w1_raw", [P, DH, HID])
        w2_raw = sb("w2_raw", [P, HT, D])
        w1 = sb("w1_part", [P, 2, DH, HID], F32R)
        w2 = sb("w2_part", [P, 2, HT, D], F32R)
        xe = sb("xe_sb", [P, ST, D])
        xeT = sb("xeT_part", [P, 2, DH, CAP], F32R)
        hid = sb("hid_f32", [P, 2, CH])
        hT = sb("hT_part", [P, 2, HT, CAP], F32R)
        ye = sb("ye_sb", [P, ST, D])
        b1 = sb("b1_sb", [P, E_MOE, HT])
        b2 = sb("b2_sb", [P, E_MOE, D])
        b1e = sb("b1_now", [P, HT])
        b_in, b1_ready, x_in, w1_in, w2_in, w1_high, w1_low, w2_high, w2_low = (sem("moe_" + n) for n in (
            "biases", "b1_ready", "x_in", "w1_in", "w2_in", "w1_high", "w1_low", "w2_high", "w2_low"))
        turned, x_high, x_low, hidden, relued, hid_high, hid_low, summed, saved, y_out, y_free = (sem("moe_" + n) for n in (
            "turned", "x_high", "x_low", "hidden", "relued", "hid_high", "hid_low", "summed", "saved", "y_out", "y_free"))
        ps = k.psum
        block = ctx.enter_context(nc.Block())

        def all_experts(eng, body):
            with eng.Fori(0, E_MOE - 1) as e:
                body(e, True)
            body(E_MOE - 1, False)

        @block.sync
        def _(sp):
            def load_w1(e):
                sp.dma_start(w1_raw[:, :, :], a["w1"][bass.ds(e * D, D), :].rearrange("(h p) f -> p h f", p=P)).then_inc(w1_in, 16)

            def load_w2(e):
                sp.dma_start(w2_raw[:, :, :], a["w2"][bass.ds(e * HID, HID), :].rearrange("(t p) d -> p t d", p=P)).then_inc(w2_in, 16)

            def load_x(e):
                sp.dma_start(xe[:, :, :], a["inbox"][bass.ds(e * CAP, CAP), :].rearrange("(s p) d -> p s d", p=P)).then_inc(x_in, 16)

            sp.dma_start(b1[:, :, :], a["b1_T"].rearrange("p (e t) -> p e t", t=HT)).then_inc(b_in, 16)
            sp.dma_start(b2[:, :, :].rearrange("p e d -> p (e d)"), a["b2"].rearrange("e d -> (e d)").partition_broadcast(P)).then_inc(b_in, 16)
            load_w1(0)
            load_w2(0)
            sp.wait_ge(k.scattered, 16 * K_MOE * NT)
            load_x(0)
            with sp.Fori(0, E_MOE - 1) as e:
                sp.wait_ge(turned, NQ * e + NQ)
                load_x(e + 1)
                sp.wait_ge(w1_low, e + 1)
                load_w1(e + 1)
                sp.wait_ge(w2_low, e + 1)
                load_w2(e + 1)

        @block.tensor
        def _(pe):
            def transposes(e, q):
                h, g = q // (ST // G), q % (ST // G)
                if q == 0:
                    pe.wait_ge(x_in, 16 * e + 16)
                pe.wait_ge(x_low, NQ * e + q + 1)
                for s in range(G):
                    last = pe.transpose(ps[:, q % 2, s * P:(s + 1) * P], xe[:, g * G + s, h * P:(h + 1) * P], k.ident[:, :])
                last.then_inc(turned, 1)

            def body(e, more):
                pe.wait_ge(x_low, NQ * e + NQ + 2)
                pe.wait_ge(w1_low, e + 1)
                for m in range(NM):
                    c, t = m // HT, m % HT
                    pe.wait_ge(hid_high, NM * e + m + 1)
                    for n, (wp, xp) in enumerate(SPLIT):
                        for h in range(DH):
                            last = pe.matmul(ps[:, 2 + m % 4, :], w1[:, wp, h, t * P:(t + 1) * P], xeT[:, xp, h, c * CH:(c + 1) * CH],
                                             start=(n == 0 and h == 0), stop=(n == 2 and h == DH - 1))
                    last.then_inc(hidden, 1)
                pe.wait_ge(w2_low, e + 1)
                for u in range(NY):
                    if u in (0, NY // 2):
                        pe.wait_ge(hid_low, NM * e + (NM // 2 if u == 0 else NM) + 2)
                    pe.wait_ge(saved, NY * e + u + 1)
                    for s in (2 * u, 2 * u + 1):
                        for t in range(HT):
                            for n, (hp, wp) in enumerate(SPLIT):
                                last = pe.matmul(ps[:, 6 + u % 2, (s % 2) * D:(s % 2 + 1) * D], hT[:, hp, t, s * P:(s + 1) * P],
                                                 w2[:, wp, t, :], start=(t == 0 and n == 0), stop=(t == HT - 1 and n == 2))
                    last.then_inc(summed, 1)
                    if more:
                        transposes(e + 1, u)

            for q in range(NQ):
                transposes(0, q)
            all_experts(pe, body)

        @block.scalar
        def _(act):
            act.sem_inc(hid_high, 4)

            def split_w1(e):
                act.wait_ge(w1_in, 16 * e + 16)
                act.activation(w1[:, HIGH, :, :], w1_raw[:, :, :], ACT.Copy).then_inc(w1_high, 1)

            def split_x(e, q):
                h, g = q // (ST // G), q % (ST // G)
                act.wait_ge(turned, NQ * e + q + 1)
                act.activation(xeT[:, HIGH, h, g * CH:(g + 1) * CH], ps[:, q % 2, :], ACT.Copy).then_inc(x_high, 1)

            def body(e, more):
                act.wait_ge(b1_ready, e + 1)
                for m in range(NM):
                    c, t = m // HT, m % HT
                    act.wait_ge(hidden, NM * e + m + 1)
                    act.wait_ge(hid_low, NM * e + m + 1)
                    act.activation(hid[:, m % 2, :], ps[:, 2 + m % 4, :], ACT.Relu, bias=b1e[:, t:t + 1]).then_inc(relued, 1)
                    act.activation(hT[:, HIGH, t, c * CH:(c + 1) * CH], ps[:, 2 + m % 4, :], ACT.Relu, bias=b1e[:, t:t + 1]).then_inc(hid_high, 1)
                    if m == 1:
                        act.wait_ge(w2_in, 16 * e + 16)
                        act.activation(w2[:, HIGH, :, :], w2_raw[:, :, :], ACT.Copy).then_inc(w2_high, 1)
                if more:
                    split_w1(e + 1)
                    for q in range(NQ):
                        split_x(e + 1, q)

            split_w1(0)
            for q in range(NQ):
                split_x(0, q)
            all_experts(act, body)

        @block.vector
        def _(dve):
            dve.sem_inc(x_low, 2)
            dve.sem_inc(hid_low, 2)
            dve.sem_inc(saved, 2)
            dve.wait_ge(b_in, 32)

            def biases(e):
                dve.tensor_copy(b1e[:, :], b1[:, bass.ds(e, 1), :].rearrange("p o t -> p (o t)")).then_inc(b1_ready, 1)

            def split_x(e, q):
                h, g = q // (ST // G), q % (ST // G)
                dve.wait_ge(x_high, NQ * e + q + 1)
                dve.tensor_tensor(xeT[:, LOW, h, g * CH:(g + 1) * CH], ps[:, q % 2, :],
                                  xeT[:, HIGH, h, g * CH:(g + 1) * CH].bitcast(F32), ALU.subtract).then_inc(x_low, 1)

            def body(e, more):
                for m in range(NM):
                    c, t = m // HT, m % HT
                    dve.wait_ge(relued, NM * e + m + 1)
                    dve.wait_ge(hid_high, NM * e + m + 1 + 4)
                    dve.tensor_tensor(hT[:, LOW, t, c * CH:(c + 1) * CH], hid[:, m % 2, :],
                                      hT[:, HIGH, t, c * CH:(c + 1) * CH].bitcast(F32), ALU.subtract).then_inc(hid_low, 1)
                if more:
                    biases(e + 1)
                dve.wait_ge(y_free, e + 1)
                for u in range(NY):
                    dve.wait_ge(summed, NY * e + u + 1)
                    dve.tensor_tensor(ye[:, 2 * u:2 * u + 2, :], ps[:, 6 + u % 2, :].rearrange("p (s d) -> p s d", s=2),
                                      b2[:, bass.ds(e, 1), :].to_broadcast([P, 2, D]), ALU.add).then_inc(saved, 1)
                    if more:
                        split_x(e + 1, u)

            biases(0)
            for q in range(NQ):
                split_x(0, q)
            all_experts(dve, body)

        @block.gpsimd
        def _(pool):
            pool.sem_inc(y_free, 1)
            pool.wait_ge(k.inbox_zeroed, 16 * 8)
            for c in range(K_MOE):
                for n in range(NT):
                    pool.indirect_dma_start(out=a["inbox"], out_offset=bass.IndirectOffsetOnAxis(ap=k.put[:, c, n:n + 1], axis=0),
                                            in_=k.stream[:, n, :], in_offset=None,
                                            bounds_check=SLOTS - 1, oob_is_err=False).then_inc(k.scattered, 16)

            def split_w1(e):
                pool.wait_ge(w1_high, e + 1)
                pool.tensor_tensor(w1[:, LOW, :, :], w1_raw[:, :, :], w1[:, HIGH, :, :].bitcast(F32), ALU.subtract).then_inc(w1_low, 1)

            def body(e, more):
                pool.wait_ge(w2_high, e + 1)
                pool.tensor_tensor(w2[:, LOW, :, :], w2_raw[:, :, :], w2[:, HIGH, :, :].bitcast(F32), ALU.subtract).then_inc(w2_low, 1)
                if more:
                    split_w1(e + 1)
                pool.wait_ge(saved, NY * e + NY + 2)
                pool.dma_start(a["outbox"][bass.ds(e * CAP, CAP), :].rearrange("(s p) d -> p s d", p=P), ye[:, :, :]).then_inc(y_out, 16)
                pool.wait_ge(y_out, 16 * e + 16)
                pool.sem_inc(y_free, 1)

            split_w1(0)
            all_experts(pool, body)


def combine(nc, k, a):
    R = 4
    with ExitStack() as ctx:
        sb, sem = k.sbuf(ctx), k.stage_sem
        got = sb("got", [P, R, K_MOE, D])
        fetched = [sem(f"fetched{r}") for r in range(R)]
        first, added = sem("combine_first"), sem("combine_added")
        block = ctx.enter_context(nc.Block())

        @block.gpsimd
        def _(pool):
            pool.wait_ge(k.take_ready, 1)
            for n in range(NT):
                if n >= R:
                    pool.wait_ge(added, n - R + 1)
                for c in range(K_MOE):
                    pool.indirect_dma_start(out=got[:, n % R, c, :], out_offset=None, in_=a["outbox"],
                                            in_offset=bass.IndirectOffsetOnAxis(ap=k.take[:, c, n:n + 1], axis=0),
                                            bounds_check=SLOTS - 1, oob_is_err=True).then_inc(fetched[n % R], 16)

        @block.vector
        def _(dve):
            for n in range(NT):
                dve.wait_ge(fetched[n % R], 32 * (n // R + 1))
                dve.scalar_tensor_tensor(k.stream[:, n, :], got[:, n % R, 0, :], k.gate[:, 0, n:n + 1], k.stream[:, n, :],
                                         ALU.mult, ALU.add).then_inc(first, 1)
                dve.wait_ge(first, n + 1)
                dve.scalar_tensor_tensor(k.stream[:, n, :], got[:, n % R, 1, :], k.gate[:, 1, n:n + 1], k.stream[:, n, :],
                                         ALU.mult, ALU.add).then_inc(added, 1)


NH = 16
HD = D // NH
HE = HD // 2
LAT = 64
NCH = T // CH
QT = CH // P
NSPLIT = 3
PAIRS = [(0, 0), (0, 1), (0, 2), (1, 0), (1, 1), (2, 0)]
KROWS = len(PAIRS) * HD
MASKED = -1e30


def fold_weights(nc, k, a):
    with ExitStack() as ctx:
        sb, sem = k.sbuf(ctx), k.stage_sem
        down = sb("down_sb", [P, 3, NH // 2, D])
        up = sb("up_sb", [P, 3, 2, HD])
        zeroed, down_in, up_in, folded, copied, cleared = (sem("fold_" + n) for n in (
            "zeroed", "down_in", "up_in", "folded", "copied", "cleared"))
        block = ctx.enter_context(nc.Block())

        @block.sync
        def _(sp):
            for w, src in enumerate((a["wq_down_T"], a["wk_down_T"], a["wv_down_T"])):
                sp.dma_start(down[:, w, :, :], src.rearrange("(m p) c -> p m c", p=P)).then_inc(down_in, 16)
            sp.wait_ge(zeroed, 1)
            for g in range(2):
                rows = slice(g * LAT, (g + 1) * LAT)
                for w, (c, e) in enumerate(((a["wq_up_c"], a["wq_up_e"]), (a["wk_up_c"], a["wk_up_e"]))):
                    sp.dma_start(up[rows, w, g, 0:HE], c).then_inc(up_in, 16)
                    sp.dma_start(up[rows, w, g, HE:HD], e).then_inc(up_in, 16)
                sp.dma_start(up[rows, 2, g, :], a["wv_up"]).then_inc(up_in, 16)

        @block.tensor
        def _(pe):
            pe.wait_ge(down_in, 48)
            pe.wait_ge(up_in, 160)
            for w in range(3):
                for m in range(NH // 2):
                    for c in range(DH):
                        at = c * D + m * 2 * HD
                        last = pe.matmul(k.psum[:, w, at:at + 2 * HD], down[:, w, m, c * P:(c + 1) * P],
                                         up[:, w, :, :].rearrange("p g d -> p (g d)"), start=True, stop=True)
            last.then_inc(folded, 1)

        @block.vector
        def _(dve):
            dve.memset(up[:, :, :, :], 0.0).then_inc(zeroed, 1)
            dve.memset(k.wrot[:, :, :, :], 0.0).then_inc(cleared, 1)
            dve.wait_ge(folded, 1)
            for w in range(3):
                last = dve.tensor_copy(k.wfold[:, w, :, :], k.psum[:, w, :].rearrange("p (c n) -> p c n", c=DH))
            last.then_inc(copied, 1)
            dve.wait_ge(copied, 1)
            dve.wait_ge(cleared, 1)
            for w in range(2):
                for c in range(DH):
                    src = k.wfold[:, w, c, :].rearrange("p (h i j) -> p h i j", h=NH, j=2)[:, :, HE // 2:, :]
                    dst = k.wrot[:, w, c, :].rearrange("p (h i j) -> p h i j", h=NH, j=2)[:, :, HE // 2:, :]
                    dve.tensor_scalar(dst[:, :, :, 0], src[:, :, :, 1], -1.0, None, ALU.mult)
                    dve.tensor_copy(dst[:, :, :, 1], src[:, :, :, 0])


def transpose_stream(nc, k, name, dst):
    with ExitStack() as ctx:
        turned, copied = k.sem(name + "_turned"), k.sem(name + "_copied")
        ps = k.psum
        block = ctx.enter_context(nc.Block())

        @block.tensor
        def _(pe):
            for i in range(NPAIR):
                if i >= 8:
                    pe.wait_ge(copied, i - 7)
                for h in range(DH):
                    for j in range(2):
                        at = (h * 2 + j) * P
                        last = pe.transpose(ps[:, i % 8, at:at + P], k.stream[:, 2 * i + j, h * P:(h + 1) * P], k.ident[:, :])
                last.then_inc(turned, 1)

        @block.vector
        def _(dve):
            for i in range(NPAIR):
                dve.wait_ge(turned, i + 1)
                for h in range(DH):
                    last = dve.tensor_copy(dst[:, h, i * 2 * P:(i + 1) * 2 * P].rearrange("c (p j) -> c j p", j=2),
                                           ps[:, i % 8, h * 2 * P:(h + 1) * 2 * P].rearrange("c (j p) -> c j p", j=2))
                last.then_inc(copied, 1)


def project_qkv(nc, k, a, xT):
    NU = NCH * 2 * DH
    with ExitStack() as ctx:
        sb, sem = k.sbuf(ctx), k.stage_sem
        cos = sb("cos_sb", [P, 2, CH])
        sin = sb("sin_sb", [P, 2, CH])
        t1 = sb("rope_t1", [P, 2, CH])
        t2 = sb("rope_t2", [P, 2, CH])
        parts = sb("qk_split", [P, 2, NSPLIT, CH], BF16)
        t_in = [sem(f"rope_in{b}") for b in (0, 1)]
        projected, t1_ready, t2_ready, rotated, p1, r1, p2, p3, v_done, v_copied = (sem("qkv_" + n) for n in (
            "projected", "t1", "t2", "rotated", "p1", "r1", "p2", "p3", "v", "v_copied"))
        stored = [sem(f"qkv_stored{b}") for b in (0, 1)]
        ps = k.psum
        block = ctx.enter_context(nc.Block())

        def store(sp, u):
            c, w, r = u // 4, (u // 2) % 2, u % 2
            sp.wait_ge(p3, u + 1)
            sp.dma_start(a["qk_parts"][w, :, r * P:(r + 1) * P, c * CH:(c + 1) * CH].rearrange("s p t -> p s t"),
                         parts[:, u % 2, :, :]).then_inc(stored[u % 2], 16)

        def split(dve, u):
            b = u % 2
            dve.wait_ge(p1, u + 1)
            dve.tensor_tensor(t1[:, b, :], t1[:, b, :], parts[:, b, 0, :], ALU.subtract).then_inc(r1, 1)
            dve.wait_ge(p2, u + 1)
            dve.tensor_tensor(parts[:, b, 2, :], t1[:, b, :], parts[:, b, 1, :], ALU.subtract).then_inc(p3, 1)

        @block.sync
        def _(sp):
            u = 0
            for c in range(NCH):
                if c >= 2:
                    sp.wait_ge(t2_ready, 4 * (c - 1))
                for dst, src in ((cos, a["cos_T"]), (sin, a["sin_T"])):
                    for g in range(P // HD):
                        sp.dma_start(dst[g * HD:(g + 1) * HD, c % 2, :], src[:, c * CH:(c + 1) * CH]).then_inc(t_in[c % 2], 16)
                if c >= 1:
                    for _ in range(4):
                        store(sp, u)
                        u += 1
            for _ in range(4):
                store(sp, u)
                u += 1
            for b in (0, 1):
                sp.wait_ge(stored[b], 16 * NU // 2)

        @block.tensor
        def _(pe):
            for c in range(NCH):
                cols = slice(c * CH, (c + 1) * CH)
                for w in range(2):
                    for r in range(DH):
                        u = (c * 2 + w) * DH + r
                        if u >= 2:
                            pe.wait_ge(t2_ready, u - 1)
                        for half, weights in enumerate((k.wfold, k.wrot)):
                            for h in range(DH):
                                last = pe.matmul(ps[:, 2 * (u % 2) + half, :], weights[:, w, h, r * P:(r + 1) * P], xT[:, h, cols],
                                                 start=(h == 0), stop=(h == DH - 1))
                        last.then_inc(projected, 1)
                for s in range(QT):
                    n = c * QT + s
                    if n >= 4:
                        pe.wait_ge(v_copied, n - 3)
                    for h in range(DH):
                        last = pe.matmul(ps[:, 4 + n % 4, 0:D], xT[:, h, n * P:(n + 1) * P], k.wfold[:, 2, h, :],
                                         start=(h == 0), stop=(h == DH - 1))
                    last.then_inc(v_done, 1)

        @block.vector
        def _(dve):
            for u in range(NU):
                c, b = u // 4, u % 2
                if u % 4 == 0:
                    dve.wait_ge(t_in[c % 2], 16 * 2 * (P // HD) * (c // 2 + 1))
                dve.wait_ge(projected, u + 1)
                if u >= 2:
                    dve.wait_ge(p3, u - 1)
                dve.tensor_tensor(t1[:, b, :], ps[:, 2 * b, :], cos[:, c % 2, :], ALU.mult).then_inc(t1_ready, 1)
                dve.tensor_tensor(t2[:, b, :], ps[:, 2 * b + 1, :], sin[:, c % 2, :], ALU.mult).then_inc(t2_ready, 1)
                dve.wait_ge(t1_ready, u + 1)
                dve.wait_ge(t2_ready, u + 1)
                dve.tensor_tensor(t1[:, b, :], t1[:, b, :], t2[:, b, :], ALU.add).then_inc(rotated, 1)
                if u > 0:
                    split(dve, u - 1)
            split(dve, NU - 1)

        @block.scalar
        def _(act):
            for u in range(NU):
                b = u % 2
                act.wait_ge(rotated, u + 1)
                if u >= 2:
                    act.wait_ge(stored[b], 16 * (u // 2))
                act.activation(parts[:, b, 0, :], t1[:, b, :], ACT.Copy).then_inc(p1, 1)
                act.wait_ge(r1, u + 1)
                act.activation(parts[:, b, 1, :], t1[:, b, :], ACT.Copy).then_inc(p2, 1)
                if u % 4 == 3:
                    for n in range(u - 3, u + 1):
                        act.wait_ge(v_done, n + 1)
                        act.activation(k.v[:, n, :], ps[:, 4 + n % 4, 0:D], ACT.Copy).then_inc(v_copied, 1)


BUFS = 3
RING_P = 8


def attention_groups():
    units = [(qc, kt) for qc in range(NCH) for kt in range(QT * (qc + 1))]
    rows = [(i, m) for i in range(NT) for m in range(i // QT + 1)]
    groups = [(i, g) for i in range(NT) for g in range(i // QT // 2 + 1)]
    closes = {rows.index((i, min(2 * g + 1, i // QT))): n for n, (i, g) in enumerate(groups)}
    return units, rows, groups, closes


def attention_plan(this_head, next_head):
    units, rows, groups, closes = attention_groups()
    SEEN, SOON = 190, 200
    AV_COST, FOLD_COST, TURN_COST = 930, 240, 60
    cost_pe = lambda columns, diag: 0.42 * columns + (56 if diag else 0)
    pe = dve = act = 0
    st = av = s = 0
    exped, used, maxed, copied, normed = {}, {}, {}, {}, {}
    reached = {}
    to_fold, folds, turned = [], 0, False
    waiting = []
    order_pe, order_dve = [], []
    log = {"MAX": maxed, "OCOPY": copied, "NORM": normed}

    def give(ready, kind, x, cost):
        waiting.append((ready, len(order_pe) + len(waiting), (kind, x), cost))

    while True:
        while waiting:
            waiting.sort()
            ready, _, (kind, x), cost = waiting[0]
            if max(ready, dve) >= pe:
                break
            waiting.pop(0)
            dve = max(ready, dve) + cost
            order_dve.append((kind, x))
            log.get(kind, reached)[x if kind in log else kind] = dve
        can = []
        left_dve = dve + sum(w[3] for w in waiting)
        if this_head:
            if st < len(units) and 4 * av > st - RING_P:
                can.append((max(pe, exped[st - 2] + SEEN if st >= 2 else 0), act - 400, "ST", st))
            if 4 * av + 3 < st:
                qc, kt = units[4 * av]
                if kt > 0 or qc == 0 or qc - 1 in copied:
                    can.append((max(pe, exped[4 * av + 3] + SEEN, copied[qc - 1] + SEEN if kt == 0 and qc else 0),
                                pe + 2500 - 150 * (st - 4 * av), "AV", av))
            if to_fold and to_fold[0] in copied and (to_fold[0] == 0 or to_fold[0] - 1 in normed) and turned == ("MCOPY" in reached):
                can.append((max(pe, copied[to_fold[0]] + SEEN), pe + 1000, "FOLD", to_fold[0]))
        if next_head:
            done = len([1 for c in closes if c < s])
            if s < len(rows) and (done < 2 or done - 2 in maxed):
                can.append((max(pe, maxed[done - 2] + SEEN if done >= 2 else 0), left_dve - 200, "S", s))
            if "MFIN" in reached and not turned and folds == len(normed):
                can.append((max(pe, reached["MFIN"] + SEEN), 0, "MTURN", 0))
        if not can and not waiting:
            return order_pe, order_dve
        if not can:
            pe = max(pe, waiting[0][0], dve) + 1
            continue
        soonest = min(c[0] for c in can)
        start, _, kind, x = min((c for c in can if c[0] <= soonest + SOON), key=lambda c: c[1])
        if kind == "ST":
            qc, kt = units[x]
            columns = CH - max(0, kt - QT * qc) * P
            pe = start + cost_pe(columns, kt >= QT * qc)
            act = max(act, pe + SEEN, used.get(x - RING_P, 0) + SEEN) + 51 + columns / 1.2
            exped[x] = act
            st += 1
        elif kind == "AV":
            pe = start + AV_COST
            used.update({u: pe for u in range(4 * x, 4 * x + 4)})
            av += 1
            qc, kt = units[4 * x + 3]
            if kt == QT * qc + QT - 1:
                to_fold.append(qc)
                give(pe + SEEN, "OCOPY", qc, 595)
        elif kind == "FOLD":
            pe = start + FOLD_COST
            to_fold.pop(0)
            folds += 1
            give(pe + SEEN, "NORM", x, 700)
        elif kind == "S":
            pe = start
            while True:
                i, m = rows[s]
                pe += cost_pe(min(CH, (i + 1) * P - m * CH), m == i // QT)
                order_pe.append((kind, s))
                s += 1
                if s - 1 in closes:
                    break
            g = closes[s - 1]
            give(pe + SEEN, "MAX", g, (60 + min(2 * CH, (i + 1) * P - groups[g][1] * 2 * CH)) / 0.96)
            if s == len(rows):
                give(pe + SEEN, "MFIN", 0, 1300)
        else:
            turned = True
            pe = start + TURN_COST
            give(pe + SEEN, "MCOPY", 0, 200)
        if kind != "S":
            order_pe.append((kind, x))


def attention(nc, k, a):
    units, rows, groups, closes = attention_groups()
    NU, NG = len(units), len(groups)
    lead_pe, lead_dve = attention_plan(False, True)
    body_plan = attention_plan(True, True)
    last_plan = attention_plan(True, False)
    NEXT = ("S", "MAX", "MFIN", "MTURN", "MCOPY")
    with ExitStack() as ctx:
        sb, sem = k.sbuf(ctx), k.stage_sem
        q6 = sb("q_rows", [P, BUFS, T], BF16)
        k6 = sb("k_rows", [P, BUFS, T], BF16)
        vh = sb("v_head", [P, BUFS, NT, 32])
        pt = sb("probs_T", [P, RING_P, CH])
        oacc = sb("o_acc", [P, 2, CH])
        mx = sb("row_max", [P, BUFS, NT, 4])
        m = sb("max_f", [P, 2, NT])
        nm = sb("neg_max", [P, NSPLIT, NT], BF16)
        mT = sb("neg_max_T", [NSPLIT * NT, P], BF16)
        rcp = sb("inv_sum", [P, 2, QT])
        identb = sb("ident_bf", [P, P], BF16)
        mask = sb("mask_q_k", [P, P], BF16)
        maskT = sb("mask_k_q", [P, P], BF16)
        fold = sb("fold", [P, 32])
        consts, s_done, st_done, exped, av_done, maxed, o_copied, folded, normed, v_ready = (sem("at_" + n) for n in (
            "consts", "s_done", "st_done", "exped", "av_done", "maxed", "o_copied", "folded", "normed", "v_ready"))
        m_step, m_split, m_turned, m_copied, inv_ready, cleared, masks = (sem("at_" + n) for n in (
            "m_step", "m_split", "m_turned", "m_copied", "inv_ready", "pt_cleared", "masks"))
        ones_ready, m_out = sem("at_ones"), sem("at_m_out")
        qk_in = [sem(f"at_qk_in{b}") for b in range(BUFS)]
        m_in = [sem(f"at_m_in{b}") for b in range(BUFS)]
        ps = k.psum
        psb = k.psum[:, 7, 256:512].bitcast(BF16)
        block = ctx.enter_context(nc.Block())

        def heads(eng, body):
            with eng.Fori(0, NH // BUFS) as i:
                for b in range(BUFS):
                    body(BUFS * i + b, b, i, body_plan)
            body(NH - 1, 0, NH // BUFS, last_plan)

        @block.sync
        def _(sp):
            def load(e, b):
                for (dst, w, side) in ((q6, 0, 0), (k6, 1, 1)):
                    for r, pair in enumerate(PAIRS):
                        sp.dma_start(dst[r * HD:(r + 1) * HD, b, :],
                                     a["qk_parts"][w, pair[side], bass.ds(e * HD, HD), :]).then_inc(qk_in[b], 16)

            def maxima(e, b):
                sp.wait_ge(m_copied, e + 1)
                sp.dma_start(a["max_rows"][b, :, :], mT[:, :]).then_inc(m_out, 16)
                sp.wait_ge(m_out, 16 * e + 16)
                sp.dma_start(q6[KROWS:KROWS + NSPLIT, b, :],
                             a["max_rows"][b, :, :].rearrange("(s i) p -> s (i p)", s=NSPLIT)).then_inc(m_in[b], 16)

            load(0, 0)
            load(1, 1)
            maxima(0, 0)

            def head(e, b, more=True):
                if more:
                    sp.wait_ge(st_done, NU * e + 1)
                    load(e + 2, (b + 2) % BUFS)
                maxima(e + 1, (b + 1) % BUFS)

            with sp.Fori(0, NH // BUFS - 1) as i:
                for b in range(BUFS):
                    head(BUFS * i + b, b)
            for e in range(NH - 1 - BUFS, NH - 1):
                head(e, e % BUFS, more=e + 2 < NH)

        @block.gpsimd
        def _(pool):
            pool.memset(identb[:, :], 0.0).then_inc(consts, 1)
            pool.memset(mask[:, :], 0.0).then_inc(consts, 1)
            pool.memset(maskT[:, :], 0.0).then_inc(consts, 1)
            pool.memset(fold[:, :], 0.0).then_inc(consts, 1)
            pool.memset(vh[:, :, :, HD + 1:], 0.0).then_inc(ones_ready, 1)
            pool.memset(vh[:, :, :, HD:HD + 1], 1.0).then_inc(ones_ready, 1)
            pool.wait_ge(consts, 4)
            pool.affine_select(out=identb[:, :], in_=identb[:, :], compare_op=ALU.not_equal, fill=1.0,
                               base=0, pattern=[[-1, P]], channel_multiplier=1).then_inc(masks, 1)
            pool.affine_select(out=mask[:, :], in_=mask[:, :], compare_op=ALU.is_ge, fill=MASKED,
                               base=0, pattern=[[-1, P]], channel_multiplier=1).then_inc(masks, 1)
            pool.affine_select(out=maskT[:, :], in_=maskT[:, :], compare_op=ALU.is_ge, fill=MASKED,
                               base=0, pattern=[[1, P]], channel_multiplier=-1).then_inc(masks, 1)
            for g in range(4):
                pool.wait_ge(masks, 3 + g)
                pool.affine_select(out=fold[:, :], in_=fold[:, :], compare_op=ALU.not_equal, fill=1.0,
                                   base=-32 * g, pattern=[[-1, 32]], channel_multiplier=1).then_inc(masks, 1)

        @block.tensor
        def _(pe):
            pe.sem_inc(st_done, 1)
            pe.sem_inc(av_done, RING_P)
            pe.wait_ge(masks, 7)
            pe.wait_ge(ones_ready, 3)

            def s_unit(e, b, s):
                i, mm = rows[s]
                if s == 0 or (s - 1) in closes:
                    g = closes[min(c for c in closes if c >= s)]
                    pe.wait_ge(maxed, NG * e + g + 1)
                g = closes[min(c for c in closes if c >= s)]
                width = min(CH, (i + 1) * P - mm * CH)
                diag = mm == i // QT
                bank = 2 * (g % 2) + mm % 2
                ins = pe.matmul(ps[:, bank, 0:width], q6[0:KROWS, b, i * P:(i + 1) * P], k6[0:KROWS, b, mm * CH:mm * CH + width],
                                start=True, stop=not diag)
                if diag:
                    ins = pe.matmul(ps[:, bank, width - P:width], identb[:, :], mask[:, :], start=False, stop=True)
                if s in closes:
                    ins.then_inc(s_done, 1)

            def next_head(kind, x, e, b, loads, folds=0):
                if kind == "S":
                    if x == 0:
                        pe.wait_ge(qk_in[b], 16 * 2 * len(PAIRS) * loads)
                    s_unit(e, b, x)
                elif kind == "MTURN":
                    pe.wait_ge(m_split, e + 1)
                    if folds:
                        pe.wait_ge(normed, NCH * (e - 1) + folds + 1)
                    pe.transpose(psb[0:NSPLIT * NT, 0:P], nm[:, :, :].rearrange("p s i -> p (s i)"), identb[:, :]).then_inc(m_turned, 1)

            for kind, x in lead_pe:
                next_head(kind, x, 0, 0, 1)

            def body(e, b, i, plan):
                pe.wait_ge(m_in[b], 16 * i + 16)
                folds, turned = 0, False
                for kind, x in plan[0]:
                    if kind in NEXT:
                        next_head(kind, x, e + 1, (b + 1) % BUFS, i + 1 + (b + 1) // BUFS, folds)
                        turned = turned or kind == "MTURN"
                    elif kind == "ST":
                        qc, kt = units[x]
                        o = max(0, kt - QT * qc) * P
                        diag = kt >= QT * qc
                        pe.wait_ge(exped, NU * e + x + 1)
                        bank = 4 + x % 2
                        ins = pe.matmul(ps[:, bank, o:CH], k6[0:KROWS + NSPLIT, b, kt * P:(kt + 1) * P],
                                        q6[0:KROWS + NSPLIT, b, qc * CH + o:(qc + 1) * CH], start=True, stop=not diag)
                        if diag:
                            ins = pe.matmul(ps[:, bank, o:o + P], identb[:, :], maskT[:, :], start=False, stop=True)
                        ins.then_inc(st_done, 1)
                    elif kind == "AV":
                        qc = units[4 * x][0]
                        if units[4 * x][1] == 0:
                            pe.wait_ge(o_copied, NCH * e + qc + 1)
                        if x == 0:
                            pe.wait_ge(v_ready, e + 1)
                            pe.wait_ge(cleared, (QT - 1) * (e + 1))
                        pe.wait_ge(exped, NU * e + 4 * x + 4 + 2)
                        for u in range(4 * x, 4 * x + 4):
                            kt = units[u][1]
                            g = kt % 4
                            o = max(0, kt - QT * qc) * P if qc else 0
                            pe.matmul(ps[32 * g:32 * g + 32, 6, o:CH], vh[:, b, kt, :], pt[:, u % RING_P, o:CH],
                                      start=(kt < 4), stop=(kt >= QT * qc)).then_inc(av_done, 1)
                    elif kind == "FOLD":
                        pe.wait_ge(normed, NCH * e + x + 1)
                        pe.wait_ge(o_copied, NCH * e + x + 1 + 1)
                        if turned:
                            pe.wait_ge(m_copied, e + 2)
                        folds += 1
                        for t in range(QT):
                            src = oacc[:, x % 2, (t // 2) * 2 * P:(t // 2 + 1) * 2 * P].rearrange("r (p j) -> r p j", j=2)[:, :, t % 2]
                            ins = pe.matmul(ps[:, 7, t * 32:t * 32 + 32], src, fold[:, :], start=True, stop=True)
                        ins.then_inc(folded, 1)

            heads(pe, body)

        @block.scalar
        def _(act):
            act.sem_inc(exped, 2)

            def body(e, b, i, plan):
                for kind, x in plan[0]:
                    if kind == "ST":
                        qc, kt = units[x]
                        o = max(0, kt - QT * qc) * P
                        act.wait_ge(st_done, NU * e + x + 1 + 1)
                        act.wait_ge(av_done, NU * e + x + 1)
                        act.activation(pt[:, x % RING_P, o:CH], ps[:, 4 + x % 2, o:CH], ACT.Exp, scale=HD ** -0.5).then_inc(exped, 1)

            heads(act, body)

        @block.vector
        def _(dve):
            dve.sem_inc(maxed, 2)
            dve.sem_inc(o_copied, 1)
            dve.sem_inc(normed, 1)
            dve.memset(k6[KROWS:KROWS + NSPLIT, :, :], 1.0).then_inc(ones_ready, 1)
            dve.memset(mx[:, :, :, :], 2 * MASKED).then_inc(m_step, 1)
            dve.wait_ge(m_step, 1)

            def take_v(e, b):
                dve.tensor_scalar(vh[:, b, :, 0:HD], k.v[:, :, bass.ds(e * HD, HD)], 1.0, None, ALU.mult).then_inc(v_ready, 1)

            def next_head(kind, x, e, b):
                if kind == "MAX":
                    i, g = groups[x]
                    width = min(2 * CH, (i + 1) * P - g * 2 * CH)
                    dve.wait_ge(s_done, NG * e + x + 1)
                    src = ps[:, 2 * (x % 2):2 * (x % 2) + 2, :].rearrange("p b c -> p (b c)")[:, 0:width]
                    dve.tensor_reduce(mx[:, b, i, g:g + 1], src, AX.X, ALU.max).then_inc(maxed, 1)
                elif kind == "MFIN":
                    base = 5 * e + 1
                    dve.wait_ge(maxed, NG * e + NG + 2)
                    dve.tensor_reduce(m[:, 0, :], mx[:, b, :, :], AX.X, ALU.max).then_inc(m_step, 1)
                    dve.wait_ge(m_step, base + 1)
                    dve.tensor_scalar(nm[:, 0, :], m[:, 0, :], -1.0, None, ALU.mult).then_inc(m_step, 1)
                    dve.wait_ge(m_step, base + 2)
                    dve.scalar_tensor_tensor(m[:, 1, :], m[:, 0, :], -1.0, nm[:, 0, :], ALU.mult, ALU.subtract).then_inc(m_step, 1)
                    dve.wait_ge(m_step, base + 3)
                    dve.tensor_copy(nm[:, 1, :], m[:, 1, :]).then_inc(m_step, 1)
                    dve.wait_ge(m_step, base + 4)
                    dve.tensor_tensor(nm[:, 2, :], m[:, 1, :], nm[:, 1, :], ALU.subtract).then_inc(m_step, 1)
                    dve.wait_ge(m_step, base + 5)
                    dve.sem_inc(m_split, 1)
                elif kind == "MCOPY":
                    dve.wait_ge(m_turned, e + 1)
                    dve.tensor_copy(mT[:, :], psb[0:NSPLIT * NT, 0:P]).then_inc(m_copied, 1)

            dve.wait_ge(ones_ready, 3)
            take_v(0, 0)
            for kind, x in lead_dve:
                next_head(kind, x, 0, 0)

            def body(e, b, i, plan):
                dve.wait_ge(av_done, NU * e + RING_P)
                for u in range(1, QT):
                    dve.memset(pt[:, u % RING_P, 0:u * P], 0.0).then_inc(cleared, 1)
                if plan is not last_plan:
                    take_v(e + 1, (b + 1) % BUFS)
                for kind, x in plan[1]:
                    if kind in NEXT:
                        next_head(kind, x, e + 1, (b + 1) % BUFS)
                    elif kind == "OCOPY":
                        dve.wait_ge(av_done, NU * e + 4 * sum(1 for q in range(0, x + 1) for _ in range(q + 1)) + RING_P)
                        dve.tensor_copy(oacc[:, x % 2, :], ps[:, 6, :]).then_inc(o_copied, 1)
                    elif kind == "NORM":
                        dve.wait_ge(folded, NCH * e + x + 1)
                        dve.reciprocal(rcp[:, x % 2, :], ps[:, 7, 0:QT * 32].rearrange("p (t d) -> p t d", d=32)[:, :, HD]).then_inc(inv_ready, 1)
                        dve.wait_ge(inv_ready, NCH * e + x + 1)
                        dve.tensor_tensor(k.attn[:, QT * x:QT * x + QT, bass.ds(e * HD, HD)],
                                          ps[:, 7, 0:QT * 32].rearrange("p (t d) -> p t d", d=32)[:, :, 0:HD],
                                          rcp[:, x % 2, :].unsqueeze(2).to_broadcast([P, QT, HD]), ALU.mult).then_inc(normed, 1)

            heads(dve, body)


def project_attention(nc, k, a):
    with ExitStack() as ctx:
        sb, sem = k.sbuf(ctx), k.stage_sem
        wc = sb("wc_sb", [P, DH, D])
        aT = sb("attn_T", [P, 2, D])
        loaded, turned, copied, projected, added = (sem("pa_" + n) for n in ("loaded", "turned", "copied", "projected", "added"))
        ps = k.psum
        block = ctx.enter_context(nc.Block())

        @block.sync
        def _(sp):
            sp.dma_start(wc[:, :, :], a["wc"].rearrange("(h p) e -> p h e", p=P)).then_inc(loaded, 16)

        @block.tensor
        def _(pe):
            pe.wait_ge(loaded, 16)
            for n in range(NT + 1):
                if n < NT:
                    if n >= 2:
                        pe.wait_ge(copied, n - 1)
                    for h in range(DH):
                        last = pe.transpose(ps[:, n % 2, h * P:(h + 1) * P], k.attn[:, n, h * P:(h + 1) * P], k.ident[:, :])
                    last.then_inc(turned, 1)
                if n > 0:
                    m = n - 1
                    pe.wait_ge(copied, m + 1)
                    if m >= 4:
                        pe.wait_ge(added, m - 3)
                    for h in range(DH):
                        last = pe.matmul(ps[:, 4 + m % 4, 0:D], aT[:, m % 2, h * P:(h + 1) * P], wc[:, h, :],
                                         start=(h == 0), stop=(h == DH - 1))
                    last.then_inc(projected, 1)

        @block.scalar
        def _(act):
            for n in range(NT):
                act.wait_ge(turned, n + 1)
                if n >= 2:
                    act.wait_ge(projected, n - 1)
                act.activation(aT[:, n % 2, :], ps[:, n % 2, 0:D], ACT.Copy).then_inc(copied, 1)

        @block.vector
        def _(dve):
            for n in range(NT):
                dve.wait_ge(projected, n + 1)
                dve.tensor_tensor(k.stream[:, n, :], k.stream[:, n, :], ps[:, 4 + n % 4, 0:D], ALU.add).then_inc(added, 1)


NE = 16
NEX = NE + 1
TOPK = 4
INTER = 128
ROUTE_SCALE = 2.5


def transpose_tiles(nc, k, name, dst):
    with ExitStack() as ctx:
        turned, high, low = k.sem(name + "_turned"), k.sem(name + "_high"), k.sem(name + "_low")
        ps = k.psum
        block = ctx.enter_context(nc.Block())

        @block.tensor
        def _(pe):
            for i in range(NPAIR):
                if i >= 8:
                    pe.wait_ge(low, i - 7)
                for h in range(DH):
                    for j in range(2):
                        at = (h * 2 + j) * P
                        last = pe.transpose(ps[:, i % 8, at:at + P], k.stream[:, 2 * i + j, h * P:(h + 1) * P], k.ident[:, :])
                last.then_inc(turned, 1)

        @block.scalar
        def _(act):
            for i in range(NPAIR):
                act.wait_ge(turned, i + 1)
                act.activation(dst[:, HIGH, :, i * 2 * P:(i + 1) * 2 * P],
                               ps[:, i % 8, :].rearrange("c (h t) -> c h t", h=DH), ACT.Copy).then_inc(high, 1)

        @block.vector
        def _(dve):
            for i in range(NPAIR):
                dve.wait_ge(high, i + 1)
                cols = slice(i * 2 * P, (i + 1) * 2 * P)
                dve.tensor_tensor(dst[:, LOW, :, cols], ps[:, i % 8, :].rearrange("c (h t) -> c h t", h=DH),
                                  dst[:, HIGH, :, cols].bitcast(F32), ALU.subtract).then_inc(low, 1)


def weigh_experts(nc, k, a, xT):
    with ExitStack() as ctx:
        sb, sem = k.sbuf(ctx), k.stage_sem
        wg = sb("gate_w_sb", [P, DH, NE])
        wg_part = sb("gate_w_part", [P, 2, DH, NE], F32R)
        logits_T = sb("logits_T", [NE, T])
        w_split, l_chunk, l_copied = sem("we_w_split"), sem("we_chunk"), sem("we_copied")
        gb = sb("gate_b_sb", [P, NE])
        scores = sb("scores", [P, NT, NE])
        biased = sb("biased", [P, NT, NE])
        top = sb("top_b", [P, NT, 8])
        top_i = sb("top_bi", [P, NT, 8], U32)
        choice = sb("choice_b", [P, NT, TOPK])
        hit = sb("hit", [P, NT, NE])
        mask = sb("mask_b", [P, NT, NE])
        total = sb("total_b", [P, NT])
        loaded, logits, scored, step = (sem("we_" + n) for n in ("loaded", "logits", "scored", "step"))
        ps = k.psum
        block = ctx.enter_context(nc.Block())

        @block.sync
        def _(sp):
            sp.dma_start(wg[:, :, :], a["gate_w_T"].rearrange("(h p) e -> p h e", p=P)).then_inc(loaded, 16)
            sp.dma_start(gb[:, :], a["gate_b"].partition_broadcast(P)).then_inc(loaded, 16)

        @block.tensor
        def _(pe):
            pe.wait_ge(w_split, 2)
            for c in range(NCH):
                if c >= 4:
                    pe.wait_ge(l_copied, c - 3)
                for n, (wp, xp) in enumerate(SPLIT):
                    for h in range(DH):
                        last = pe.matmul(ps[0:NE, c % 4, :], wg_part[:, wp, h, :], xT[:, xp, h, c * CH:(c + 1) * CH],
                                         start=(n == 0 and h == 0), stop=(n == 2 and h == DH - 1))
                last.then_inc(l_chunk, 1)
            for n in range(NT):
                pe.wait_ge(l_copied, n // QT + 1)
                last = pe.transpose(ps[:, 4, n * NE:(n + 1) * NE], logits_T[:, n * P:(n + 1) * P], k.ident[0:NE, 0:NE])
            last.then_inc(logits, 1)

        @block.scalar
        def _(act):
            act.wait_ge(loaded, 32)
            act.activation(wg_part[:, HIGH, :, :], wg[:, :, :], ACT.Copy).then_inc(w_split, 1)
            for c in range(NCH):
                act.wait_ge(l_chunk, c + 1)
                act.activation(logits_T[:, c * CH:(c + 1) * CH], ps[0:NE, c % 4, :], ACT.Copy).then_inc(l_copied, 1)
            act.wait_ge(logits, 1)
            act.activation(scores[:, :, :], ps[:, 4, :].rearrange("p (n e) -> p n e", e=NE), ACT.Sigmoid).then_inc(scored, 1)

        @block.vector
        def _(dve):
            s = Steps(step)
            dve.memset(k.comb[:, NE, :], 1.0)
            dve.wait_ge(w_split, 1)
            dve.tensor_tensor(wg_part[:, LOW, :, :], wg[:, :, :], wg_part[:, HIGH, :, :].bitcast(F32), ALU.subtract).then_inc(w_split, 1)
            dve.wait_ge(scored, 1)
            s.link(dve, dve.tensor_tensor(biased[:, :, :], scores[:, :, :], gb[:, :].unsqueeze(1).to_broadcast([P, NT, NE]), ALU.add))
            for n in range(NT):
                last = dve.max(top[:, n, :], biased[:, n, :])
            s.link(dve, last)
            for n in range(NT):
                last = dve.max_index(top_i[:, n, :], top[:, n, :], biased[:, n, :])
            s.link(dve, last)
            s.link(dve, dve.tensor_copy(choice[:, :, :], top_i[:, :, 0:TOPK]))
            for c in range(TOPK):
                dst = mask if c == 0 else hit
                s.link(dve, dve.tensor_tensor(dst[:, :, :], k.iota[:, 0:NE].unsqueeze(1).to_broadcast([P, NT, NE]),
                                              choice[:, :, c].unsqueeze(2).to_broadcast([P, NT, NE]), ALU.is_equal))
                if c:
                    s.link(dve, dve.tensor_tensor(mask[:, :, :], mask[:, :, :], hit[:, :, :], ALU.add))
            s.link(dve, dve.tensor_tensor(scores[:, :, :], scores[:, :, :], mask[:, :, :], ALU.mult))
            s.link(dve, dve.tensor_reduce(total[:, :], scores[:, :, :], AX.X, ALU.add))
            s.link(dve, dve.reciprocal(total[:, :], total[:, :]))
            s.link(dve, dve.tensor_scalar(total[:, :], total[:, :], ROUTE_SCALE, None, ALU.mult))
            dve.tensor_tensor(k.comb[:, 0:NE, :].rearrange("p e n -> p n e"), scores[:, :, :],
                              total[:, :].unsqueeze(2).to_broadcast([P, NT, NE]), ALU.mult)


def swiglu_experts(nc, k, a, xT):
    WCOLS = DH * 2 * INTER
    with ExitStack() as ctx:
        sb, sem = k.sbuf(ctx), k.stage_sem
        w_raw = sb("w_raw", [P, WCOLS + D])
        w_part = sb("w_part", [P, 2, 2, WCOLS + D], F32R)
        sig = sb("sig", [P, 2, CH])
        act_g = sb("act_gate", [P, 2, CH])
        hid = sb("hidden_f32", [P, 2, CH])
        hT = sb("hidden_T", [P, 2, 2, CH], F32R)
        w_in, w_high, w_low, w_used = (sem("sw_" + n) for n in ("w_in", "w_high", "w_low", "w_used"))
        up_done, sig_done, t_done, full, high, low, down_done, added = (sem("sw_" + n) for n in (
            "up", "sig", "t", "full", "high", "low", "down", "added"))
        ps = k.psum
        block = ctx.enter_context(nc.Block())

        def units(eng, first, step):
            first()
            with eng.Fori(0, NE // 2) as i:
                for b in (0, 1):
                    for c in range(NCH):
                        step(2 * i + b, b, c, False)
            for c in range(NCH):
                step(NE, 0, c, c == NCH - 1, final=True)

        def after(e, b, c):
            if c < NCH - 1:
                return e, b, c + 1
            return e + 1, 1 - b, 0

        @block.sync
        def _(sp):
            def load(e):
                sp.wait_ge(w_low, e + 1)
                sp.dma_start(w_raw[:, 0:WCOLS].rearrange("p (h f) -> p h f", h=DH),
                             a["w13_T"][bass.ds(e * D, D), :].rearrange("(h p) f -> p h f", p=P)).then_inc(w_in, 16)
                sp.dma_start(w_raw[:, WCOLS:], a["w2_T"][bass.ds(e * INTER, INTER), :]).then_inc(w_in, 16)
            with sp.Fori(0, NEX) as e:
                load(e)

        @block.tensor
        def _(pe):
            pe.sem_inc(down_done, 2)

            def up(e, b, c):
                u = NCH * e + c
                if c == 0:
                    pe.wait_ge(w_low, e + 2)
                pe.wait_ge(full, u + 1)
                for half in range(2):
                    for n, (wp, xp) in enumerate(SPLIT):
                        for h in range(DH):
                            at = h * 2 * INTER + half * INTER
                            last = pe.matmul(ps[:, 2 * half + c % 2, :], w_part[:, b, wp, at:at + INTER],
                                             xT[:, xp, h, c * CH:(c + 1) * CH], start=(n == 0 and h == 0), stop=(n == 2 and h == DH - 1))
                last.then_inc(up_done, 1)

            def step(e, b, c, is_last, final=False):
                if not is_last:
                    up(*after(e, b, c))
                u = NCH * e + c
                pe.wait_ge(low, u + 1 + 2)
                pe.wait_ge(added, u + 1)
                for s in range(QT):
                    for n, (hp, wp) in enumerate(SPLIT):
                        last = pe.matmul(ps[:, 4 + 2 * (c % 2) + s // 2, (s % 2) * D:(s % 2 + 1) * D], hT[:, c % 2, hp, s * P:(s + 1) * P],
                                         w_part[:, b, wp, WCOLS:], start=(n == 0), stop=(n == 2))
                last.then_inc(down_done, 1)

            units(pe, lambda: up(0, 0, 0), step)

        @block.scalar
        def _(act):
            def weights(e, b):
                act.wait_ge(w_in, 32 * (e + 1))
                act.wait_ge(down_done, NCH * e - NCH + 2)
                act.activation(w_part[:, b, HIGH, :], w_raw[:, :], ACT.Copy).then_inc(w_high, 1)

            def sigmoid(e, b, c):
                u = NCH * e + c
                act.wait_ge(up_done, u + 1)
                act.wait_ge(full, u + 1)
                act.activation(sig[:, c % 2, :], ps[:, c % 2, :], ACT.Sigmoid).then_inc(sig_done, 1)

            def hidden_high(e, b, c):
                u = NCH * e + c
                act.wait_ge(full, u + 1 + 2)
                act.wait_ge(down_done, u + 1)
                act.activation(hT[:, c % 2, HIGH, :], hid[:, c % 2, :], ACT.Copy).then_inc(high, 1)

            def first():
                act.wait_ge(w_in, 32)
                act.activation(w_part[:, 0, HIGH, :], w_raw[:, :], ACT.Copy).then_inc(w_high, 1)
                sigmoid(0, 0, 0)

            def step(e, b, c, is_last, final=False):
                hidden_high(e, b, c)
                if not is_last:
                    sigmoid(*after(e, b, c))
                if c == 1 and not final:
                    weights(e + 1, 1 - b)

            units(act, first, step)

        @block.gpsimd
        def _(pool):
            def weights(e, b):
                pool.wait_ge(w_high, e + 1)
                pool.tensor_tensor(w_part[:, b, LOW, :], w_raw[:, :], w_part[:, b, HIGH, :].bitcast(F32), ALU.subtract).then_inc(w_low, 1)

            def step(e, b, c, is_last, final=False):
                u = NCH * e + c
                pool.wait_ge(high, u + 1)
                pool.tensor_tensor(hT[:, c % 2, LOW, :], hid[:, c % 2, :], hT[:, c % 2, HIGH, :].bitcast(F32), ALU.subtract).then_inc(low, 1)
                if c == 2 and not final:
                    weights(e + 1, 1 - b)

            pool.sem_inc(w_low, 1)
            pool.sem_inc(low, 2)
            units(pool, lambda: weights(0, 0), step)

        @block.vector
        def _(dve):
            dve.sem_inc(full, 2)
            dve.sem_inc(added, 2)

            def hidden(e, b, c):
                u = NCH * e + c
                dve.wait_ge(sig_done, u + 1)
                dve.tensor_tensor(act_g[:, c % 2, :], ps[:, c % 2, :], sig[:, c % 2, :], ALU.mult).then_inc(t_done, 1)
                dve.wait_ge(low, u + 1)
                dve.wait_ge(t_done, u + 1)
                dve.tensor_tensor(hid[:, c % 2, :], act_g[:, c % 2, :], ps[:, 2 + c % 2, :], ALU.mult).then_inc(full, 1)

            def step(e, b, c, is_last, final=False):
                if not is_last:
                    hidden(*after(e, b, c))
                dve.wait_ge(down_done, NCH * e + c + 1 + 2)
                for s in range(QT):
                    n = c * QT + s
                    last = dve.scalar_tensor_tensor(k.stream[:, n, :], ps[:, 4 + 2 * (c % 2) + s // 2, (s % 2) * D:(s % 2 + 1) * D],
                                                    k.comb[:, bass.ds(e, 1), n], k.stream[:, n, :], ALU.mult, ALU.add)
                last.then_inc(added, 1)

            units(dve, lambda: hidden(0, 0, 0), step)


def store_out(nc, k, out):
    with ExitStack() as ctx:
        stored = k.sem("stored")
        block = ctx.enter_context(nc.Block())

        @block.sync
        def _(sp):
            sp.dma_start(out.rearrange("(i p j) c -> p i (j c)", p=P, j=2),
                         k.stream[:, :, :].rearrange("p (i j) c -> p i (j c)", j=2)).then_inc(stored, 16)
            sp.wait_ge(stored, 16)


def build_program(nc, a, out):
    with ExitStack() as ctx:
        k = Parts()
        k.passing = []

        def stage_sem(name):
            k.passing.append(nc.alloc_semaphore(name=name))
            return k.passing[-1]

        k.stage_sem = stage_sem
        k.sem = lambda name: nc.alloc_semaphore(name=name)
        k.sbuf = lambda c: (lambda name, shape, dt=F32: c.enter_context(nc.sbuf_tensor(name, shape, dt)))
        sb = k.sbuf(ctx)
        k.psum = ctx.enter_context(nc.psum_tensor("psum", [P, 8, CH], F32))
        k.stream = sb("stream", [P, NT, D])
        k.ident = sb("ident", [P, P])
        k.ones = sb("ones", [P, P])
        k.zeros = sb("zeros", [P, D])
        k.eps = sb("eps", [P, 2])
        k.stats = sb("stats", [P, NT, 6])
        k.moments = sb("moments", [P, NT, 2])
        k.rstd = sb("rstd", [P, NT])
        k.ln_sems = [k.sem("ln_" + n) for n in ("stats", "aggregated", "root", "inv", "normed")]
        k.ln_turn = 0
        k.x_saved = k.sem("x_saved")
        k.x_loaded, k.zeros_ready, k.inbox_zeroed = k.sem("x_loaded"), k.sem("zeros_ready"), k.sem("inbox_zeroed")
        k.iota = sb("iota", [P, 16])
        k.before = sb("before", [P, P])
        k.gate = sb("gate", [P, K_MOE, NT])
        k.take = sb("take", [P, K_MOE, NT], U32)
        k.put = sb("put", [P, K_MOE, NT], U32)
        k.take_ready, k.scattered = k.sem("take_ready"), k.sem("scattered")
        build_scan(nc, k, a)
        make_indices(nc, k)
        route_tokens(nc, k, a)
        experts(nc, k, a)
        combine(nc, k, a)
        layer_norm(nc, k)
        build_attention(nc, k, a)
        with ExitStack() as ffn:
            sf = k.sbuf(ffn)
            xT = sf("x3_T", [P, 2, DH, T], F32R)
            k.comb = sf("comb", [P, NEX, NT])
            transpose_tiles(nc, k, "x3", xT)
            weigh_experts(nc, k, a, xT)
            swiglu_experts(nc, k, a, xT)
        layer_norm(nc, k)
        store_out(nc, k, out)


def build_attention(nc, k, a):
    with ExitStack() as ctx:
        sb = k.sbuf(ctx)
        k.v = sb("v_all", [P, NT, D])
        with ExitStack() as inner:
            si = k.sbuf(inner)
            k.wfold = si("w_fold", [P, 3, DH, D])
            k.wrot = si("w_rot", [P, 2, DH, D])
            xT = si("x2_T", [P, DH, T])
            fold_weights(nc, k, a)
            transpose_stream(nc, k, "x2", xT)
            project_qkv(nc, k, a, xT)
        k.attn = sb("attn", [P, NT, D])
        attention(nc, k, a)
        project_attention(nc, k, a)
        layer_norm(nc, k)


def build_scan(nc, k, a):
    with ExitStack() as scan:
        ss = k.sbuf(scan)
        k.xpT, k.gateT = ss("xpT", [P, DH, XW]), ss("gateT", [P, DH, TP])
        k.Dv = ss("Dv_sb", [P, DH])
        k.bad = ss("bad", [P, 1], mybir.dt.int32)
        k.A, k.B, k.csum = (ss(n, [P, DH, NS]) for n in ("A_sb", "B_sb", "csum_sb"))
        project_in(nc, k, a)
        load_scan_weights(nc, k, a)
        scan_chunks(nc, k, a)
        seams = nc.values_load(k.bad[0:1, 0:1], min_val=0, max_val=P * D * NS)
        with nc.If(seams > 0):
            nc.all_engine_barrier()
            reload_x(nc, k, a)
            nc.all_engine_barrier()
            scan_steps(nc, k, a)
            nc.all_engine_barrier()
        nc.all_engine_barrier()
        project_out(nc, k, a)
        free_semaphores(nc, k)
        layer_norm(nc, k)


SCRATCH = {"x_proj": ([D, TP], F32), "max_rows": ([BUFS, NSPLIT * NT, P], BF16), "qk_parts": ([2, NSPLIT, D, T], BF16), "inbox": ([8 * 1024, D], F32), "outbox": ([8 * 1024, D], F32)}


def host_layout(inputs):
    import numpy as np
    n = {k: np.asarray(v) for k, v in inputs.items()}
    c = np.ascontiguousarray
    x = n["L0_attn_x"][0]
    return {
        "x": c(x), "xs_T": c(x[::TS].T), "w_in_T": c(n["L0_attn_w_in"].T), "b_in": n["L0_attn_b_in"],
        "g_norm": n["L0_attn_g_norm"], "A": n["L0_attn_A"], "Bm": n["L0_attn_Bm"], "Cm": n["L0_attn_Cm"],
        "Dv": n["L0_attn_Dv"], "w_out_T": c(n["L0_attn_w_out"].T), "b_out": n["L0_attn_b_out"],
        "wg": n["L0_ffn_wg"], "w1": n["L0_ffn_w1"].reshape(E_MOE * D, HID), "w2": n["L0_ffn_w2"].reshape(E_MOE * HID, D),
        "b1_T": c(n["L0_ffn_b1"].reshape(E_MOE * HID // P, P).T), "b2": n["L0_ffn_b2"],
        "wq_down_T": c(n["L1_attn_Wq_down"].T), "wk_down_T": c(n["L1_attn_Wk_down"].T), "wv_down_T": c(n["L1_attn_Wv_down"].T),
        "wq_up_c": n["L1_attn_Wq_up_c"], "wq_up_e": n["L1_attn_Wq_up_e"],
        "wk_up_c": n["L1_attn_Wk_up_c"], "wk_up_e": n["L1_attn_Wk_up_e"], "wv_up": n["L1_attn_Wv_up"],
        "wc": n["L1_attn_Wc"], **rope_tables(),
        "gate_w_T": c(n["L1_ffn_gate_w"].T), "gate_b": n["L1_ffn_gate_b"],
        "w13_T": c(np.concatenate((n["L1_ffn_w13"], n["L1_ffn_w13_s"][None])).transpose(0, 2, 1)).reshape(NEX * D, 2 * INTER),
        "w2_T": c(np.concatenate((n["L1_ffn_w2"], n["L1_ffn_w2_s"][None])).transpose(0, 2, 1)).reshape(NEX * INTER, D),
    }


def rope_tables():
    import numpy as np
    inv = (np.float32(1.0) / np.float32(10000.0) ** (np.arange(0, HE, 2, dtype=np.float32) / np.float32(HE))).astype(np.float32)
    angle = np.arange(T, dtype=np.float32)[:, None] * inv[None, :]
    angle = np.concatenate((angle, angle), axis=-1).T
    cos, sin = np.ones((HD, T), np.float32), np.zeros((HD, T), np.float32)
    cos[HE:], sin[HE:] = np.cos(angle), np.sin(angle)
    return {"cos_T": cos, "sin_T": sin}


def kernel(**inputs):
    import numpy as np
    import concourse.bacc as bacc
    from concourse.bass_utils import run_bass_kernel_spmd

    nc = bacc.Bacc("TRN2", target_bir_lowering=False, num_devices=1)
    arrays = {f"in_{name}": np.ascontiguousarray(v) for name, v in host_layout(inputs).items()}
    a = {name[3:]: nc.dram_tensor(name, v.shape, mybir.dt.from_np(v.dtype), kind="ExternalInput").ap()
         for name, v in arrays.items()}
    for name, (shape, dt) in SCRATCH.items():
        a[name] = nc.dram_tensor(name, shape, dt).ap()
    out = nc.dram_tensor("out", (T, D), F32, kind="ExternalOutput").ap()
    build_program(nc, a, out)
    result = run_bass_kernel_spmd(nc, [arrays], core_ids=[0])
    return result.results[0]["out"].reshape(1, T, D)
```

```python
from contextlib import ExitStack

import concourse.bass as bass
from concourse import mybir

P = 128
ACT = mybir.ActivationFunctionType
ALU = mybir.AluOpType
AX = mybir.AxisListType
F32 = mybir.dt.float32
BF16 = mybir.dt.bfloat16
U32 = mybir.dt.uint32
F32R = mybir.dt.float32r

T = 4096
D = 256
DH = D // P
TS = 2
TP = T // TS
NS = 64
NT = T // P
NPAIR = TP // P
CH = 512
CHUNKS = 8
LEN = TP // CHUNKS
WARM = 32
BL = 8
RING_X = 4
XW = WARM + TP + LEN - BL + 2 * BL
E_MOE = 8
K_MOE = 2
HID = 1024
CAP = K_MOE * ((T + E_MOE - 1) // E_MOE)
SLOTS = E_MOE * CAP
RMS_EPS = 1e-6
LN_EPS = 1e-5


HIGH, LOW = 0, 1
SPLIT = ((HIGH, HIGH), (LOW, HIGH), (HIGH, LOW))


class Parts:
    pass


class Steps:

    def __init__(self, sem, base=0):
        self.sem, self.base, self.n = sem, base, 0

    def link(self, eng, ins):
        self.n += 1
        ins.then_inc(self.sem, 1)
        eng.wait_ge(self.sem, self.base + self.n)


def project_in(nc, k, a):
    with ExitStack() as ctx:
        sb, sem = k.sbuf(ctx), k.stage_sem
        xT = sb("xsT", [P, DH, TP])
        sq = sb("xsq", [P, 2, DH, CH])
        rms = sb("rms", [P, 2, CH])
        sig = sb("gate_sig", [P, 2, CH])
        w = sb("w_in_sb", [P, DH, 2 * D])
        g = sb("g_norm_sb", [P, DH])
        b = sb("b_in_sb", [P, 2 * DH])
        w_in, gb_in = sem("w_in_in"), sem("gb_in")
        x_in = [sem(f"xsT_in{c}") for c in range(TP // CH)]
        const_ready, squares, meansq, root, scaled = (sem(n) for n in (
            "ones_ready", "squares_ready", "meansq_ready", "root_ready", "scaled_ready"))
        inv_ready, projected, drained, sigmoid, gated = (sem(n) for n in (
            "inv_rms_ready", "xz_ready", "xz_drained", "gate_sigmoid", "gate_done"))
        NC = TP // CH
        ps = k.psum
        block = ctx.enter_context(nc.Block())

        @block.sync
        def _(sp):
            for c in range(NC):
                sp.dma_start(xT[:, :, c * CH:(c + 1) * CH],
                             a["xs_T"].rearrange("(h p) t -> p h t", p=P)[:, :, c * CH:(c + 1) * CH]).then_inc(x_in[c], 16)
                if c == 0:
                    sp.dma_start(g[:, :], a["g_norm"].rearrange("(h p) -> p h", p=P),
                                 allow_slow_non_contiguous=True).then_inc(gb_in, 16)
                    sp.dma_start(b[:, :], a["b_in"].rearrange("(e p) -> p e", p=P),
                                 allow_slow_non_contiguous=True).then_inc(gb_in, 16)
                    sp.dma_start(w[:, :, :], a["w_in_T"].rearrange("(h p) e -> p h e", p=P)).then_inc(w_in, 16)
            sp.wait_ge(k.zeros_ready, 1)
            for e in range(8):
                sp.dma_start(a["inbox"][e * 1024:(e + 1) * 1024, :].rearrange("(s p) c -> p s c", p=P),
                             k.zeros[:, :].unsqueeze(1).to_broadcast([P, 8, D])).then_inc(k.inbox_zeroed, 16)

        @block.gpsimd
        def _(pool):
            pool.memset(k.ident[:, :], 0.0).then_inc(const_ready, 1)
            pool.memset(k.ones[:, :], 1.0).then_inc(const_ready, 1)
            pool.memset(k.eps[:, 0:1], RMS_EPS).then_inc(const_ready, 1)
            pool.memset(k.eps[:, 1:2], LN_EPS).then_inc(const_ready, 1)
            pool.memset(k.zeros[:, :], 0.0).then_inc(k.zeros_ready, 1)
            pool.wait_ge(const_ready, 4)
            pool.affine_select(out=k.ident[:, :], in_=k.ident[:, :], compare_op=ALU.not_equal, fill=1.0,
                               base=0, pattern=[[-1, P]], channel_multiplier=1).then_inc(const_ready, 1)

        @block.vector
        def _(dve):
            dve.memset(k.xpT[:, :, 0:WARM], 0.0)
            dve.memset(k.xpT[:, :, WARM + TP:], 0.0)
            dve.wait_ge(gb_in, 32)
            for c in range(NC):
                cols = slice(c * CH, (c + 1) * CH)
                dve.wait_ge(x_in[c], 16)
                if c >= 2:
                    dve.wait_ge(meansq, c - 1)
                dve.tensor_tensor(sq[:, c % 2, :, :], xT[:, :, cols], xT[:, :, cols], ALU.mult).then_inc(squares, 1)
            for c in range(NC):
                cols = slice(c * CH, (c + 1) * CH)
                dve.wait_ge(root, c + 1)
                dve.reciprocal(rms[:, c % 2, :], rms[:, c % 2, :]).then_inc(inv_ready, 1)
                dve.wait_ge(inv_ready, c + 1)
                for h in range(DH):
                    dve.scalar_tensor_tensor(xT[:, h, cols], xT[:, h, cols], g[:, h:h + 1], rms[:, c % 2, :],
                                             ALU.mult, ALU.mult).then_inc(scaled, 1)
            for c in range(NC):
                cols = slice(c * CH, (c + 1) * CH)
                for h in range(DH):
                    n = c * DH + h
                    dve.wait_ge(sigmoid, n + 1)
                    dve.scalar_tensor_tensor(k.gateT[:, h, cols], ps[:, 4 + n % 2, :], b[:, DH + h:DH + h + 1],
                                             sig[:, n % 2, :], ALU.add, ALU.mult).then_inc(gated, 1)

        @block.tensor
        def _(pe):
            pe.wait_ge(const_ready, 5)
            for c in range(NC):
                pe.wait_ge(squares, c + 1)
                for h in range(DH):
                    last = pe.matmul(ps[:, c, :], k.ones[:, :], sq[:, c % 2, h, :], start=(h == 0), stop=(h == DH - 1))
                last.then_inc(meansq, 1)
            pe.wait_ge(w_in, 16)
            for c in range(NC):
                cols = slice(c * CH, (c + 1) * CH)
                pe.wait_ge(scaled, DH * (c + 1))
                for e in range(2 * DH):
                    bank = 6 + e if e < DH else 4 + (e - DH)
                    if c >= 1:
                        if e < DH:
                            pe.wait_ge(drained, DH * (c - 1) + e + 1)
                        else:
                            pe.wait_ge(gated, DH * (c - 1) + e - DH + 1)
                    for h in range(DH):
                        last = pe.matmul(ps[:, bank, :], w[:, h, e * P:(e + 1) * P], xT[:, h, cols],
                                         start=(h == 0), stop=(h == DH - 1))
                    last.then_inc(projected, 1)

        @block.scalar
        def _(act):
            act.wait_ge(const_ready, 5)
            for c in range(NC):
                act.wait_ge(meansq, c + 1)
                if c >= 2:
                    act.wait_ge(scaled, DH * (c - 1))
                act.activation(rms[:, c % 2, :], ps[:, c, :], ACT.Sqrt, bias=k.eps[:, 0:1], scale=1.0 / D).then_inc(root, 1)
            for c in range(NC):
                cols = slice(c * CH, (c + 1) * CH)
                for e in range(2 * DH):
                    act.wait_ge(projected, 2 * DH * c + e + 1)
                    if e < DH:
                        act.activation(k.xpT[:, e, WARM + c * CH:WARM + (c + 1) * CH], ps[:, 6 + e, :], ACT.Identity, bias=b[:, e:e + 1]).then_inc(drained, 1)
                    else:
                        n = c * DH + e - DH
                        if n >= 2:
                            act.wait_ge(gated, n - 1)
                        act.activation(sig[:, n % 2, :], ps[:, 4 + n % 2, :], ACT.Sigmoid, bias=b[:, e:e + 1]).then_inc(sigmoid, 1)


def load_scan_weights(nc, k, a):
    with ExitStack() as loc:
        cm = k.sbuf(loc)("cm_sb", [P, DH, NS])
        ab_in, csum, copied, a_copied = k.sem("ab_in"), k.sem("csum_ready"), k.sem("csum_copied"), k.sem("a_copied")
        block = loc.enter_context(nc.Block())

        @block.sync
        def _(sp):
            for dst, src in ((k.A, a["A"]), (k.B, a["Bm"]), (cm, a["Cm"])):
                sp.dma_start(dst[:, :, :], src.rearrange("(h p) s -> p h s", p=P)).then_inc(ab_in, 16)
            sp.dma_start(k.Dv[:, :], a["Dv"].rearrange("(h p) -> p h", p=P), allow_slow_non_contiguous=True).then_inc(ab_in, 16)
            sp.dma_start(k.stream[:, :, :].rearrange("p (i j) c -> p i (j c)", j=2),
                         a["x"].rearrange("(i p j) c -> p i (j c)", p=P, j=2)).then_inc(k.x_loaded, 16)
            sp.dma_start(a["x_proj"].rearrange("(h p) t -> p h t", p=P), k.xpT[:, :, WARM:WARM + TP]).then_inc(k.x_saved, 16)

        @block.tensor
        def _(pe):
            pe.wait_ge(ab_in, 64)
            for h in range(DH):
                last = pe.matmul(k.psum[:, 1, 0:NS], k.ones[:, :], cm[:, h, :], start=(h == 0), stop=(h == DH - 1))
            last.then_inc(csum, 1)

        @block.vector
        def _(dve):
            dve.wait_ge(ab_in, 64)
            dve.tensor_copy(k.psum[:, 0, 0:DH * NS].rearrange("p (h s) -> p h s", h=DH), k.A[:, :, :]).then_inc(a_copied, 1)
            dve.wait_ge(csum, 1)
            dve.tensor_copy(k.csum[:, 0, :], k.psum[:, 1, 0:NS]).then_inc(copied, 1)
            dve.tensor_copy(k.csum[:, 1, :], k.psum[:, 1, 0:NS]).then_inc(copied, 1)


def scan_chunks(nc, k, a):
    GW = CHUNKS * NS
    NMAIN = LEN // BL
    NWARM = WARM // BL
    with ExitStack() as ctx:
        sb, sem = k.sbuf(ctx), k.stage_sem
        hist = sb("h_hist", [P, 2, BL, DH, GW])
        diag = sb("csum_diag", [P, NS, P])
        xb = sb("x_times_b", [P, RING_X, DH, GW])
        xs = sb("x_slab", [P, 2, DH, CHUNKS, BL])
        warm = sb("warm_end", [P, DH, GW])
        diff = sb("seam_diff", [P, DH, CHUNKS - 1, NS])
        count = sb("seam_count", [P, 1])
        xs_ready, xb_ready, ha_ready, u_ready, h_ready, y_done, y_taken, h_zero, diags, warm_kept = (
            sem("ch_" + n) for n in ("xs", "xb", "ha", "u", "h", "y_done", "y_taken", "h_zero", "diag", "warm"))
        compared, counted, summed, told = (sem("ch_" + n) for n in ("compared", "counted", "summed", "told"))
        ps = k.psum
        ha, u = ps[:, 3:5, :], ps[:, 5:7, :]
        block = ctx.enter_context(nc.Block())

        def ring(B):
            return (B - NWARM) % 2

        @block.vector
        def _(dve):
            dve.memset(hist[:, ring(-1), BL - 1, :, :], 0.0).then_inc(h_zero, 1)
            for s in range(NS):
                last = dve.tensor_scalar(diag[:, s, :], k.ident[:, :], k.csum[:, 0, s:s + 1], None, ALU.mult)
            last.then_inc(diags, 1)

            def slab(B, slot):
                src = k.xpT[:, :, bass.ds(B * BL, TP)].rearrange("p h (c l) -> p h c l", l=LEN)[:, :, :, 0:BL]
                dve.tensor_scalar(xs[:, slot, :, :, :], src, 1.0, None, ALU.mult).then_inc(xs_ready, 1)

            def steps(B, slot):
                for t in range(BL):
                    prev = hist[:, slot, t - 1] if t else hist[:, 1 - slot, BL - 1]
                    for g in range(DH):
                        n = 2 * BL * B + 2 * t + g
                        if isinstance(n, int) and n < 2:
                            dve.wait_ge(h_zero, 1)
                        else:
                            dve.wait_ge(h_ready, n - 1)
                        dve.tensor_tensor(ha[:, g, :].rearrange("p (c s) -> p c s", s=NS), prev[:, g, :].rearrange("p (c s) -> p c s", s=NS),
                                          ps[:, 0, g * NS:(g + 1) * NS].unsqueeze(1).to_broadcast([P, CHUNKS, NS]), ALU.mult).then_inc(ha_ready, 1)
                        dve.wait_ge(xb_ready, n + 1)
                        dve.wait_ge(ha_ready, n + 1)
                        dve.tensor_tensor(u[:, g, :], ha[:, g, :], xb[:, t % RING_X, g, :], ALU.add).then_inc(u_ready, 1)

            def take_y(m, bank):
                dve.wait_ge(y_done, m + 1)
                for h in range(DH):
                    cols = k.xpT[:, h, bass.ds(WARM + m * BL, TP)].rearrange("p (c l) -> p c l", l=LEN)[:, :, 0:BL]
                    last = dve.scalar_tensor_tensor(cols, cols, k.Dv[:, h:h + 1],
                                                    ps[:, 1 + bank, 0:BL * DH * CHUNKS].rearrange("p (t h c) -> p h c t", t=BL, h=DH)[:, h],
                                                    ALU.mult, ALU.add)
                last.then_inc(y_taken, 1)

            slab(0, ring(0))
            for B in range(NWARM):
                slab(B + 1, ring(B + 1))
                steps(B, ring(B))
            dve.wait_ge(k.x_saved, 16)
            slab(NWARM + 1, 1)
            steps(NWARM, 0)
            slab(NWARM + 2, 0)
            steps(NWARM + 1, 1)
            take_y(0, 0)
            with dve.Fori(1, NMAIN // 2) as i:
                slab(NWARM + 2 * i + 1, 1)
                steps(NWARM + 2 * i, 0)
                take_y(2 * i - 1, 1)
                slab(NWARM + 2 * i + 2, 0)
                steps(NWARM + 2 * i + 1, 1)
                take_y(2 * i, 0)
            dve.wait_ge(h_ready, 2 * (WARM + LEN))
            dve.wait_ge(warm_kept, 2)
            for g in range(DH):
                last = dve.tensor_tensor(diff[:, g, :, :].rearrange("p c s -> p (c s)"), warm[:, g, NS:], hist[:, 1, BL - 1, g, 0:GW - NS], ALU.not_equal)
            last.then_inc(compared, 1)
            dve.wait_ge(compared, 1)
            dve.tensor_reduce(count[:, :], diff[:, :, :, :].rearrange("p h c s -> p (h c s)"), AX.X, ALU.add).then_inc(counted, 1)
            take_y(NMAIN - 1, 1)
            dve.wait_ge(summed, 1)
            dve.tensor_copy(k.bad[:, :], ps[:, 7, 0:1]).then_inc(told, 1)
            dve.wait_ge(told, 1)

        @block.gpsimd
        def _(pool):
            def products(B, slot):
                pool.wait_ge(xs_ready, B + 1)
                for t in range(BL):
                    for g in range(DH):
                        n = 2 * BL * B + 2 * t + g
                        if not isinstance(n, int) or n >= 2 * RING_X:
                            pool.wait_ge(u_ready, n - 2 * RING_X + 1)
                        pool.tensor_tensor(xb[:, t % RING_X, g, :].rearrange("p (c s) -> p c s", s=NS),
                                           xs[:, slot, g, :, t].unsqueeze(2).to_broadcast([P, CHUNKS, NS]),
                                           k.B[:, g, :].unsqueeze(1).to_broadcast([P, CHUNKS, NS]), ALU.mult).then_inc(xb_ready, 1)

            for B in range(NWARM):
                products(B, ring(B))
            with pool.Fori(0, NMAIN // 2) as i:
                products(NWARM + 2 * i, 0)
                products(NWARM + 2 * i + 1, 1)

        @block.scalar
        def _(act):
            def steps(B, slot):
                for t in range(BL):
                    for g in range(DH):
                        n = 2 * BL * B + 2 * t + g
                        act.wait_ge(u_ready, n + 1)
                        if isinstance(B, int) and B == NWARM - 1 and t == BL - 1:
                            act.activation(warm[:, g, :], u[:, g, :], ACT.Tanh).then_inc(warm_kept, 1)
                        act.activation(hist[:, slot, t, g, :], u[:, g, :], ACT.Tanh).then_inc(h_ready, 1)

            for B in range(NWARM + 2):
                steps(B, ring(B))
            with act.Fori(1, NMAIN // 2) as i:
                for j in range(2):
                    act.wait_ge(y_done, 2 * i + j - 1)
                    steps(NWARM + 2 * i + j, j)

        @block.tensor
        def _(pe):
            pe.wait_ge(diags, 1)

            def outputs(m, j):
                pe.wait_ge(h_ready, 2 * BL * (NWARM + m + 1))
                for s in range(NS):
                    last = pe.matmul(ps[:, 1 + j, 0:BL * DH * CHUNKS], diag[:, s, :],
                                     hist[:, j, :, :, :].rearrange("p t h (c s) -> p (t h) c s", s=NS)[:, :, :, s],
                                     start=(s == 0), stop=(s == NS - 1))
                last.then_inc(y_done, 1)

            outputs(0, 0)
            outputs(1, 1)
            with pe.Fori(1, NMAIN // 2) as i:
                for j in range(2):
                    pe.wait_ge(y_taken, 2 * i + j - 1)
                    outputs(2 * i + j, j)
            pe.wait_ge(counted, 1)
            pe.matmul(ps[:, 7, 0:1], k.ones[:, :], count[:, :], start=True, stop=True).then_inc(summed, 1)


def reload_x(nc, k, a):
    with ExitStack() as loc:
        back = k.sem("x_back")
        block = loc.enter_context(nc.Block())

        @block.sync
        def _(sp):
            sp.dma_start(k.xpT[:, :, WARM:WARM + TP], a["x_proj"].rearrange("(h p) t -> p h t", p=P)).then_inc(back, 16)
            sp.wait_ge(back, 16)


def scan_steps(nc, k, a):
    U = 8
    with ExitStack() as ctx:
        sb, sem = k.sbuf(ctx), k.stage_sem
        h = sb("seq_h", [P, 2, DH, NS])
        ha = sb("seq_ha", [P, 2, DH, NS])
        u = sb("seq_u", [P, 2, DH, NS])
        junk = sb("seq_junk", [P, NS])
        xs = sb("seq_x", [P, DH, U])
        ys = sb("seq_y", [P, DH, U])
        zeroed, x_slab, ha_ready, u_ready, h_ready, y_ready, y_saved = (sem("seq_" + n) for n in (
            "zeroed", "x_slab", "ha_ready", "u_ready", "h_ready", "y_ready", "y_saved"))
        block = ctx.enter_context(nc.Block())

        @block.vector
        def _(dve):
            dve.memset(h[:, (U - 1) % 2, :, :], 0.0).then_inc(zeroed, 1)
            dve.wait_ge(zeroed, 1)
            with dve.Fori(0, TP // U) as i:
                base = i * U
                dve.tensor_copy(xs[:, :, :], k.xpT[:, :, bass.ds(base + WARM, U)]).then_inc(x_slab, 1)
                dve.wait_ge(x_slab, i + 1)
                for t in range(U + 1):
                    if t < U:
                        if t > 0:
                            dve.wait_ge(h_ready, base + t)
                        dve.tensor_tensor(ha[:, t % 2, :, :], h[:, (t - 1) % 2, :, :], k.A[:, :, :], ALU.mult).then_inc(ha_ready, 1)
                        dve.wait_ge(ha_ready, base + t + 1)
                        for c in range(DH):
                            last = dve.scalar_tensor_tensor(u[:, t % 2, c, :], k.B[:, c, :], xs[:, c, t:t + 1], ha[:, t % 2, c, :],
                                                            ALU.mult, ALU.add)
                        last.then_inc(u_ready, 1)
                    else:
                        dve.wait_ge(h_ready, base + U)
                    if t > 0:
                        for c in range(DH):
                            last = dve.tensor_tensor_reduce(out=junk[:, :], in0=h[:, (t - 1) % 2, c, :], in1=k.csum[:, c, :],
                                                            scale=1.0, scalar=0.0, op0=ALU.mult, op1=ALU.add,
                                                            accum_out=ys[:, c, t - 1:t])
                            last.then_inc(y_ready, 1)
                            dve.wait_ge(y_ready, (base + t - 1) * DH + c + 1)
                for c in range(DH):
                    last = dve.scalar_tensor_tensor(k.xpT[:, c, bass.ds(base + WARM, U)], xs[:, c, :], k.Dv[:, c:c + 1], ys[:, c, :],
                                                    ALU.mult, ALU.add)
                last.then_inc(y_saved, 1)
                dve.wait_ge(y_saved, i + 1)

        @block.scalar
        def _(act):
            with act.Fori(0, TP // U) as i:
                for t in range(U):
                    act.wait_ge(u_ready, i * U + t + 1)
                    act.activation(h[:, t % 2, :, :], u[:, t % 2, :, :], ACT.Tanh).then_inc(h_ready, 1)


def free_semaphores(nc, k):
    nc.all_engine_barrier()
    nc.clear_and_free_semaphores(k.passing)
    nc.all_engine_barrier()
    k.passing = []


LNG = 4


class Norm:

    def __init__(self, k):
        self.k, self.turn = k, k.ln_turn
        k.ln_turn += 1

    def stats(self, dve, g):
        k = self.k
        added, aggregated, _, _, _ = k.ln_sems
        for n in range(g * LNG, (g + 1) * LNG):
            dve.bn_stats(k.stats[:, n, :], k.stream[:, n, :]).then_inc(added, 1)
        for n in range(g * LNG, (g + 1) * LNG):
            dve.wait_ge(added, NT * self.turn + n + 1)
            last = dve.bn_aggr(k.moments[:, n, :], k.stats[:, n, :])
        last.then_inc(aggregated, 1)

    def root(self, act, g):
        k = self.k
        _, aggregated, root, _, _ = k.ln_sems
        act.wait_ge(aggregated, NT // LNG * self.turn + g + 1)
        act.activation(k.rstd[:, g * LNG:(g + 1) * LNG], k.moments[:, g * LNG:(g + 1) * LNG, 1], ACT.Sqrt,
                       bias=k.eps[:, 1:2]).then_inc(root, 1)

    def apply(self, dve, g):
        k = self.k
        _, _, root, inv, normed = k.ln_sems
        dve.wait_ge(root, NT // LNG * self.turn + g + 1)
        dve.reciprocal(k.rstd[:, g * LNG:(g + 1) * LNG], k.rstd[:, g * LNG:(g + 1) * LNG]).then_inc(inv, 1)
        dve.wait_ge(inv, NT // LNG * self.turn + g + 1)
        for n in range(g * LNG, (g + 1) * LNG):
            last = dve.tensor_scalar(k.stream[:, n, :], k.stream[:, n, :], k.moments[:, n, 0:1], k.rstd[:, n:n + 1],
                                     ALU.subtract, ALU.mult)
        last.then_inc(normed, 1)

    def wait(self, eng, g):
        eng.wait_ge(self.k.ln_sems[4], NT // LNG * self.turn + g + 1)


NG_LN = NT // LNG


def project_out(nc, k, a):
    norm = Norm(k)
    assert CH == LNG * P
    with ExitStack() as ctx:
        sb, sem = k.sbuf(ctx), k.stage_sem
        w = sb("w_out_sb", [P, DH, D])
        bo = sb("b_out_sb", [1, D])
        wg = sb("wg_sb", [P, DH, E_MOE])
        xt = sb("route_xT", [P, 2, DH, CH])
        logits_T = sb("route_logits_T", [E_MOE, T])
        loaded, wg_in, z_ready, projected, added = (sem("po_" + n) for n in ("loaded", "wg_in", "z", "proj", "added"))
        turned, copied, l_done, l_copied, scored = (sem("route_" + n) for n in ("turned", "copied", "l_done", "l_copied", "scored"))
        ps = k.psum
        block = ctx.enter_context(nc.Block())

        @block.sync
        def _(sp):
            sp.dma_start(w[:, :, :], a["w_out_T"].rearrange("(h p) e -> p h e", p=P)).then_inc(loaded, 16)
            sp.dma_start(bo[:, :], a["b_out"].rearrange("(o e) -> o e", o=1)).then_inc(loaded, 16)
            sp.dma_start(wg[:, :, :], a["wg"].rearrange("(h p) e -> p h e", p=P)).then_inc(wg_in, 16)

        @block.vector
        def _(dve):
            NC = TP // CH
            for c in range(NC):
                cols = slice(c * CH, (c + 1) * CH)
                for h in range(DH):
                    dve.tensor_tensor(k.gateT[:, h, cols], k.xpT[:, h, WARM + c * CH:WARM + (c + 1) * CH],
                                      k.gateT[:, h, cols], ALU.mult).then_inc(z_ready, 1)
            dve.wait_ge(k.x_loaded, 16)
            for i in range(NPAIR):
                dve.wait_ge(projected, i + 1)
                pair = k.stream[:, 2 * i:2 * i + 2, :]
                dve.tensor_tensor(pair, pair, ps[:, i % 4, 0:D].unsqueeze(1).to_broadcast([P, 2, D]), ALU.add).then_inc(added, 1)
                g = (i + 1) * 2 // LNG - 1
                if (i + 1) * 2 % LNG == 0:
                    dve.wait_ge(added, i + 1)
                    norm.stats(dve, g)
                    if g >= 1:
                        norm.apply(dve, g - 1)
            norm.apply(dve, NG_LN - 1)

        @block.scalar
        def _(act):
            def copy(g):
                if g >= 2:
                    act.wait_ge(l_done, g - 1)
                for h in range(DH):
                    act.wait_ge(turned, DH * g + h + 1)
                    act.activation(xt[:, g % 2, h, :], ps[:, 4 + h, :], ACT.Copy).then_inc(copied, 1)

            def scores(g):
                act.wait_ge(l_done, g + 1)
                act.activation(logits_T[:, g * CH:(g + 1) * CH], ps[0:E_MOE, 6, :], ACT.Copy).then_inc(l_copied, 1)

            for g in range(NG_LN + 3):
                if g < NG_LN:
                    norm.root(act, g)
                if 2 <= g < NG_LN + 2:
                    copy(g - 2)
                if g >= 3:
                    scores(g - 3)

        @block.tensor
        def _(pe):
            def turn(g):
                norm.wait(pe, g)
                if g >= 1:
                    pe.wait_ge(copied, DH * g)
                for h in range(DH):
                    for t in range(LNG):
                        last = pe.transpose(ps[:, 4 + h, t * P:(t + 1) * P], k.stream[:, g * LNG + t, h * P:(h + 1) * P], k.ident[:, :])
                    last.then_inc(turned, 1)

            def scores(g):
                pe.wait_ge(copied, DH * g + DH)
                if g >= 1:
                    pe.wait_ge(l_copied, g)
                for h in range(DH):
                    last = pe.matmul(ps[0:E_MOE, 6, :], wg[:, h, :], xt[:, g % 2, h, :], start=(h == 0), stop=(h == DH - 1))
                last.then_inc(l_done, 1)

            pe.wait_ge(loaded, 32)
            pe.wait_ge(wg_in, 16)
            for i in range(NPAIR):
                pe.wait_ge(z_ready, DH * (i * P // CH + 1))
                if i >= 4:
                    pe.wait_ge(added, i - 3)
                acc = ps[:, i % 4, 0:D]
                for h in range(DH):
                    pe.matmul(acc, k.gateT[:, h, i * P:(i + 1) * P], w[:, h, :], start=(h == 0), stop=False)
                pe.matmul(acc, k.ones[0:1, :], bo[:, :], start=False, stop=True).then_inc(projected, 1)
                g = (i + 1) * 2 // LNG - 1
                if (i + 1) * 2 % LNG == 0:
                    if g >= 2:
                        turn(g - 2)
                    if g >= 3:
                        scores(g - 3)
            for g in range(NG_LN, NG_LN + 3):
                if g < NG_LN + 2:
                    turn(g - 2)
                scores(g - 3)
            for n in range(NT):
                pe.wait_ge(l_copied, n // LNG + 1)
                last = pe.transpose(ps[:, 7, n * E_MOE:(n + 1) * E_MOE], logits_T[:, n * P:(n + 1) * P], k.ident[0:E_MOE, 0:E_MOE])
            last.then_inc(scored, 1)


def make_indices(nc, k):
    with ExitStack() as loc:
        iota_i = k.sbuf(loc)("iota_i", [P, 16], mybir.dt.int32)
        made, tri = k.sem("iota_made"), k.sem("tri_made")
        block = loc.enter_context(nc.Block())

        @block.gpsimd
        def _(pool):
            pool.iota(iota_i[:, :], pattern=[[1, 16]], base=0, channel_multiplier=0).then_inc(made, 1)
            pool.memset(k.before[:, :], 1.0).then_inc(tri, 1)
            pool.wait_ge(tri, 1)
            pool.affine_select(out=k.before[:, :], in_=k.before[:, :], compare_op=ALU.is_ge, fill=0.0,
                               base=-1, pattern=[[1, P]], channel_multiplier=-1).then_inc(tri, 1)

        @block.vector
        def _(dve):
            dve.wait_ge(made, 1)
            dve.tensor_copy(k.iota[:, :], iota_i[:, :]).then_inc(made, 1)


def route_tokens(nc, k, a):
    with ExitStack() as ctx:
        sb, sem = k.sbuf(ctx), k.stage_sem
        logits = sb("route_logits", [P, NT, E_MOE])
        top = sb("route_top", [P, NT, 8])
        top_i = sb("route_top_i", [P, NT, 8], U32)
        choice = sb("route_choice", [P, K_MOE, NT])
        mask = sb("route_mask", [P, K_MOE, NT, E_MOE])
        pairs = sb("route_pairs", [P, K_MOE, NPAIR, E_MOE])
        total = sb("route_total", [P, K_MOE, NPAIR, E_MOE])
        upto = sb("route_upto", [P, K_MOE, NPAIR, E_MOE])
        loc = sb("route_loc", [P, K_MOE, NT, E_MOE])
        slot = sb("route_slot", [P, K_MOE, NT])
        valid = sb("route_valid", [P, K_MOE, NT])
        row = sb("route_row", [P, K_MOE, NT])
        step, prefixed, gap, put_ready = (sem("route_" + n) for n in ("step", "prefixed", "gap", "put_ready"))
        es = sem("route_exp")
        ps = k.psum
        block = ctx.enter_context(nc.Block())

        @block.tensor
        def _(pe):
            pe.wait_ge(step, 4)
            pe.matmul(ps[:, 6, 0:2 * P], k.before[:, :], pairs[:, :, :, :], start=True, stop=True)
            pe.matmul(ps[:, 5, 0:2 * P], k.ones[:, :], pairs[:, :, :, :], start=True, stop=True).then_inc(prefixed, 1)

        @block.scalar
        def _(act):
            act.wait_ge(gap, 1)
            act.activation(k.gate[:, 1, :], k.gate[:, 0, :], ACT.Exp).then_inc(es, 1)

        @block.vector
        def _(dve):
            s = Steps(step)
            s.link(dve, dve.tensor_copy(logits[:, :, :], ps[:, 7, 0:NT * E_MOE].rearrange("p (n e) -> p n e", e=E_MOE)))
            for n in range(NT):
                last = dve.max(top[:, n, :], logits[:, n, :])
            s.link(dve, last)
            for n in range(NT):
                last = dve.max_index(top_i[:, n, :], top[:, n, :], logits[:, n, :])
            s.link(dve, last)
            for c in range(K_MOE):
                last = dve.tensor_copy(choice[:, c, :], top_i[:, :, c])
            chosen = sem("route_chosen")
            last.then_inc(chosen, 1)
            dve.wait_ge(chosen, 1)
            for c in range(K_MOE):
                last = dve.tensor_tensor(mask[:, c, :, :], k.iota[:, 0:E_MOE].unsqueeze(1).to_broadcast([P, NT, E_MOE]),
                                         choice[:, c, :].unsqueeze(2).to_broadcast([P, NT, E_MOE]), ALU.is_equal)
            masked = sem("route_masked")
            last.then_inc(masked, 1)
            dve.wait_ge(masked, 1)
            for c in range(K_MOE):
                two = mask[:, c, :, :].rearrange("p (i j) e -> p i j e", j=2)
                last = dve.tensor_tensor(pairs[:, c, :, :], two[:, :, 0, :], two[:, :, 1, :], ALU.add)
            s.link(dve, last)
            dve.tensor_tensor(k.gate[:, 0, :], top[:, :, 1], top[:, :, 0], ALU.subtract).then_inc(gap, 1)
            dve.wait_ge(prefixed, 1)
            s.link(dve, dve.tensor_copy(total[:, :, :, :], ps[:, 5, 0:2 * P].rearrange("p (c i e) -> p c i e", c=K_MOE, e=E_MOE)))
            for e in range(E_MOE):
                last = dve.tensor_tensor_scan(upto[:, :, :, e].rearrange("p c i -> p (c i)"), k.ones[:, 0:K_MOE * NPAIR],
                                              total[:, :, :, e].rearrange("p c i -> p (c i)"), 0.0, ALU.mult, ALU.add)
            s.link(dve, last)
            s.link(dve, dve.tensor_tensor(upto[:, :, :, :], upto[:, :, :, :], total[:, :, :, :], ALU.subtract))
            s.link(dve, dve.tensor_tensor(upto[:, :, :, :], upto[:, :, :, :],
                                          ps[:, 6, 0:2 * P].rearrange("p (c i e) -> p c i e", c=K_MOE, e=E_MOE), ALU.add))
            for c in range(K_MOE):
                l2 = loc[:, c, :, :].rearrange("p (i j) e -> p i j e", j=2)
                m2 = mask[:, c, :, :].rearrange("p (i j) e -> p i j e", j=2)
                dve.tensor_copy(l2[:, :, 0, :], upto[:, c, :, :])
                last = dve.tensor_tensor(l2[:, :, 1, :], upto[:, c, :, :], m2[:, :, 0, :], ALU.add)
            s.link(dve, last)
            s.link(dve, dve.tensor_tensor(loc[:, :, :, :], loc[:, :, :, :], mask[:, :, :, :], ALU.mult))
            s.link(dve, dve.tensor_reduce(slot[:, :, :], loc[:, :, :, :], AX.X, ALU.add))
            s.link(dve, dve.tensor_scalar(valid[:, :, :], slot[:, :, :], float(CAP), None, ALU.is_lt))
            s.link(dve, dve.scalar_tensor_tensor(row[:, :, :], choice[:, :, :], float(CAP), slot[:, :, :], ALU.mult, ALU.add))
            s.link(dve, dve.tensor_scalar(slot[:, :, :], valid[:, :, :], float(-2 * SLOTS), float(2 * SLOTS), ALU.mult, ALU.add))
            s.link(dve, dve.tensor_tensor(slot[:, :, :], slot[:, :, :], row[:, :, :], ALU.add))
            dve.tensor_copy(k.put[:, :, :], slot[:, :, :]).then_inc(put_ready, 1)
            s.link(dve, dve.tensor_tensor(row[:, :, :], row[:, :, :], valid[:, :, :], ALU.mult))
            dve.tensor_copy(k.take[:, :, :], row[:, :, :]).then_inc(k.take_ready, 1)
            dve.wait_ge(es, 1)
            s.link(dve, dve.tensor_scalar(k.gate[:, 0, :], k.gate[:, 1, :], 1.0, None, ALU.add))
            s.link(dve, dve.reciprocal(k.gate[:, 0, :], k.gate[:, 0, :]))
            s.link(dve, dve.tensor_tensor(k.gate[:, 1, :], k.gate[:, 1, :], k.gate[:, 0, :], ALU.mult))
            s.link(dve, dve.tensor_tensor(k.gate[:, :, :], k.gate[:, :, :], valid[:, :, :], ALU.mult))


def experts(nc, k, a):
    ST = CAP // P
    HT = HID // P
    G = CH // P
    NQ = DH * ST // G
    NM = HT * CAP // CH
    NY = ST // 2
    with ExitStack() as ctx:
        sb, sem = k.sbuf(ctx), k.stage_sem
        w1_raw = sb("w1_raw", [P, DH, HID])
        w2_raw = sb("w2_raw", [P, HT, D])
        w1 = sb("w1_part", [P, 2, DH, HID], F32R)
        w2 = sb("w2_part", [P, 2, HT, D], F32R)
        xe = sb("xe_sb", [P, ST, D])
        xeT = sb("xeT_part", [P, 2, DH, CAP], F32R)
        hid = sb("hid_f32", [P, 2, CH])
        hT = sb("hT_part", [P, 2, HT, CAP], F32R)
        ye = sb("ye_sb", [P, ST, D])
        b1 = sb("b1_sb", [P, E_MOE, HT])
        b2 = sb("b2_sb", [P, E_MOE, D])
        b1e = sb("b1_now", [P, HT])
        b_in, b1_ready, x_in, w1_in, w2_in, w1_high, w1_low, w2_high, w2_low = (sem("moe_" + n) for n in (
            "biases", "b1_ready", "x_in", "w1_in", "w2_in", "w1_high", "w1_low", "w2_high", "w2_low"))
        turned, x_high, x_low, hidden, relued, hid_high, hid_low, summed, saved, y_out, y_free = (sem("moe_" + n) for n in (
            "turned", "x_high", "x_low", "hidden", "relued", "hid_high", "hid_low", "summed", "saved", "y_out", "y_free"))
        ps = k.psum
        block = ctx.enter_context(nc.Block())

        def all_experts(eng, body):
            with eng.Fori(0, E_MOE - 1) as e:
                body(e, True)
            body(E_MOE - 1, False)

        @block.sync
        def _(sp):
            def load_w1(e):
                sp.dma_start(w1_raw[:, :, :], a["w1"][bass.ds(e * D, D), :].rearrange("(h p) f -> p h f", p=P)).then_inc(w1_in, 16)

            def load_w2(e):
                sp.dma_start(w2_raw[:, :, :], a["w2"][bass.ds(e * HID, HID), :].rearrange("(t p) d -> p t d", p=P)).then_inc(w2_in, 16)

            def load_x(e):
                sp.dma_start(xe[:, :, :], a["inbox"][bass.ds(e * CAP, CAP), :].rearrange("(s p) d -> p s d", p=P)).then_inc(x_in, 16)

            sp.dma_start(b1[:, :, :], a["b1_T"].rearrange("p (e t) -> p e t", t=HT)).then_inc(b_in, 16)
            sp.dma_start(b2[:, :, :].rearrange("p e d -> p (e d)"), a["b2"].rearrange("e d -> (e d)").partition_broadcast(P)).then_inc(b_in, 16)
            load_w1(0)
            load_w2(0)
            sp.wait_ge(k.scattered, 16 * K_MOE * NT)
            load_x(0)
            with sp.Fori(0, E_MOE - 1) as e:
                sp.wait_ge(turned, NQ * e + NQ)
                load_x(e + 1)
                sp.wait_ge(w1_low, e + 1)
                load_w1(e + 1)
                sp.wait_ge(w2_low, e + 1)
                load_w2(e + 1)

        @block.tensor
        def _(pe):
            def transposes(e, q):
                h, g = q // (ST // G), q % (ST // G)
                if q == 0:
                    pe.wait_ge(x_in, 16 * e + 16)
                pe.wait_ge(x_low, NQ * e + q + 1)
                for s in range(G):
                    last = pe.transpose(ps[:, q % 2, s * P:(s + 1) * P], xe[:, g * G + s, h * P:(h + 1) * P], k.ident[:, :])
                last.then_inc(turned, 1)

            def body(e, more):
                pe.wait_ge(x_low, NQ * e + NQ + 2)
                pe.wait_ge(w1_low, e + 1)
                for m in range(NM):
                    c, t = m // HT, m % HT
                    pe.wait_ge(hid_high, NM * e + m + 1)
                    for n, (wp, xp) in enumerate(SPLIT):
                        for h in range(DH):
                            last = pe.matmul(ps[:, 2 + m % 4, :], w1[:, wp, h, t * P:(t + 1) * P], xeT[:, xp, h, c * CH:(c + 1) * CH],
                                             start=(n == 0 and h == 0), stop=(n == 2 and h == DH - 1))
                    last.then_inc(hidden, 1)
                pe.wait_ge(w2_low, e + 1)
                for u in range(NY):
                    if u in (0, NY // 2):
                        pe.wait_ge(hid_low, NM * e + (NM // 2 if u == 0 else NM) + 2)
                    pe.wait_ge(saved, NY * e + u + 1)
                    for s in (2 * u, 2 * u + 1):
                        for t in range(HT):
                            for n, (hp, wp) in enumerate(SPLIT):
                                last = pe.matmul(ps[:, 6 + u % 2, (s % 2) * D:(s % 2 + 1) * D], hT[:, hp, t, s * P:(s + 1) * P],
                                                 w2[:, wp, t, :], start=(t == 0 and n == 0), stop=(t == HT - 1 and n == 2))
                    last.then_inc(summed, 1)
                    if more:
                        transposes(e + 1, u)

            for q in range(NQ):
                transposes(0, q)
            all_experts(pe, body)

        @block.scalar
        def _(act):
            act.sem_inc(hid_high, 4)

            def split_w1(e):
                act.wait_ge(w1_in, 16 * e + 16)
                act.activation(w1[:, HIGH, :, :], w1_raw[:, :, :], ACT.Copy).then_inc(w1_high, 1)

            def split_x(e, q):
                h, g = q // (ST // G), q % (ST // G)
                act.wait_ge(turned, NQ * e + q + 1)
                act.activation(xeT[:, HIGH, h, g * CH:(g + 1) * CH], ps[:, q % 2, :], ACT.Copy).then_inc(x_high, 1)

            def body(e, more):
                act.wait_ge(b1_ready, e + 1)
                for m in range(NM):
                    c, t = m // HT, m % HT
                    act.wait_ge(hidden, NM * e + m + 1)
                    act.wait_ge(hid_low, NM * e + m + 1)
                    act.activation(hid[:, m % 2, :], ps[:, 2 + m % 4, :], ACT.Relu, bias=b1e[:, t:t + 1]).then_inc(relued, 1)
                    act.activation(hT[:, HIGH, t, c * CH:(c + 1) * CH], ps[:, 2 + m % 4, :], ACT.Relu, bias=b1e[:, t:t + 1]).then_inc(hid_high, 1)
                    if m == 1:
                        act.wait_ge(w2_in, 16 * e + 16)
                        act.activation(w2[:, HIGH, :, :], w2_raw[:, :, :], ACT.Copy).then_inc(w2_high, 1)
                if more:
                    split_w1(e + 1)
                    for q in range(NQ):
                        split_x(e + 1, q)

            split_w1(0)
            for q in range(NQ):
                split_x(0, q)
            all_experts(act, body)

        @block.vector
        def _(dve):
            dve.sem_inc(x_low, 2)
            dve.sem_inc(hid_low, 2)
            dve.sem_inc(saved, 2)
            dve.wait_ge(b_in, 32)

            def biases(e):
                dve.tensor_copy(b1e[:, :], b1[:, bass.ds(e, 1), :].rearrange("p o t -> p (o t)")).then_inc(b1_ready, 1)

            def split_x(e, q):
                h, g = q // (ST // G), q % (ST // G)
                dve.wait_ge(x_high, NQ * e + q + 1)
                dve.tensor_tensor(xeT[:, LOW, h, g * CH:(g + 1) * CH], ps[:, q % 2, :],
                                  xeT[:, HIGH, h, g * CH:(g + 1) * CH].bitcast(F32), ALU.subtract).then_inc(x_low, 1)

            def body(e, more):
                for m in range(NM):
                    c, t = m // HT, m % HT
                    dve.wait_ge(relued, NM * e + m + 1)
                    dve.wait_ge(hid_high, NM * e + m + 1 + 4)
                    dve.tensor_tensor(hT[:, LOW, t, c * CH:(c + 1) * CH], hid[:, m % 2, :],
                                      hT[:, HIGH, t, c * CH:(c + 1) * CH].bitcast(F32), ALU.subtract).then_inc(hid_low, 1)
                if more:
                    biases(e + 1)
                dve.wait_ge(y_free, e + 1)
                for u in range(NY):
                    dve.wait_ge(summed, NY * e + u + 1)
                    dve.tensor_tensor(ye[:, 2 * u:2 * u + 2, :], ps[:, 6 + u % 2, :].rearrange("p (s d) -> p s d", s=2),
                                      b2[:, bass.ds(e, 1), :].to_broadcast([P, 2, D]), ALU.add).then_inc(saved, 1)
                    if more:
                        split_x(e + 1, u)

            biases(0)
            for q in range(NQ):
                split_x(0, q)
            all_experts(dve, body)

        @block.gpsimd
        def _(pool):
            pool.sem_inc(y_free, 1)
            pool.wait_ge(k.inbox_zeroed, 16 * 8)
            for c in range(K_MOE):
                for n in range(NT):
                    pool.indirect_dma_start(out=a["inbox"], out_offset=bass.IndirectOffsetOnAxis(ap=k.put[:, c, n:n + 1], axis=0),
                                            in_=k.stream[:, n, :], in_offset=None,
                                            bounds_check=SLOTS - 1, oob_is_err=False).then_inc(k.scattered, 16)

            def split_w1(e):
                pool.wait_ge(w1_high, e + 1)
                pool.tensor_tensor(w1[:, LOW, :, :], w1_raw[:, :, :], w1[:, HIGH, :, :].bitcast(F32), ALU.subtract).then_inc(w1_low, 1)

            def body(e, more):
                pool.wait_ge(w2_high, e + 1)
                pool.tensor_tensor(w2[:, LOW, :, :], w2_raw[:, :, :], w2[:, HIGH, :, :].bitcast(F32), ALU.subtract).then_inc(w2_low, 1)
                if more:
                    split_w1(e + 1)
                pool.wait_ge(saved, NY * e + NY + 2)
                pool.dma_start(a["outbox"][bass.ds(e * CAP, CAP), :].rearrange("(s p) d -> p s d", p=P), ye[:, :, :]).then_inc(y_out, 16)
                pool.wait_ge(y_out, 16 * e + 16)
                pool.sem_inc(y_free, 1)

            split_w1(0)
            all_experts(pool, body)


def combine(nc, k, a, xT):
    R = 8
    PAIRS_LN = LNG // 2
    norm = Norm(k)
    with ExitStack() as ctx:
        sb, sem = k.sbuf(ctx), k.stage_sem
        got = sb("got", [P, R, K_MOE, D])
        fetched = [sem(f"fetched{r}") for r in range(R)]
        first, added, turned, high, low = (sem("combine_" + n) for n in ("first", "added", "turned", "high", "low"))
        ps = k.psum

        def columns(part, i):
            return xT[:, part, :, i * 2 * P:(i + 1) * 2 * P].rearrange("c h (p j) -> c h j p", j=2)

        def banks(i, h):
            return ps[:, 4 + i % 4, h * 2 * P:(h + 1) * 2 * P].rearrange("c (j p) -> c j p", j=2)

        fold = fold_weights(k, a, ctx)
        block = ctx.enter_context(nc.Block())

        @block.sync
        def _(sp):
            fold["sync"](sp)

        @block.gpsimd
        def _(pool):
            pool.wait_ge(k.take_ready, 1)
            for n in range(NT):
                if n >= R:
                    pool.wait_ge(added, n - R + 1)
                for c in range(K_MOE):
                    pool.indirect_dma_start(out=got[:, n % R, c, :], out_offset=None, in_=a["outbox"],
                                            in_offset=bass.IndirectOffsetOnAxis(ap=k.take[:, c, n:n + 1], axis=0),
                                            bounds_check=SLOTS - 1, oob_is_err=True).then_inc(fetched[n % R], 16)

        @block.tensor
        def _(pe):
            fold["tensor"](pe)
            for i in range(NPAIR):
                norm.wait(pe, i // PAIRS_LN)
                if i >= 4:
                    pe.wait_ge(low, i - 3)
                for h in range(DH):
                    for j in range(2):
                        at = (h * 2 + j) * P
                        last = pe.transpose(ps[:, 4 + i % 4, at:at + P], k.stream[:, 2 * i + j, h * P:(h + 1) * P], k.ident[:, :])
                last.then_inc(turned, 1)

        @block.scalar
        def _(act):
            def turn(g):
                for i in range(g * PAIRS_LN, (g + 1) * PAIRS_LN):
                    act.wait_ge(turned, i + 1)
                    for h in range(DH):
                        last = act.activation(columns(HIGH, i)[:, h], banks(i, h), ACT.Copy)
                    last.then_inc(high, 1)

            for g in range(NG_LN):
                norm.root(act, g)
                if g >= 1:
                    turn(g - 1)
                if g == 3:
                    fold["scalar"](act)
            turn(NG_LN - 1)

        @block.vector
        def _(dve):
            fold["zeros"](dve)

            def turn(g):
                for i in range(g * PAIRS_LN, (g + 1) * PAIRS_LN):
                    dve.wait_ge(high, i + 1)
                    for h in range(DH):
                        last = dve.tensor_tensor(columns(LOW, i)[:, h], banks(i, h), columns(HIGH, i)[:, h].bitcast(F32), ALU.subtract)
                    last.then_inc(low, 1)

            for n in range(NT):
                if n == 4 * LNG:
                    fold["vector"](dve)
                if n == 5 * LNG:
                    fold["lows"](dve)
                dve.wait_ge(fetched[n % R], 32 * (n // R + 1))
                dve.scalar_tensor_tensor(k.stream[:, n, :], got[:, n % R, 0, :], k.gate[:, 0, n:n + 1], k.stream[:, n, :],
                                         ALU.mult, ALU.add).then_inc(first, 1)
                dve.wait_ge(first, n + 1)
                dve.scalar_tensor_tensor(k.stream[:, n, :], got[:, n % R, 1, :], k.gate[:, 1, n:n + 1], k.stream[:, n, :],
                                         ALU.mult, ALU.add).then_inc(added, 1)
                if (n + 1) % LNG == 0:
                    g = n // LNG
                    dve.wait_ge(added, n + 1)
                    norm.stats(dve, g)
                    if g >= 1:
                        norm.apply(dve, g - 1)
                    if g >= 2:
                        turn(g - 2)
            norm.apply(dve, NG_LN - 1)
            turn(NG_LN - 2)
            turn(NG_LN - 1)


NH = 16
HD = D // NH
HE = HD // 2
LAT = 64
NCH = T // CH
QT = CH // P
NSPLIT = 3
PAIRS = [(0, 0), (0, 1), (0, 2), (1, 0), (1, 1), (2, 0)]
KROWS = len(PAIRS) * HD
MASKED = -1e30


def fold_weights(k, a, ctx):
    sb, sem = k.sbuf(ctx), k.stage_sem
    down = sb("down_sb", [P, 3, NH // 2, D])
    up = sb("up_sb", [P, 3, 2, HD])
    full = sb("fold_f32", [P, 3, DH, D])
    rot = sb("rot_f32", [P, 2, DH, P])
    zeroed, down_in, up_in, folded, copied, turned, high = (sem("fold_" + n) for n in (
        "zeroed", "down_in", "up_in", "folded", "copied", "turned", "high"))
    low = sem("fold_low")

    def sync(sp):
        for w, src in enumerate((a["wq_down_T"], a["wk_down_T"], a["wv_down_T"])):
            sp.dma_start(down[:, w, :, :], src.rearrange("(m p) c -> p m c", p=P)).then_inc(down_in, 16)
        sp.wait_ge(zeroed, 1)
        for g in range(2):
            rows = slice(g * LAT, (g + 1) * LAT)
            for w, (c, e) in enumerate(((a["wq_up_c"], a["wq_up_e"]), (a["wk_up_c"], a["wk_up_e"]))):
                sp.dma_start(up[rows, w, g, 0:HE], c).then_inc(up_in, 16)
                sp.dma_start(up[rows, w, g, HE:HD], e).then_inc(up_in, 16)
            sp.dma_start(up[rows, 2, g, :], a["wv_up"]).then_inc(up_in, 16)

    def tensor(pe):
        pe.wait_ge(down_in, 48)
        pe.wait_ge(up_in, 160)
        for w in range(3):
            for m in range(NH // 2):
                for c in range(DH):
                    at = c * D + m * 2 * HD
                    last = pe.matmul(k.psum[:, w, at:at + 2 * HD], down[:, w, m, c * P:(c + 1) * P],
                                     up[:, w, :, :].rearrange("p g d -> p (g d)"), start=True, stop=True)
        last.then_inc(folded, 1)

    def zeros(dve):
        dve.memset(up[:, :, :, :], 0.0).then_inc(zeroed, 1)

    def vector(dve):
        dve.wait_ge(folded, 1)
        for w in range(2):
            for c in range(DH):
                dve.tensor_copy(full[:, w, c, :].rearrange("p (r h d) -> p r h d", r=2, h=NH),
                                k.psum[:, w, c * D:(c + 1) * D].rearrange("p (h r d) -> p r h d", h=NH, r=2))
        dve.tensor_copy(full[:, 2, :, :], k.psum[:, 2, :].rearrange("p (c n) -> p c n", c=DH)).then_inc(copied, 1)
        dve.wait_ge(copied, 1)
        for w in range(2):
            for c in range(DH):
                src = full[:, w, c, P:].rearrange("p (i j) -> p i j", j=2)
                dst = rot[:, w, c, :].rearrange("p (i j) -> p i j", j=2)
                dve.tensor_scalar(dst[:, :, 0], src[:, :, 1], -1.0, None, ALU.mult)
                last = dve.tensor_copy(dst[:, :, 1], src[:, :, 0])
        last.then_inc(turned, 1)

    def lows(dve):
        dve.wait_ge(high, 2)
        dve.tensor_tensor(k.wfold[:, LOW, :, :, :], full[:, :, :, :], k.wfold[:, HIGH, :, :, :].bitcast(F32), ALU.subtract).then_inc(low, 1)
        dve.tensor_tensor(k.wrot[:, LOW, :, :, :], rot[:, :, :, :], k.wrot[:, HIGH, :, :, :].bitcast(F32), ALU.subtract).then_inc(low, 1)

    def scalar(act):
        act.wait_ge(copied, 1)
        act.activation(k.wfold[:, HIGH, :, :, :], full[:, :, :, :], ACT.Copy).then_inc(high, 1)
        act.wait_ge(turned, 1)
        act.activation(k.wrot[:, HIGH, :, :, :], rot[:, :, :, :], ACT.Copy).then_inc(high, 1)

    return {"sync": sync, "tensor": tensor, "zeros": zeros, "vector": vector, "lows": lows, "scalar": scalar}


def project_qkv(nc, k, a, xT):
    NU = NCH * 2
    PLAIN, ROT = 0, 1
    with ExitStack() as ctx:
        sb, sem = k.sbuf(ctx), k.stage_sem
        cos = sb("cos_sb", [P, 2, CH])
        sin = sb("sin_sb", [P, 2, CH])
        rest = sb("qk_rest", [P, 2, 2, CH])
        t2 = sb("rope_t2", [P, 2, CH])
        parts = sb("qk_split", [P, 2, 2, NSPLIT, CH], BF16)
        t_in = [sem(f"rope_in{b}") for b in (0, 1)]
        t1_ready, t2_ready, rotated, v_done, v_copied = (sem("qkv_" + n) for n in (
            "t1", "t2", "rotated", "v", "v_copied"))
        projected, p1, r1, p2, p3 = ([sem(f"qkv_{n}{r}") for r in (PLAIN, ROT)] for n in ("projected", "p1", "r1", "p2", "p3"))
        stored = [[sem(f"qkv_stored{r}{b}") for b in (0, 1)] for r in (PLAIN, ROT)]
        ps = k.psum
        block = ctx.enter_context(nc.Block())

        def bank(m, r, rot=0):
            return m % 2 if r == PLAIN else 2 + 2 * (m % 2) + rot

        @block.sync
        def _(sp):
            def store(m):
                c, w = m // 2, m % 2
                for r in (PLAIN, ROT):
                    sp.wait_ge(p3[r], m + 1)
                    sp.dma_start(a["qk_parts"][w, :, r * P:(r + 1) * P, c * CH:(c + 1) * CH].rearrange("s p t -> p s t"),
                                 parts[:, r, m % 2, :, :]).then_inc(stored[r][m % 2], 16)

            for c in range(NCH):
                if c >= 2:
                    sp.wait_ge(t2_ready, 2 * (c - 1))
                for dst, src in ((cos, a["cos_T"]), (sin, a["sin_T"])):
                    sp.dma_start(dst[:, c % 2, :], src[:, c * CH:(c + 1) * CH]).then_inc(t_in[c % 2], 16)
                if c >= 1:
                    store(2 * c - 2)
                    store(2 * c - 1)
            store(NU - 2)
            store(NU - 1)
            for r in (PLAIN, ROT):
                for b in (0, 1):
                    sp.wait_ge(stored[r][b], 16 * NU // 2)

        @block.tensor
        def _(pe):
            def project(out, weights, column, w, cols):
                for n, (wp, xp) in enumerate(SPLIT):
                    for h in range(DH):
                        last = pe.matmul(out, weights[:, wp, w, h, column:column + P], xT[:, xp, h, cols],
                                         start=(n == 0 and h == 0), stop=(n == 2 and h == DH - 1))
                return last

            for c in range(NCH):
                cols = slice(c * CH, (c + 1) * CH)
                for w in range(2):
                    m = 2 * c + w
                    if m >= 2:
                        pe.wait_ge(r1[PLAIN], m - 1)
                    project(ps[:, bank(m, PLAIN), :], k.wfold, 0, w, cols).then_inc(projected[PLAIN], 1)
                    if m >= 2:
                        pe.wait_ge(t2_ready, m - 1)
                    project(ps[:, bank(m, ROT), :], k.wfold, P, w, cols)
                    project(ps[:, bank(m, ROT, 1), :], k.wrot, 0, w, cols).then_inc(projected[ROT], 1)
                    for n in range(m * QT // 2, (m + 1) * QT // 2):
                        if n >= 2:
                            pe.wait_ge(v_copied, n - 1)
                        for i, (wp, xp) in enumerate(SPLIT):
                            for h in range(DH):
                                last = pe.matmul(ps[:, 6 + n % 2, 0:D], xT[:, xp, h, n * P:(n + 1) * P], k.wfold[:, wp, 2, h, :],
                                                 start=(i == 0 and h == 0), stop=(i == 2 and h == DH - 1))
                        last.then_inc(v_done, 1)

        @block.vector
        def _(dve):
            def first_rest(m, r):
                dve.wait_ge(p1[r], m + 1)
                value = ps[:, bank(m, PLAIN), :] if r == PLAIN else rest[:, r, m % 2, :]
                dve.tensor_tensor(rest[:, r, m % 2, :], value, parts[:, r, m % 2, 0, :], ALU.subtract).then_inc(r1[r], 1)

            def third(m, r):
                dve.wait_ge(p2[r], m + 1)
                dve.tensor_tensor(parts[:, r, m % 2, 2, :], rest[:, r, m % 2, :], parts[:, r, m % 2, 1, :], ALU.subtract).then_inc(p3[r], 1)

            for m in range(NU):
                c = m // 2
                if m >= 1:
                    first_rest(m - 1, ROT)
                first_rest(m, PLAIN)
                if m % 2 == 0:
                    dve.wait_ge(t_in[c % 2], 16 * 2 * (c // 2 + 1))
                dve.wait_ge(projected[ROT], m + 1)
                dve.tensor_tensor(rest[:, ROT, m % 2, :], ps[:, bank(m, ROT), :], cos[:, c % 2, :], ALU.mult).then_inc(t1_ready, 1)
                dve.tensor_tensor(t2[:, m % 2, :], ps[:, bank(m, ROT, 1), :], sin[:, c % 2, :], ALU.mult).then_inc(t2_ready, 1)
                if m >= 1:
                    third(m - 1, ROT)
                third(m, PLAIN)
                dve.wait_ge(t1_ready, m + 1)
                dve.wait_ge(t2_ready, m + 1)
                dve.tensor_tensor(rest[:, ROT, m % 2, :], rest[:, ROT, m % 2, :], t2[:, m % 2, :], ALU.add).then_inc(rotated, 1)
            first_rest(NU - 1, ROT)
            third(NU - 1, ROT)

        @block.scalar
        def _(act):
            def first_part(m, r):
                act.wait_ge(projected[PLAIN] if r == PLAIN else rotated, m + 1)
                if m >= 2:
                    act.wait_ge(stored[r][m % 2], 16 * (m // 2))
                value = ps[:, bank(m, PLAIN), :] if r == PLAIN else rest[:, r, m % 2, :]
                act.activation(parts[:, r, m % 2, 0, :], value, ACT.Copy).then_inc(p1[r], 1)

            def second_part(m, r):
                act.wait_ge(r1[r], m + 1)
                act.activation(parts[:, r, m % 2, 1, :], rest[:, r, m % 2, :], ACT.Copy).then_inc(p2[r], 1)

            for m in range(NU):
                first_part(m, PLAIN)
                if m >= 1:
                    second_part(m - 1, ROT)
                second_part(m, PLAIN)
                first_part(m, ROT)
                for n in range(m * QT // 2, (m + 1) * QT // 2):
                    act.wait_ge(v_done, n + 1)
                    act.activation(k.v[:, n, :], ps[:, 6 + n % 2, 0:D], ACT.Copy).then_inc(v_copied, 1)
            second_part(NU - 1, ROT)


BUFS = 3
RING_P = 8


def attention_groups():
    units = [(qc, kt) for qc in range(NCH) for kt in range(QT * (qc + 1))]
    rows = [(i, m) for i in range(NT) for m in range(i // QT + 1)]
    groups = [(i, g) for i in range(NT) for g in range(i // QT // 2 + 1)]
    closes = {rows.index((i, min(2 * g + 1, i // QT))): n for n, (i, g) in enumerate(groups)}
    return units, rows, groups, closes


def attention_plan(this_head, next_head, previous=False, carry=False):
    units, rows, groups, closes = attention_groups()
    SEEN, SOON = 190, 200
    AV_COST, FOLD_COST, TURN_COST = 930, 240, 60
    cost_pe = lambda columns, diag: 0.42 * columns + (56 if diag else 0)
    pe, dve, act = 0, 1500 if previous else 0, 700 if previous else 0
    st, av, s = 0, -1 if previous else 0, 0
    last_av = len(units) // 4 - (1 if carry else 0)
    exped, used, maxed = {-2: 0, -1: act}, {}, {}
    copied, normed = ({}, {-2: 0}) if previous else ({-1: 0}, {-1: 0})
    reached = {}
    to_fold, folds, turned = [], 0, False
    waiting = []
    order_pe, order_dve = [], []
    log = {"MAX": maxed, "OCOPY": copied, "NORM": normed}

    def give(ready, kind, x, cost):
        waiting.append((ready, len(order_pe) + len(waiting), (kind, x), cost))

    while True:
        while waiting:
            waiting.sort()
            ready, _, (kind, x), cost = waiting[0]
            if max(ready, dve) >= pe:
                break
            waiting.pop(0)
            dve = max(ready, dve) + cost
            order_dve.append((kind, x))
            log.get(kind, reached)[x if kind in log else kind] = dve
        can = []
        left_dve = dve + sum(w[3] for w in waiting)
        if this_head:
            if st < len(units) and 4 * av > st - RING_P:
                can.append((max(pe, exped[st - 2] + SEEN), act - 400, "ST", st))
            if 4 * av + 3 < st and av < last_av:
                qc, kt = units[4 * av]
                closing = units[4 * av + 3][1] == QT * qc + QT - 1
                if (kt > 0 or qc - 1 in copied) and not (closing and len(to_fold) == 2):
                    can.append((max(pe, exped[4 * av + 3] + SEEN, copied[qc - 1] + SEEN if kt == 0 else 0),
                                pe + 1500 - 100 * (st - 4 * av), "AV", av))
            if to_fold and to_fold[0] in copied and to_fold[0] - 1 in normed and turned == ("MCOPY" in reached):
                can.append((max(pe, copied[to_fold[0]] + SEEN), pe + 1000, "FOLD", to_fold[0]))
        if next_head:
            done = len([1 for c in closes if c < s])
            if s < len(rows) and (done < 2 or done - 2 in maxed):
                can.append((max(pe, maxed[done - 2] + SEEN if done >= 2 else 0), left_dve - 800, "S", s))
            if "MFIN" in reached and not turned and folds == len(normed) - 1:
                can.append((max(pe, reached["MFIN"] + SEEN), 0, "MTURN", 0))
        if not can and not waiting:
            return order_pe, order_dve
        if not can:
            pe = max(pe, waiting[0][0], dve) + 1
            continue
        soonest = min(c[0] for c in can)
        start, _, kind, x = min((c for c in can if c[0] <= soonest + SOON), key=lambda c: c[1])
        if kind == "ST":
            qc, kt = units[x]
            columns = CH - max(0, kt - QT * qc) * P
            pe = start + cost_pe(columns, kt >= QT * qc)
            act = max(act, pe + SEEN, used.get(x - RING_P, 0) + SEEN) + 51 + columns / 1.2
            exped[x] = act
            st += 1
        elif kind == "AV":
            pe = start + AV_COST
            used.update({u: pe for u in range(4 * x, 4 * x + 4)})
            av += 1
            qc, kt = units[4 * x + 3]
            if kt == QT * qc + QT - 1:
                to_fold.append(qc if x >= 0 else -1)
                give(pe + SEEN, "OCOPY", to_fold[-1], 595)
        elif kind == "FOLD":
            pe = start + FOLD_COST
            to_fold.pop(0)
            folds += 1
            give(pe + SEEN, "NORM", x, 700)
        elif kind == "S":
            pe = start
            while True:
                i, m = rows[s]
                pe += cost_pe(min(CH, (i + 1) * P - m * CH), m == i // QT)
                order_pe.append((kind, s))
                s += 1
                if s - 1 in closes:
                    break
            g = closes[s - 1]
            give(pe + SEEN, "MAX", g, (60 + min(2 * CH, (i + 1) * P - groups[g][1] * 2 * CH)) / 0.96)
            if s == len(rows):
                give(pe + SEEN, "MFIN", 0, 1300)
        else:
            turned = True
            pe = start + TURN_COST
            give(pe + SEEN, "MCOPY", 0, 200)
        if kind != "S":
            order_pe.append((kind, x))


def attention(nc, k, a):
    units, rows, groups, closes = attention_groups()
    NU, NG = len(units), len(groups)
    lead_pe, lead_dve = attention_plan(False, True)
    first_plan = attention_plan(True, True, carry=True)
    body_plan = attention_plan(True, True, previous=True, carry=True)
    last_plan = attention_plan(True, False, previous=True)
    NEXT = ("S", "MAX", "MFIN", "MTURN", "MCOPY")
    with ExitStack() as ctx:
        sb, sem = k.sbuf(ctx), k.stage_sem
        q6 = sb("q_rows", [P, BUFS, T], BF16)
        k6 = sb("k_rows", [P, BUFS, T], BF16)
        vh = sb("v_head", [P, BUFS, NT, 32])
        pt = sb("probs_T", [P, RING_P, CH])
        oacc = sb("o_acc", [P, 2, CH])
        mx = sb("row_max", [P, BUFS, NT, 4])
        m = sb("max_f", [P, 2, NT])
        nm = sb("neg_max", [P, NSPLIT, NT], BF16)
        mT = sb("neg_max_T", [NSPLIT * NT, P], BF16)
        rcp = sb("inv_sum", [P, 2, QT])
        identb = sb("ident_bf", [P, P], BF16)
        mask = sb("mask_q_k", [P, P], BF16)
        maskT = sb("mask_k_q", [P, P], BF16)
        fold = sb("fold", [P, 32])
        consts, s_done, st_done, exped, av_done, maxed, o_copied, folded, normed, v_ready = (sem("at_" + n) for n in (
            "consts", "s_done", "st_done", "exped", "av_done", "maxed", "o_copied", "folded", "normed", "v_ready"))
        m_step, m_split, m_turned, m_copied, inv_ready, cleared, masks = (sem("at_" + n) for n in (
            "m_step", "m_split", "m_turned", "m_copied", "inv_ready", "pt_cleared", "masks"))
        ones_ready, m_out = sem("at_ones"), sem("at_m_out")
        qk_in = [sem(f"at_qk_in{b}") for b in range(BUFS)]
        m_in = [sem(f"at_m_in{b}") for b in range(BUFS)]
        ps = k.psum
        psb = k.psum[:, 7, 256:512].bitcast(BF16)
        block = ctx.enter_context(nc.Block())

        def heads(eng, body):
            body(0, 0, 0, first_plan)
            with eng.Fori(0, NH // BUFS - 1) as i:
                for b in range(1, BUFS + 1):
                    body(BUFS * i + b, b % BUFS, i + b // BUFS, body_plan)
            for e in range(NH - BUFS, NH - 1):
                body(e, e % BUFS, e // BUFS, body_plan)
            body(NH - 1, (NH - 1) % BUFS, (NH - 1) // BUFS, last_plan)

        @block.sync
        def _(sp):
            def load(e, b):
                for (dst, w, side) in ((q6, 0, 0), (k6, 1, 1)):
                    for r, pair in enumerate(PAIRS):
                        sp.dma_start(dst[r * HD:(r + 1) * HD, b, :],
                                     a["qk_parts"][w, pair[side]].rearrange("(r x) t -> r x t", r=2)[:, bass.ds(e * HE, HE), :]).then_inc(qk_in[b], 16)

            def maxima(e, b):
                sp.wait_ge(m_copied, e + 1)
                sp.dma_start(a["max_rows"][b, :, :], mT[:, :]).then_inc(m_out, 16)
                sp.wait_ge(m_out, 16 * e + 16)
                sp.dma_start(q6[KROWS:KROWS + NSPLIT, b, :],
                             a["max_rows"][b, :, :].rearrange("(s i) p -> s (i p)", s=NSPLIT)).then_inc(m_in[b], 16)

            load(0, 0)
            load(1, 1)
            maxima(0, 0)

            def head(e, b, more=True):
                if more:
                    sp.wait_ge(st_done, NU * e + 1)
                    load(e + 2, (b + 2) % BUFS)
                maxima(e + 1, (b + 1) % BUFS)

            with sp.Fori(0, NH // BUFS - 1) as i:
                for b in range(BUFS):
                    head(BUFS * i + b, b)
            for e in range(NH - 1 - BUFS, NH - 1):
                head(e, e % BUFS, more=e + 2 < NH)

        @block.gpsimd
        def _(pool):
            pool.memset(identb[:, :], 0.0).then_inc(consts, 1)
            pool.memset(mask[:, :], 0.0).then_inc(consts, 1)
            pool.memset(maskT[:, :], 0.0).then_inc(consts, 1)
            pool.memset(fold[:, :], 0.0).then_inc(consts, 1)
            pool.memset(vh[:, :, :, HD + 1:], 0.0).then_inc(ones_ready, 1)
            pool.memset(vh[:, :, :, HD:HD + 1], 1.0).then_inc(ones_ready, 1)
            pool.wait_ge(consts, 4)
            pool.affine_select(out=identb[:, :], in_=identb[:, :], compare_op=ALU.not_equal, fill=1.0,
                               base=0, pattern=[[-1, P]], channel_multiplier=1).then_inc(masks, 1)
            pool.affine_select(out=mask[:, :], in_=mask[:, :], compare_op=ALU.is_ge, fill=MASKED,
                               base=0, pattern=[[-1, P]], channel_multiplier=1).then_inc(masks, 1)
            pool.affine_select(out=maskT[:, :], in_=maskT[:, :], compare_op=ALU.is_ge, fill=MASKED,
                               base=0, pattern=[[1, P]], channel_multiplier=-1).then_inc(masks, 1)
            for g in range(4):
                pool.wait_ge(masks, 3 + g)
                pool.affine_select(out=fold[:, :], in_=fold[:, :], compare_op=ALU.not_equal, fill=1.0,
                                   base=-32 * g, pattern=[[-1, 32]], channel_multiplier=1).then_inc(masks, 1)

        @block.tensor
        def _(pe):
            pe.sem_inc(st_done, 1)
            pe.sem_inc(av_done, RING_P)
            pe.sem_inc(folded, 2)
            pe.wait_ge(masks, 7)
            pe.wait_ge(ones_ready, 3)

            def s_unit(e, b, s):
                i, mm = rows[s]
                if s == 0 or (s - 1) in closes:
                    g = closes[min(c for c in closes if c >= s)]
                    pe.wait_ge(maxed, NG * e + g + 1)
                g = closes[min(c for c in closes if c >= s)]
                width = min(CH, (i + 1) * P - mm * CH)
                diag = mm == i // QT
                bank = 2 * (g % 2) + mm % 2
                ins = pe.matmul(ps[:, bank, 0:width], q6[0:KROWS, b, i * P:(i + 1) * P], k6[0:KROWS, b, mm * CH:mm * CH + width],
                                start=True, stop=not diag)
                if diag:
                    ins = pe.matmul(ps[:, bank, width - P:width], identb[:, :], mask[:, :], start=False, stop=True)
                if s in closes:
                    ins.then_inc(s_done, 1)

            def next_head(kind, x, e, b, loads, folds=0):
                if kind == "S":
                    if x == 0:
                        pe.wait_ge(qk_in[b], 16 * 2 * len(PAIRS) * loads)
                    s_unit(e, b, x)
                elif kind == "MTURN":
                    pe.wait_ge(m_split, e + 1)
                    if folds:
                        pe.wait_ge(normed, NCH * (e - 1) + folds + 1)
                    pe.transpose(psb[0:NSPLIT * NT, 0:P], nm[:, :, :].rearrange("p s i -> p (s i)"), identb[:, :]).then_inc(m_turned, 1)

            for kind, x in lead_pe:
                next_head(kind, x, 0, 0, 1)

            def body(e, b, i, plan):
                folds, turned = 0, False
                for kind, x in plan[0]:
                    if kind in NEXT:
                        next_head(kind, x, e + 1, (b + 1) % BUFS, i + 1 + (b + 1) // BUFS, folds)
                        turned = turned or kind == "MTURN"
                    elif kind == "ST":
                        if x == 0:
                            pe.wait_ge(m_in[b], 16 * i + 16)
                        qc, kt = units[x]
                        o = max(0, kt - QT * qc) * P
                        diag = kt >= QT * qc
                        pe.wait_ge(exped, NU * e + x + 1)
                        bank = 4 + x % 2
                        ins = pe.matmul(ps[:, bank, o:CH], k6[0:KROWS + NSPLIT, b, kt * P:(kt + 1) * P],
                                        q6[0:KROWS + NSPLIT, b, qc * CH + o:(qc + 1) * CH], start=True, stop=not diag)
                        if diag:
                            ins = pe.matmul(ps[:, bank, o:o + P], identb[:, :], maskT[:, :], start=False, stop=True)
                        ins.then_inc(st_done, 1)
                    elif kind == "AV":
                        qc = units[4 * x][0]
                        if units[4 * x][1] == 0:
                            pe.wait_ge(o_copied, NCH * e + qc + 1)
                        if x == 0:
                            pe.wait_ge(v_ready, e + 1)
                            pe.wait_ge(cleared, (QT - 1) * (e + 1))
                        pe.wait_ge(exped, NU * e + 4 * x + 4 + 2)
                        for u in range(4 * x, 4 * x + 4):
                            kt = units[u][1]
                            g = kt % 4
                            o = max(0, kt - QT * qc) * P if qc else 0
                            pe.matmul(ps[32 * g:32 * g + 32, 6, o:CH], vh[:, b if x >= 0 else (b - 1) % BUFS, kt, :], pt[:, u % RING_P, o:CH],
                                      start=(kt < 4), stop=(kt >= QT * qc)).then_inc(av_done, 1)
                    elif kind == "FOLD":
                        pe.wait_ge(normed, NCH * e + x + 1)
                        pe.wait_ge(o_copied, NCH * e + x + 1 + 1)
                        if turned:
                            pe.wait_ge(m_copied, e + 2)
                        folds = x + 1
                        for t in range(QT):
                            src = oacc[:, x % NCH % 2, (t // 2) * 2 * P:(t // 2 + 1) * 2 * P].rearrange("r (p j) -> r p j", j=2)[:, :, t % 2]
                            ins = pe.matmul(ps[:, 7, t * 32:t * 32 + 32], src, fold[:, :], start=True, stop=True)
                        ins.then_inc(folded, 1)

            heads(pe, body)

        @block.scalar
        def _(act):
            act.sem_inc(exped, 2)

            def body(e, b, i, plan):
                for kind, x in plan[0]:
                    if kind == "ST":
                        qc, kt = units[x]
                        o = max(0, kt - QT * qc) * P
                        act.wait_ge(st_done, NU * e + x + 1 + 1)
                        act.wait_ge(av_done, NU * e + x + 1)
                        act.activation(pt[:, x % RING_P, o:CH], ps[:, 4 + x % 2, o:CH], ACT.Exp, scale=HD ** -0.5).then_inc(exped, 1)

            heads(act, body)

        @block.vector
        def _(dve):
            dve.sem_inc(maxed, 2)
            dve.sem_inc(o_copied, 1)
            dve.sem_inc(normed, 1)
            dve.memset(k6[KROWS:KROWS + NSPLIT, :, :], 1.0).then_inc(ones_ready, 1)
            dve.memset(mx[:, :, :, :], 2 * MASKED).then_inc(m_step, 1)
            dve.wait_ge(m_step, 1)

            def take_v(e, b):
                dve.tensor_scalar(vh[:, b, :, 0:HD], k.v[:, :, bass.ds(e * HD, HD)], 1.0, None, ALU.mult).then_inc(v_ready, 1)

            def next_head(kind, x, e, b):
                if kind == "MAX":
                    i, g = groups[x]
                    width = min(2 * CH, (i + 1) * P - g * 2 * CH)
                    dve.wait_ge(s_done, NG * e + x + 1)
                    src = ps[:, 2 * (x % 2):2 * (x % 2) + 2, :].rearrange("p b c -> p (b c)")[:, 0:width]
                    dve.tensor_reduce(mx[:, b, i, g:g + 1], src, AX.X, ALU.max).then_inc(maxed, 1)
                elif kind == "MFIN":
                    base = 5 * e + 1
                    dve.wait_ge(maxed, NG * e + NG + 2)
                    dve.tensor_reduce(m[:, 0, :], mx[:, b, :, :], AX.X, ALU.max).then_inc(m_step, 1)
                    dve.wait_ge(m_step, base + 1)
                    dve.tensor_scalar(nm[:, 0, :], m[:, 0, :], -1.0, None, ALU.mult).then_inc(m_step, 1)
                    dve.wait_ge(m_step, base + 2)
                    dve.scalar_tensor_tensor(m[:, 1, :], m[:, 0, :], -1.0, nm[:, 0, :], ALU.mult, ALU.subtract).then_inc(m_step, 1)
                    dve.wait_ge(m_step, base + 3)
                    dve.tensor_copy(nm[:, 1, :], m[:, 1, :]).then_inc(m_step, 1)
                    dve.wait_ge(m_step, base + 4)
                    dve.tensor_tensor(nm[:, 2, :], m[:, 1, :], nm[:, 1, :], ALU.subtract).then_inc(m_step, 1)
                    dve.wait_ge(m_step, base + 5)
                    dve.sem_inc(m_split, 1)
                elif kind == "MCOPY":
                    dve.wait_ge(m_turned, e + 1)
                    dve.tensor_copy(mT[:, :], psb[0:NSPLIT * NT, 0:P]).then_inc(m_copied, 1)

            dve.wait_ge(ones_ready, 3)
            take_v(0, 0)
            for kind, x in lead_dve:
                next_head(kind, x, 0, 0)

            def body(e, b, i, plan):
                dve.wait_ge(av_done, NU * e - 4 + RING_P)
                for u in range(1, QT):
                    dve.memset(pt[:, u % RING_P, 0:u * P], 0.0).then_inc(cleared, 1)
                if plan is not last_plan:
                    take_v(e + 1, (b + 1) % BUFS)
                for kind, x in plan[1]:
                    if kind in NEXT:
                        next_head(kind, x, e + 1, (b + 1) % BUFS)
                    elif kind == "OCOPY":
                        dve.wait_ge(folded, NCH * e + x + 1)
                        dve.wait_ge(av_done, NU * e + 4 * sum(1 for q in range(0, x + 1) for _ in range(q + 1)) + RING_P)
                        dve.tensor_copy(oacc[:, x % NCH % 2, :], ps[:, 6, :]).then_inc(o_copied, 1)
                    elif kind == "NORM":
                        qc, head = (x, e) if x >= 0 else (NCH - 1, e - 1)
                        sums = ps[:, 7, 0:QT * 32].rearrange("p (t d) -> p t d", d=32)
                        dve.wait_ge(folded, NCH * e + x + 1 + 2)
                        dve.reciprocal(rcp[:, qc % 2, :], sums[:, :, HD]).then_inc(inv_ready, 1)
                        dve.wait_ge(inv_ready, NCH * e + x + 1)
                        dve.tensor_tensor(k.attn[:, QT * qc:QT * qc + QT, bass.ds(head * HD, HD)], sums[:, :, 0:HD],
                                          rcp[:, qc % 2, :].unsqueeze(2).to_broadcast([P, QT, HD]), ALU.mult).then_inc(normed, 1)

            heads(dve, body)


def project_attention(nc, k, a, xT):
    norm = Norm(k)
    PAIRS_LN = LNG // 2
    with ExitStack() as ctx:
        sb, sem = k.sbuf(ctx), k.stage_sem
        wc = sb("wc_sb", [P, DH, D])
        aT = sb("attn_T", [P, 2, D])
        loaded, turned, copied, projected, added = (sem("pa_" + n) for n in ("loaded", "turned", "copied", "projected", "added"))
        x_turned, high, low = (sem("x3_" + n) for n in ("turned", "high", "low"))
        ps = k.psum
        block = ctx.enter_context(nc.Block())

        @block.sync
        def _(sp):
            sp.dma_start(wc[:, :, :], a["wc"].rearrange("(h p) e -> p h e", p=P)).then_inc(loaded, 16)

        @block.tensor
        def _(pe):
            def turn(g):
                norm.wait(pe, g)
                for i in range(g * PAIRS_LN, (g + 1) * PAIRS_LN):
                    if i >= 2:
                        pe.wait_ge(low, i - 1)
                    for h in range(DH):
                        for j in range(2):
                            at = (h * 2 + j) * P
                            last = pe.transpose(ps[:, 2 + i % 2, at:at + P], k.stream[:, 2 * i + j, h * P:(h + 1) * P], k.ident[:, :])
                    last.then_inc(x_turned, 1)

            pe.wait_ge(loaded, 16)
            for n in range(NT + 1):
                if n < NT:
                    if n >= 2:
                        pe.wait_ge(copied, n - 1)
                    for h in range(DH):
                        last = pe.transpose(ps[:, n % 2, h * P:(h + 1) * P], k.attn[:, n, h * P:(h + 1) * P], k.ident[:, :])
                    last.then_inc(turned, 1)
                if n > 0:
                    m = n - 1
                    pe.wait_ge(copied, m + 1)
                    if m >= 4:
                        pe.wait_ge(added, m - 3)
                    for h in range(DH):
                        last = pe.matmul(ps[:, 4 + m % 4, 0:D], aT[:, m % 2, h * P:(h + 1) * P], wc[:, h, :],
                                         start=(h == 0), stop=(h == DH - 1))
                    last.then_inc(projected, 1)
                if n % LNG == 2 and n // LNG >= 2:
                    turn(n // LNG - 2)
            turn(NG_LN - 2)
            turn(NG_LN - 1)

        @block.scalar
        def _(act):
            def turn(g):
                for i in range(g * PAIRS_LN, (g + 1) * PAIRS_LN):
                    act.wait_ge(x_turned, i + 1)
                    act.activation(xT[:, HIGH, :, i * 2 * P:(i + 1) * 2 * P],
                                   ps[:, 2 + i % 2, :].rearrange("c (h t) -> c h t", h=DH), ACT.Copy).then_inc(high, 1)

            for n in range(NT):
                act.wait_ge(turned, n + 1)
                if n >= 2:
                    act.wait_ge(projected, n - 1)
                act.activation(aT[:, n % 2, :], ps[:, n % 2, 0:D], ACT.Copy).then_inc(copied, 1)
                if n % LNG == 2 and n // LNG >= 1:
                    norm.root(act, n // LNG - 1)
                if n % LNG == 3 and n // LNG >= 2:
                    turn(n // LNG - 2)
            norm.root(act, NG_LN - 1)
            turn(NG_LN - 2)
            turn(NG_LN - 1)

        @block.vector
        def _(dve):
            def turn(g):
                for i in range(g * PAIRS_LN, (g + 1) * PAIRS_LN):
                    dve.wait_ge(high, i + 1)
                    cols = slice(i * 2 * P, (i + 1) * 2 * P)
                    dve.tensor_tensor(xT[:, LOW, :, cols], ps[:, 2 + i % 2, :].rearrange("c (h t) -> c h t", h=DH),
                                      xT[:, HIGH, :, cols].bitcast(F32), ALU.subtract).then_inc(low, 1)

            for n in range(NT):
                dve.wait_ge(projected, n + 1)
                dve.tensor_tensor(k.stream[:, n, :], k.stream[:, n, :], ps[:, 4 + n % 4, 0:D], ALU.add).then_inc(added, 1)
                if n % LNG == LNG - 1:
                    g = n // LNG
                    dve.wait_ge(added, n + 1)
                    norm.stats(dve, g)
                if n % LNG == 2 and n // LNG >= 1:
                    norm.apply(dve, n // LNG - 1)
                if n % LNG == 3 and n // LNG >= 2:
                    turn(n // LNG - 2)
            norm.apply(dve, NG_LN - 1)
            turn(NG_LN - 2)
            turn(NG_LN - 1)


NE = 16
NEX = NE + 1
TOPK = 4
INTER = 128
ROUTE_SCALE = 2.5


def weigh_experts(nc, k, a, xT):
    with ExitStack() as ctx:
        sb, sem = k.sbuf(ctx), k.stage_sem
        wg = sb("gate_w_sb", [P, DH, NE])
        wg_part = sb("gate_w_part", [P, 2, DH, NE], F32R)
        logits_T = sb("logits_T", [NE, T])
        w_split, l_chunk, l_copied = sem("we_w_split"), sem("we_chunk"), sem("we_copied")
        gb = sb("gate_b_sb", [P, NE])
        scores = sb("scores", [P, NT, NE])
        biased = sb("biased", [P, NT, NE])
        top = sb("top_b", [P, NT, 8])
        top_i = sb("top_bi", [P, NT, 8], U32)
        choice = sb("choice_b", [P, NT, TOPK])
        hit = sb("hit", [P, NT, NE])
        mask = sb("mask_b", [P, NT, NE])
        total = sb("total_b", [P, NT])
        loaded, logits, scored, step = (sem("we_" + n) for n in ("loaded", "logits", "scored", "step"))
        ps = k.psum
        block = ctx.enter_context(nc.Block())

        @block.sync
        def _(sp):
            sp.dma_start(wg[:, :, :], a["gate_w_T"].rearrange("(h p) e -> p h e", p=P)).then_inc(loaded, 16)
            sp.dma_start(gb[:, :], a["gate_b"].partition_broadcast(P)).then_inc(loaded, 16)

        @block.tensor
        def _(pe):
            pe.wait_ge(w_split, 2)
            for c in range(NCH):
                if c >= 4:
                    pe.wait_ge(l_copied, c - 3)
                for n, (wp, xp) in enumerate(SPLIT):
                    for h in range(DH):
                        last = pe.matmul(ps[0:NE, c % 4, :], wg_part[:, wp, h, :], xT[:, xp, h, c * CH:(c + 1) * CH],
                                         start=(n == 0 and h == 0), stop=(n == 2 and h == DH - 1))
                last.then_inc(l_chunk, 1)
            for n in range(NT):
                pe.wait_ge(l_copied, n // QT + 1)
                last = pe.transpose(ps[:, 4, n * NE:(n + 1) * NE], logits_T[:, n * P:(n + 1) * P], k.ident[0:NE, 0:NE])
            last.then_inc(logits, 1)

        @block.scalar
        def _(act):
            act.wait_ge(loaded, 32)
            act.activation(wg_part[:, HIGH, :, :], wg[:, :, :], ACT.Copy).then_inc(w_split, 1)
            for c in range(NCH):
                act.wait_ge(l_chunk, c + 1)
                act.activation(logits_T[:, c * CH:(c + 1) * CH], ps[0:NE, c % 4, :], ACT.Copy).then_inc(l_copied, 1)
            act.wait_ge(logits, 1)
            act.activation(scores[:, :, :], ps[:, 4, :].rearrange("p (n e) -> p n e", e=NE), ACT.Sigmoid).then_inc(scored, 1)

        @block.vector
        def _(dve):
            s = Steps(step)
            dve.memset(k.comb[:, NE, :], 1.0)
            dve.wait_ge(w_split, 1)
            dve.tensor_tensor(wg_part[:, LOW, :, :], wg[:, :, :], wg_part[:, HIGH, :, :].bitcast(F32), ALU.subtract).then_inc(w_split, 1)
            dve.wait_ge(scored, 1)
            s.link(dve, dve.tensor_tensor(biased[:, :, :], scores[:, :, :], gb[:, :].unsqueeze(1).to_broadcast([P, NT, NE]), ALU.add))
            for n in range(NT):
                last = dve.max(top[:, n, :], biased[:, n, :])
            s.link(dve, last)
            for n in range(NT):
                last = dve.max_index(top_i[:, n, :], top[:, n, :], biased[:, n, :])
            s.link(dve, last)
            s.link(dve, dve.tensor_copy(choice[:, :, :], top_i[:, :, 0:TOPK]))
            for c in range(TOPK):
                dst = mask if c == 0 else hit
                s.link(dve, dve.tensor_tensor(dst[:, :, :], k.iota[:, 0:NE].unsqueeze(1).to_broadcast([P, NT, NE]),
                                              choice[:, :, c].unsqueeze(2).to_broadcast([P, NT, NE]), ALU.is_equal))
                if c:
                    s.link(dve, dve.tensor_tensor(mask[:, :, :], mask[:, :, :], hit[:, :, :], ALU.add))
            s.link(dve, dve.tensor_tensor(scores[:, :, :], scores[:, :, :], mask[:, :, :], ALU.mult))
            s.link(dve, dve.tensor_reduce(total[:, :], scores[:, :, :], AX.X, ALU.add))
            s.link(dve, dve.reciprocal(total[:, :], total[:, :]))
            s.link(dve, dve.tensor_scalar(total[:, :], total[:, :], ROUTE_SCALE, None, ALU.mult))
            dve.tensor_tensor(k.comb[:, 0:NE, :].rearrange("p e n -> p n e"), scores[:, :, :],
                              total[:, :].unsqueeze(2).to_broadcast([P, NT, NE]), ALU.mult)


def swiglu_experts(nc, k, a, xT, out):
    assert QT == LNG
    norm = Norm(k)
    WCOLS = DH * 2 * INTER
    with ExitStack() as ctx:
        sb, sem = k.sbuf(ctx), k.stage_sem
        w_raw = k.attn[:, :, :].rearrange("p n c -> p (n c)")[:, 0:WCOLS + D]
        w_part = sb("w_part", [P, 2, 2, WCOLS + D], F32R)
        sig = sb("sig", [P, 2, CH])
        act_g = sb("act_gate", [P, 2, CH])
        hid = sb("hidden_f32", [P, 2, CH])
        hT = sb("hidden_T", [P, 2, 2, CH], F32R)
        w_in, w_high, w_low, stored = (sem("sw_" + n) for n in ("w_in", "w_high", "w_low", "stored"))
        up_done, sig_done, t_done, full, high, low, down_done, added = (sem("sw_" + n) for n in (
            "up", "sig", "t", "full", "high", "low", "down", "added"))
        ps = k.psum
        block = ctx.enter_context(nc.Block())

        def units(eng, first, step):
            first()
            with eng.Fori(0, NE // 2) as i:
                for b in (0, 1):
                    for c in range(NCH):
                        step(2 * i + b, b, c, False)
            for c in range(NCH):
                step(NE, 0, c, c == NCH - 1, final=True)

        def after(e, b, c):
            if c < NCH - 1:
                return e, b, c + 1
            return e + 1, 1 - b, 0

        @block.sync
        def _(sp):
            def load(e):
                sp.wait_ge(w_low, e + 1)
                sp.dma_start(w_raw[:, 0:WCOLS].rearrange("p (h f) -> p h f", h=DH),
                             a["w13_T"][bass.ds(e * D, D), :].rearrange("(h p) f -> p h f", p=P)).then_inc(w_in, 16)
                sp.dma_start(w_raw[:, WCOLS:], a["w2_T"][bass.ds(e * INTER, INTER), :]).then_inc(w_in, 16)
            with sp.Fori(0, NEX) as e:
                load(e)
            for c in range(NCH):
                norm.wait(sp, c)
                tiles = slice(c * QT // 2, (c + 1) * QT // 2)
                sp.dma_start(out.rearrange("(i p j) c -> p i (j c)", p=P, j=2)[:, tiles, :],
                             k.stream[:, :, :].rearrange("p (i j) c -> p i (j c)", j=2)[:, tiles, :]).then_inc(stored, 16)
            sp.wait_ge(stored, 16 * NCH)

        @block.tensor
        def _(pe):
            pe.sem_inc(down_done, 2)

            def up(e, b, c):
                u = NCH * e + c
                if c == 0:
                    pe.wait_ge(w_low, e + 2)
                pe.wait_ge(full, u + 1)
                for half in range(2):
                    for n, (wp, xp) in enumerate(SPLIT):
                        for h in range(DH):
                            at = h * 2 * INTER + half * INTER
                            last = pe.matmul(ps[:, 2 * half + c % 2, :], w_part[:, b, wp, at:at + INTER],
                                             xT[:, xp, h, c * CH:(c + 1) * CH], start=(n == 0 and h == 0), stop=(n == 2 and h == DH - 1))
                last.then_inc(up_done, 1)

            def step(e, b, c, is_last, final=False):
                if not is_last:
                    up(*after(e, b, c))
                u = NCH * e + c
                pe.wait_ge(low, u + 1 + 2)
                pe.wait_ge(added, u + 1)
                for s in range(QT):
                    for n, (hp, wp) in enumerate(SPLIT):
                        last = pe.matmul(ps[:, 4 + 2 * (c % 2) + s // 2, (s % 2) * D:(s % 2 + 1) * D], hT[:, c % 2, hp, s * P:(s + 1) * P],
                                         w_part[:, b, wp, WCOLS:], start=(n == 0), stop=(n == 2))
                last.then_inc(down_done, 1)

            units(pe, lambda: up(0, 0, 0), step)

        @block.scalar
        def _(act):
            def weights(e, b):
                act.wait_ge(w_in, 32 * (e + 1))
                act.wait_ge(down_done, NCH * e - NCH + 2)
                act.activation(w_part[:, b, HIGH, :], w_raw[:, :], ACT.Copy).then_inc(w_high, 1)

            def sigmoid(e, b, c):
                u = NCH * e + c
                act.wait_ge(up_done, u + 1)
                act.wait_ge(full, u + 1)
                act.activation(sig[:, c % 2, :], ps[:, c % 2, :], ACT.Sigmoid).then_inc(sig_done, 1)

            def hidden_high(e, b, c):
                u = NCH * e + c
                act.wait_ge(full, u + 1 + 2)
                act.wait_ge(down_done, u + 1)
                act.activation(hT[:, c % 2, HIGH, :], hid[:, c % 2, :], ACT.Copy).then_inc(high, 1)

            def first():
                act.wait_ge(w_in, 32)
                act.activation(w_part[:, 0, HIGH, :], w_raw[:, :], ACT.Copy).then_inc(w_high, 1)
                sigmoid(0, 0, 0)

            def step(e, b, c, is_last, final=False):
                hidden_high(e, b, c)
                if not is_last:
                    sigmoid(*after(e, b, c))
                if c == 1 and not final:
                    weights(e + 1, 1 - b)
                if final and c >= 1:
                    norm.root(act, c - 1)
                if is_last:
                    norm.root(act, c)

            units(act, first, step)

        @block.gpsimd
        def _(pool):
            def weights(e, b):
                pool.wait_ge(w_high, e + 1)
                pool.tensor_tensor(w_part[:, b, LOW, :], w_raw[:, :], w_part[:, b, HIGH, :].bitcast(F32), ALU.subtract).then_inc(w_low, 1)

            pool.sem_inc(w_low, 1)
            weights(0, 0)
            with pool.Fori(0, NE // 2) as i:
                weights(2 * i + 1, 1)
                weights(2 * i + 2, 0)

        @block.vector
        def _(dve):
            dve.sem_inc(full, 2)
            dve.sem_inc(added, 2)
            dve.sem_inc(low, 2)

            def hidden(e, b, c):
                u = NCH * e + c
                dve.wait_ge(sig_done, u + 1)
                dve.tensor_tensor(act_g[:, c % 2, :], ps[:, c % 2, :], sig[:, c % 2, :], ALU.mult).then_inc(t_done, 1)
                dve.wait_ge(low, u + 1)
                dve.wait_ge(t_done, u + 1)
                dve.tensor_tensor(hid[:, c % 2, :], act_g[:, c % 2, :], ps[:, 2 + c % 2, :], ALU.mult).then_inc(full, 1)

            def hidden_low(e, b, c):
                u = NCH * e + c
                dve.wait_ge(high, u + 1)
                dve.tensor_tensor(hT[:, c % 2, LOW, :], hid[:, c % 2, :], hT[:, c % 2, HIGH, :].bitcast(F32), ALU.subtract).then_inc(low, 1)

            def first():
                hidden(0, 0, 0)
                hidden_low(0, 0, 0)

            def step(e, b, c, is_last, final=False):
                if not is_last:
                    hidden(*after(e, b, c))
                dve.wait_ge(down_done, NCH * e + c + 1 + 2)
                for s in range(QT):
                    if s == QT // 2 and not is_last:
                        hidden_low(*after(e, b, c))
                    n = c * QT + s
                    last = dve.scalar_tensor_tensor(k.stream[:, n, :], ps[:, 4 + 2 * (c % 2) + s // 2, (s % 2) * D:(s % 2 + 1) * D],
                                                    k.comb[:, bass.ds(e, 1), n], k.stream[:, n, :], ALU.mult, ALU.add)
                last.then_inc(added, 1)
                if final:
                    dve.wait_ge(added, NCH * e + c + 1 + 2)
                    norm.stats(dve, c)
                    if c >= 1:
                        norm.apply(dve, c - 1)
                    if is_last:
                        norm.apply(dve, c)

            units(dve, first, step)


def build_program(nc, a, out):
    with ExitStack() as ctx:
        k = Parts()
        k.passing = []

        def stage_sem(name):
            k.passing.append(nc.alloc_semaphore(name=name))
            return k.passing[-1]

        k.stage_sem = stage_sem
        k.sem = lambda name: nc.alloc_semaphore(name=name)
        k.sbuf = lambda c: (lambda name, shape, dt=F32: c.enter_context(nc.sbuf_tensor(name, shape, dt)))
        sb = k.sbuf(ctx)
        k.psum = ctx.enter_context(nc.psum_tensor("psum", [P, 8, CH], F32))
        k.stream = sb("stream", [P, NT, D])
        k.ident = sb("ident", [P, P])
        k.ones = sb("ones", [P, P])
        k.zeros = sb("zeros", [P, D])
        k.eps = sb("eps", [P, 2])
        k.stats = sb("stats", [P, NT, 6])
        k.moments = sb("moments", [P, NT, 2])
        k.rstd = sb("rstd", [P, NT])
        k.ln_sems = [k.sem("ln_" + n) for n in ("stats", "aggregated", "root", "inv", "normed")]
        k.ln_turn = 0
        k.x_saved = k.sem("x_saved")
        k.x_loaded, k.zeros_ready, k.inbox_zeroed = k.sem("x_loaded"), k.sem("zeros_ready"), k.sem("inbox_zeroed")
        k.iota = sb("iota", [P, 16])
        k.before = sb("before", [P, P])
        k.gate = sb("gate", [P, K_MOE, NT])
        k.take = sb("take", [P, K_MOE, NT], U32)
        k.put = sb("put", [P, K_MOE, NT], U32)
        k.take_ready, k.scattered = k.sem("take_ready"), k.sem("scattered")
        build_scan(nc, k, a)
        make_indices(nc, k)
        route_tokens(nc, k, a)
        experts(nc, k, a)
        free_semaphores(nc, k)
        build_attention(nc, k, a, out)


def build_attention(nc, k, a, out):
    with ExitStack() as ctx:
        sb = k.sbuf(ctx)
        k.v = sb("v_all", [P, NT, D])
        with ExitStack() as inner:
            si = k.sbuf(inner)
            k.wfold = si("w_fold", [P, 2, 3, DH, D], F32R)
            k.wrot = si("w_rot", [P, 2, 2, DH, P], F32R)
            xT = si("x2_T", [P, 2, DH, T], F32R)
            combine(nc, k, a, xT)
            project_qkv(nc, k, a, xT)
        k.attn = sb("attn", [P, NT, D])
        attention(nc, k, a)
        xT = sb("x3_T", [P, 2, DH, T], F32R)
        project_attention(nc, k, a, xT)
        free_semaphores(nc, k)
        k.comb = sb("comb", [P, NEX, NT])
        weigh_experts(nc, k, a, xT)
        swiglu_experts(nc, k, a, xT, out)


def build_scan(nc, k, a):
    with ExitStack() as scan:
        ss = k.sbuf(scan)
        k.xpT, k.gateT = ss("xpT", [P, DH, XW]), ss("gateT", [P, DH, TP])
        k.Dv = ss("Dv_sb", [P, DH])
        k.bad = ss("bad", [P, 1], mybir.dt.int32)
        k.A, k.B, k.csum = (ss(n, [P, DH, NS]) for n in ("A_sb", "B_sb", "csum_sb"))
        project_in(nc, k, a)
        load_scan_weights(nc, k, a)
        scan_chunks(nc, k, a)
        seams = nc.values_load(k.bad[0:1, 0:1], min_val=0, max_val=P * D * NS)
        with nc.If(seams > 0):
            nc.all_engine_barrier()
            reload_x(nc, k, a)
            nc.all_engine_barrier()
            scan_steps(nc, k, a)
            nc.all_engine_barrier()
        nc.all_engine_barrier()
        project_out(nc, k, a)
        free_semaphores(nc, k)


SCRATCH = {"x_proj": ([D, TP], F32), "max_rows": ([BUFS, NSPLIT * NT, P], BF16), "qk_parts": ([2, NSPLIT, D, T], BF16), "inbox": ([8 * 1024, D], F32), "outbox": ([8 * 1024, D], F32)}


def host_layout(inputs):
    import numpy as np
    n = {k: np.asarray(v) for k, v in inputs.items()}
    c = np.ascontiguousarray
    x = n["L0_attn_x"][0]
    return {
        "x": c(x), "xs_T": c(x[::TS].T), "w_in_T": c(n["L0_attn_w_in"].T), "b_in": n["L0_attn_b_in"],
        "g_norm": n["L0_attn_g_norm"], "A": n["L0_attn_A"], "Bm": n["L0_attn_Bm"], "Cm": n["L0_attn_Cm"],
        "Dv": n["L0_attn_Dv"], "w_out_T": c(n["L0_attn_w_out"].T), "b_out": n["L0_attn_b_out"],
        "wg": n["L0_ffn_wg"], "w1": n["L0_ffn_w1"].reshape(E_MOE * D, HID), "w2": n["L0_ffn_w2"].reshape(E_MOE * HID, D),
        "b1_T": c(n["L0_ffn_b1"].reshape(E_MOE * HID // P, P).T), "b2": n["L0_ffn_b2"],
        "wq_down_T": c(n["L1_attn_Wq_down"].T), "wk_down_T": c(n["L1_attn_Wk_down"].T), "wv_down_T": c(n["L1_attn_Wv_down"].T),
        "wq_up_c": n["L1_attn_Wq_up_c"], "wq_up_e": n["L1_attn_Wq_up_e"],
        "wk_up_c": n["L1_attn_Wk_up_c"], "wk_up_e": n["L1_attn_Wk_up_e"], "wv_up": n["L1_attn_Wv_up"],
        "wc": n["L1_attn_Wc"], **rope_tables(),
        "gate_w_T": c(n["L1_ffn_gate_w"].T), "gate_b": n["L1_ffn_gate_b"],
        "w13_T": c(np.concatenate((n["L1_ffn_w13"], n["L1_ffn_w13_s"][None])).transpose(0, 2, 1)).reshape(NEX * D, 2 * INTER),
        "w2_T": c(np.concatenate((n["L1_ffn_w2"], n["L1_ffn_w2_s"][None])).transpose(0, 2, 1)).reshape(NEX * INTER, D),
    }


def rope_tables():
    import numpy as np
    inv = (np.float32(1.0) / np.float32(10000.0) ** (np.arange(0, HE, 2, dtype=np.float32) / np.float32(HE))).astype(np.float32)
    angle = np.arange(T, dtype=np.float32)[:, None] * inv[None, :]
    angle = np.concatenate((angle, angle), axis=-1).T
    return {"cos_T": np.tile(np.cos(angle), (NH, 1)), "sin_T": np.tile(np.sin(angle), (NH, 1))}


def kernel(**inputs):
    import numpy as np
    import concourse.bacc as bacc
    from concourse.bass_utils import run_bass_kernel_spmd

    nc = bacc.Bacc("TRN2", target_bir_lowering=False, num_devices=1)
    arrays = {f"in_{name}": np.ascontiguousarray(v) for name, v in host_layout(inputs).items()}
    a = {name[3:]: nc.dram_tensor(name, v.shape, mybir.dt.from_np(v.dtype), kind="ExternalInput").ap()
         for name, v in arrays.items()}
    for name, (shape, dt) in SCRATCH.items():
        a[name] = nc.dram_tensor(name, shape, dt).ap()
    out = nc.dram_tensor("out", (T, D), F32, kind="ExternalOutput").ap()
    build_program(nc, a, out)
    result = run_bass_kernel_spmd(nc, [arrays], core_ids=[0])
    return result.results[0]["out"].reshape(1, T, D)
```
